# Optimizing a Trainium2 kernel written in Bass

```python
import numpy as np
import jax
import jax.numpy as jnp

def _softmax(x, axis=-1):
    return jax.nn.softmax(x, axis=axis)

def _gelu(x):
    return jax.nn.gelu(x, approximate=True)

def _silu(x):
    return jax.nn.silu(x)

def _sigmoid(x):
    return jax.nn.sigmoid(x)

def _layernorm(x, axis=-1, eps=1e-05):
    m = jnp.mean(x, axis=axis, keepdims=True)
    v = jnp.var(x, axis=axis, keepdims=True)
    return (x - m) / jnp.sqrt(v + eps)

def _scatter_add(tgt, idx, src, axis=0):
    return tgt.at[idx].add(src)

def _segment_sum(src, seg, n):
    return jax.ops.segment_sum(src, seg, n)
kernel_name = 'mk_adaln_d1_jaxref_r8_fbd7e8'

def setup_inputs(seed: int=0):
    np.random.seed(seed)
    _w = jnp.asarray

    def _L0_attn_setup():
        import jax, jax.numpy as jnp
        import numpy as np
        HIDDEN = 128
        HEADS = 16
        HEAD_DIM = HIDDEN // HEADS
        SPARSITY_RATIO = 0.5
        key = jax.random.key(seed)
        ks = jax.random.split(key, 6)
        B, S = (2, 256)
        lim = float(np.sqrt(6.0 / (HIDDEN + HIDDEN)))
        x = jax.random.normal(ks[0], (B, S, HIDDEN), dtype=jnp.float32)
        Wq = jax.random.uniform(ks[1], (HIDDEN, HIDDEN), minval=-lim, maxval=lim, dtype=jnp.float32)
        Wk = jax.random.uniform(ks[2], (HIDDEN, HIDDEN), minval=-lim, maxval=lim, dtype=jnp.float32)
        Wv = jax.random.uniform(ks[3], (HIDDEN, HIDDEN), minval=-lim, maxval=lim, dtype=jnp.float32)
        Wo = jax.random.uniform(ks[4], (HIDDEN, HIDDEN), minval=-lim, maxval=lim, dtype=jnp.float32)
        bo = jnp.zeros((HIDDEN,), dtype=jnp.float32)
        adaptive_threshold = jnp.asarray(0.1, dtype=jnp.float32)
        return {'x': x, 'Wq': Wq, 'Wk': Wk, 'Wv': Wv, 'Wo': Wo, 'bo': bo, 'adaptive_threshold': adaptive_threshold}
    _L0_attn_in = _L0_attn_setup()

    def _L0_ffn_setup():
        import jax, jax.numpy as jnp
        import numpy as np
        B, T, C, H, E = (1, 32, 128, 256, 8)
        STD = 0.02
        key = jax.random.key(seed)
        ks = jax.random.split(key, 8)
        f32 = jnp.float32
        return {'x': jax.random.normal(ks[0], (B, T, C), f32), 'up': jax.random.normal(ks[1], (E, H, C), f32) * STD, 'gate': jax.random.normal(ks[2], (E, H, C), f32) * STD, 'down': jax.random.normal(ks[3], (E, C, H), f32) * STD, 'router': jax.random.normal(ks[4], (E, C), f32) * STD, 'w_up_s': jax.random.normal(ks[5], (H, C), f32) * STD, 'w_gate_s': jax.random.normal(ks[6], (H, C), f32) * STD, 'w_down_s': jax.random.normal(ks[7], (C, H), f32) * STD}
    _L0_ffn_in = _L0_ffn_setup()
    _L0_c = _w((lambda *s: np.random.randn(*s).astype(np.float32) * 0.05)(2, 128))
    _L0_wmod = _w((lambda *s: np.random.randn(*s).astype(np.float32) * 0.05)(128, 6 * 128) * 128 ** (-0.5))
    _d = {'L0_attn_x': _L0_attn_in['x'], 'L0_attn_Wq': _L0_attn_in['Wq'], 'L0_attn_Wk': _L0_attn_in['Wk'], 'L0_attn_Wv': _L0_attn_in['Wv'], 'L0_attn_Wo': _L0_attn_in['Wo'], 'L0_attn_bo': _L0_attn_in['bo'], 'L0_attn_adaptive_threshold': _L0_attn_in['adaptive_threshold'], 'L0_ffn_up': _L0_ffn_in['up'], 'L0_ffn_gate': _L0_ffn_in['gate'], 'L0_ffn_down': _L0_ffn_in['down'], 'L0_ffn_router': _L0_ffn_in['router'], 'L0_ffn_w_up_s': _L0_ffn_in['w_up_s'], 'L0_ffn_w_gate_s': _L0_ffn_in['w_gate_s'], 'L0_ffn_w_down_s': _L0_ffn_in['w_down_s'], 'L0_c': _L0_c, 'L0_wmod': _L0_wmod}
    _x0 = _d['L0_attn_x']
    _d['L0_attn_x'] = jax.random.normal(jax.random.fold_in(jax.random.key(seed), 1), (2, 1024, 128), dtype=_x0.dtype)
    del _x0
    return _d

def reference(L0_attn_x, L0_attn_Wq, L0_attn_Wk, L0_attn_Wv, L0_attn_Wo, L0_attn_bo, L0_attn_adaptive_threshold, L0_ffn_up, L0_ffn_gate, L0_ffn_down, L0_ffn_router, L0_ffn_w_up_s, L0_ffn_w_gate_s, L0_ffn_w_down_s, L0_c, L0_wmod):

    def _L0_attn_ref(x, Wq, Wk, Wv, Wo, bo, adaptive_threshold):
        import jax, jax.numpy as jnp
        import numpy as np
        HIDDEN = 128
        HEADS = 16
        HEAD_DIM = HIDDEN // HEADS
        SPARSITY_RATIO = 0.5
        B, S, _ = x.shape
        H, D = (HEADS, HEAD_DIM)
        q = (x @ Wq.T).reshape(B, S, H, D).transpose(0, 2, 1, 3)
        k = (x @ Wk.T).reshape(B, S, H, D).transpose(0, 2, 1, 3)
        v = (x @ Wv.T).reshape(B, S, H, D).transpose(0, 2, 1, 3)
        scores = jnp.einsum('bhqd,bhkd->bhqk', q, k) / jnp.sqrt(jnp.asarray(D, x.dtype))
        k_keep = max(1, int(S * (1.0 - SPARSITY_RATIO)))
        topv = jax.lax.top_k(scores, k_keep)[0]
        kth = topv[..., -1:]
        thr = jnp.clip(adaptive_threshold, 0.0, 1.0)
        keep = (scores >= kth) & (scores >= thr)
        neg_inf = jnp.asarray(-jnp.inf, scores.dtype)
        masked = jnp.where(keep, scores, neg_inf)
        attn = jax.nn.softmax(masked, axis=-1)
        out = jnp.einsum('bhqk,bhkd->bhqd', attn, v)
        out = out.transpose(0, 2, 1, 3).reshape(B, S, H * D)
        return out @ Wo.T + bo

    def _L0_ffn_ref(x, up, gate, down, router, w_up_s, w_gate_s, w_down_s):
        import jax, jax.numpy as jnp
        import numpy as np
        B, T, C, H, E = (1, 32, 128, 256, 8)
        STD = 0.02
        b, t, c = x.shape
        x_ = x.reshape(b * t, c)
        logits = x_ @ router.T
        idx = jnp.argmax(logits, axis=-1)
        onehot = jax.nn.one_hot(idx, router.shape[0], dtype=x.dtype)
        u = jnp.einsum('bc,ehc->ebh', x_, up)
        g = jnp.einsum('bc,ehc->ebh', x_, gate)
        h = jax.nn.silu(g) * u
        ye = jnp.einsum('ebh,ech->ebc', h, down)
        y = jnp.einsum('ebc,be->bc', ye, onehot)
        ys = jax.nn.silu(x_ @ w_gate_s.T) * (x_ @ w_up_s.T) @ w_down_s.T
        return (y + ys).reshape(b, t, c)
    x = L0_attn_x
    mod = (_silu(L0_c) @ L0_wmod).reshape(L0_c.shape[0], 6, 1, -1)
    sa, ca, ga, sb, cb, gb = (mod[:, 0], mod[:, 1], mod[:, 2], mod[:, 3], mod[:, 4], mod[:, 5])
    ga = (2 * (ga >= 0) - 1) * jnp.maximum(jnp.abs(ga), 0.25)
    gb = (2 * (gb >= 0) - 1) * jnp.maximum(jnp.abs(gb), 0.25)
    h = _layernorm(x, axis=-1) * (1 + ca) + sa
    x = x + ga * _L0_attn_ref(h, L0_attn_Wq, L0_attn_Wk, L0_attn_Wv, L0_attn_Wo, L0_attn_bo, L0_attn_adaptive_threshold)
    h = _layernorm(x, axis=-1) * (1 + cb) + sb
    x = x + gb * _L0_ffn_ref(h, L0_ffn_up, L0_ffn_gate, L0_ffn_down, L0_ffn_router, L0_ffn_w_up_s, L0_ffn_w_gate_s, L0_ffn_w_down_s)
    return x

_drawn_inputs = setup_inputs


def setup_inputs(seed=0):
    import zlib

    import numpy as np

    out = dict(_drawn_inputs(seed))
    spreads = {'L0_attn_bo': (0.0, 0.324)}
    factors = {'L0_ffn_up': 8.0,
     'L0_ffn_gate': 8.0,
     'L0_ffn_down': 8.0,
     'L0_ffn_router': 8.0,
     'L0_ffn_w_up_s': 8.0,
     'L0_ffn_w_gate_s': 8.0,
     'L0_ffn_w_down_s': 8.0}
    for name, (base, spread) in spreads.items():
        noise = np.random.default_rng([zlib.crc32(name.encode()), seed]).standard_normal(out[name].shape)
        drawn = base * np.exp(spread * noise) if base else spread * noise
        out[name] = jnp.asarray(drawn.astype(out[name].dtype))
    for name, factor in factors.items():
        out[name] = (out[name] * factor).astype(out[name].dtype)
    return out
```

```python
import concourse.bass as bass
from concourse import mybir
from contextlib import ExitStack

F32 = mybir.dt.float32
BF16 = mybir.dt.bfloat16
I32 = mybir.dt.int32
ACT = mybir.ActivationFunctionType
ALU = mybir.AluOpType
AX = mybir.AxisListType

P = 128
B, S, C = 2, 1024, 128
H, D = 16, 8
QT = S // P
HEADS = B * H
PAIRS = HEADS // 2
SLOTS = 2 * QT
KEEP = S // 2
E, F = 8, 256
FB = F // P
PARTS = 3
REP = PARTS * PARTS
KROWS = REP * D
AUX = 96
UROWS = AUX + PARTS
WROWS = AUX + 2 * PARTS
CAP = P // 2
VW = 32
CHUNK = 512
CT = CHUNK // P
EPS = 1e-5
NWT = 4 + 3 * (E + 1) * FB
SEARCH_LINKS = 48
FF_LINKS = 17
DAMP = [1.0, 1.0, 0.6, 0.9, 0.5]
SLOPE = 2.5066 / S / 4.5 / 2
SLACK = 2.0 ** -21
BISECT = 36


def prepare(nc, T, x, wq, wk, wv, wo, bo, thr, up, gate, down, router, up_s, gate_s, down_s, c_in, wmod, qk_aug):
    sem = T.sem
    loads = sem("prep_loads"); att_loads = sem("prep_att_loads"); cload = sem("prep_c_load"); consts = sem("prep_consts")
    chain_p = sem("prep_chain_pool")
    silu_done = sem("prep_silu"); mod_ready = sem("prep_mod_ready"); mod_done = sem("prep_mod_done")
    wt_ready = sem("prep_wt_ready"); wt_done = sem("prep_wt_done")
    chain = sem("prep_chain_dve"); chain_a = sem("prep_chain_act")
    x_loaded = [sem(f"prep_x_loaded{n}") for n in range(2)]
    var_ready = sem("prep_var"); std_ready = sem("prep_std"); xhat_ready = sem("prep_xhat")
    xt_ready = sem("prep_xt"); ht_ready = sem("prep_ht")
    qkv_ready = sem("prep_qkv"); v_done = sem("prep_v_done"); part1 = sem("prep_part1")
    qkv_used = sem("prep_qkv_used"); parts_ready = sem("prep_parts")
    tp_ready = sem("prep_tp_ready"); tp_done = sem("prep_tp_done"); qtok_done = sem("prep_qtok_done")
    stored = [sem(f"prep_stored{w}") for w in range(2)]
    nat = T.nat
    groups = (NWT + 3) // 4
    NCH = B * S // CHUNK

    with nc.Block() as block:
        @block.sync
        def _(sp):
            for b in range(B):
                sp.dma_start(T.cT[:, b:b + 1], c_in[b, :].rearrange("(c o) -> c o", o=1)).then_inc(cload, 16)
            sp.dma_start(T.wmod[:, :], wmod).then_inc(cload, 16)
            sp.dma_start(T.borow[:, :], bo.rearrange("(a n) -> a n", a=1)).then_inc(cload, 16)
            sp.dma_start(T.thr0[:, :], thr.partition_broadcast(P)).then_inc(cload, 16)
            sp.dma_start(T.x[:, 0:CT, :], x[0:CHUNK, :].rearrange("(t p) c -> p t c", p=P)).then_inc(x_loaded[0], 16)
            for n, w in enumerate((wq, wk, wv, wo)):
                sp.dma_start(nat[:, n, :], w).then_inc(att_loads, 16)
            sp.dma_start(T.x[:, CT:, :], x[CHUNK:, :].rearrange("(t p) c -> p t c", p=P)).then_inc(x_loaded[1], 16)
            n = 4
            for w, ws in ((gate, gate_s), (up, up_s)):
                sp.dma_start(nat[:, n:n + E * FB, :], w.rearrange("e (f p) c -> p (e f) c", p=P)).then_inc(loads, 16)
                sp.dma_start(nat[:, n + E * FB:n + (E + 1) * FB, :], ws.rearrange("(f p) c -> p f c", p=P)).then_inc(loads, 16)
                n += (E + 1) * FB
            sp.dma_start(nat[:, n:n + E * FB, :].rearrange("p (e f) n -> p e (f n)", e=E), down.rearrange("e c h -> c e h")).then_inc(loads, 16)
            sp.dma_start(nat[:, n + E * FB:n + (E + 1) * FB, :].rearrange("p f n -> p (f n)"), down_s).then_inc(loads, 16)
            sp.dma_start(T.rt_nat[:, :], router).then_inc(loads, 16)
            for ch in range(NCH):
                for w in range(2):
                    sp.wait_ge(tp_done, ch * 2 + w + 1)
                    for j in range(REP):
                        part = j // PARTS if w else j % PARTS
                        dst = qk_aug[w, (ch * CHUNK // S) * H:(ch * CHUNK // S + 1) * H, j * D:(j + 1) * D,
                                     ch * CHUNK % S:ch * CHUNK % S + CHUNK]
                        sp.dma_start(dst, T.qkT[:, w * PARTS + part, :]).then_inc(stored[w], 16)
            for w in range(2):
                sp.wait_ge(stored[w], NCH * REP * 16)

        @block.gpsimd
        def _(pool):
            n = [0]

            def link(ins):
                n[0] += 1
                ins.then_inc(chain_p, 1)
                pool.wait_ge(chain_p, n[0])
            link(pool.memset(T.ident[:, :], 0.0))
            link(pool.affine_select(out=T.ident[:, :], in_=T.ident[:, :], compare_op=ALU.not_equal, fill=1.0,
                                    base=0, pattern=[[-1, P]], channel_multiplier=1))
            pool.tensor_copy(T.ident_b[:, :], T.ident[:, :]).then_inc(consts, 1)
            link(pool.memset(T.tri[:, :], 1.0))
            link(pool.affine_select(out=T.tri[:, :], in_=T.tri[:, :], compare_op=ALU.is_ge, fill=0.0,
                                    base=0, pattern=[[1, P]], channel_multiplier=-1))
            link(pool.memset(T.ones_b[:, :], 1.0))
            link(pool.memset(T.zeros_b[:, :], 0.0))
            link(pool.memset(T.ones_f[:, :], 1.0))
            link(pool.iota(T.iota_i[:, :], pattern=[[1, P]], base=1, channel_multiplier=0))
            link(pool.tensor_copy(T.iota[:, :], T.iota_i[:, :]))
            for e in range(2):
                link(pool.memset(T.QB[64:P, e, :], 0.0))
                link(pool.memset(T.KB[64:P, e, :], 0.0))
                link(pool.memset(T.KB[AUX:P, e, :], 1.0))
                link(pool.memset(T.V32[:, e, :, :], 0.0))
                link(pool.memset(T.V32[:, e, :, D:D + 1], 1.0))
            link(pool.memset(T.tpm[:, :, :], 0.0))
            link(pool.memset(T.half[:, :], 0.0))
            link(pool.memset(T.half[0:CAP, 0:1], 1.0))
            link(pool.memset(T.half[CAP:P, 1:2], 1.0))
            link(pool.memset(T.osel[:, :, :], 0.0))
            for c in range(2):
                for par in range(2):
                    link(pool.affine_select(out=T.osel[:, c, :], in_=T.osel[:, c, :], compare_op=ALU.not_equal, fill=1.0,
                                            base=-32 * (2 * par + c), pattern=[[-1, D + 1]], channel_multiplier=1))
            link(pool.iota(T.iota_i[:, 0:E], pattern=[[-1, E]], base=E, channel_multiplier=0))
            link(pool.tensor_copy(T.down_count[:, :], T.iota_i[:, 0:E]))
            pool.memset(T.epsc[:, :], EPS).then_inc(consts, 1)
            for ch in range(NCH):
                pool.wait_ge(parts_ready, (ch + 1) * CT)
                b, t0 = ch * CHUNK // S, (ch % (S // CHUNK)) * CT
                for t in range(CT):
                    for p in range(PARTS):
                        last = pool.tensor_copy(T.Qtok[:, b * H:(b + 1) * H, t0 + t, p, :],
                                                T.qkp[:, t, p, 0:C].rearrange("p (h d) -> p h d", d=D))
                last.then_inc(qtok_done, 1)

        @block.scalar
        def _(act):
            act.wait_ge(cload, 80)
            act.activation(T.sc[:, :], T.cT[:, :], ACT.Silu).then_inc(silu_done, 1)
            act.wait_ge(consts, 2)
            for ch in range(NCH):
                act.wait_ge(var_ready, ch + 1)
                act.activation(T.std[:, :], T.mv[:, :, 1], ACT.Sqrt, bias=T.epsc[:, 0:1]).then_inc(std_ready, 1)
                for t in range(CT):
                    g = ch * CT + t
                    b, tt = g // QT, g % QT
                    act.wait_ge(qkv_ready, g + 1)
                    if g >= CT:
                        act.wait_ge(qtok_done, ch)
                        act.wait_ge(tp_ready, 2 * ch)
                    act.activation(T.qkp[:, t, 0, :], T.pA[:, (g % 2) * 512:(g % 2) * 512 + 2 * C], ACT.Copy).then_inc(part1, 1)
                    act.activation(T.V[:, b * H:(b + 1) * H, tt, :],
                                   T.pA[:, (g % 2) * 512 + 2 * C:(g % 2) * 512 + 3 * C].rearrange("p (h d) -> p h d", d=D),
                                   ACT.Copy).then_inc(v_done, 1)
                for w in range(2):
                    act.wait_ge(tp_ready, ch * 2 + w + 1)
                    if ch:
                        act.wait_ge(stored[w], ch * REP * 16)
                    act.activation(T.qkT[:, w * PARTS:(w + 1) * PARTS, :],
                                   T.pUW_b[:, w * 2048:w * 2048 + PARTS * CHUNK].rearrange("p (a n) -> p a n", a=PARTS),
                                   ACT.Copy).then_inc(tp_done, 1)

        @block.vector
        def _(dve):
            def done(ins, s, value):
                ins.then_inc(s, 1)
                dve.wait_ge(s, value)

            n = [0]

            def link(ins):
                n[0] += 1
                ins.then_inc(chain, 1)
                dve.wait_ge(chain, n[0])
            dve.wait_ge(cload, 80)
            link(dve.tensor_scalar(T.thrc[:, :], T.thr0[:, :], 0.0, 1.0, ALU.max, ALU.min))
            link(dve.tensor_scalar(T.negthr[:, :], T.thrc[:, :], -1.0, None, ALU.mult))
            dve.wait_ge(mod_ready, 1)
            link(dve.tensor_copy(T.mod[:, :], T.pO[:, 0:6 * B]))
            for m in (1, 4):
                link(dve.tensor_scalar(T.mod[:, m * B:(m + 1) * B], T.mod[:, m * B:(m + 1) * B], 1.0, None, ALU.add))
            g = T.gates[:, :]
            link(dve.tensor_copy(g, T.pM[:, 0:2 * B * C]))
            link(dve.scalar_tensor_tensor(T.gabs[:, :], g, -1.0, g, ALU.mult, ALU.max))
            link(dve.tensor_scalar(g, g, 0.0, 2.0, ALU.is_ge, ALU.mult))
            link(dve.tensor_scalar(T.gabs[:, :], T.gabs[:, :], 0.25, None, ALU.max))
            link(dve.tensor_scalar(g, g, -1.0, None, ALU.add))
            dve.tensor_tensor(g, g, T.gabs[:, :], ALU.mult).then_inc(mod_done, 1)
            for k in range(groups):
                dve.wait_ge(wt_ready, k + 1)
                m = min(4, NWT - 4 * k)
                src = T.pO if k % 2 == 0 else T.pM
                if k == 0:
                    dve.tensor_scalar(T.wT[:, 0:C], src[:, 0:C], float(D) ** -0.5, None, ALU.mult)
                    dve.tensor_copy(T.wT[:, C:4 * C], src[:, C:4 * C]).then_inc(wt_done, 1)
                else:
                    dve.tensor_copy(T.wT[:, 4 * k * C:(4 * k + m) * C], src[:, 0:m * C]).then_inc(wt_done, 1)
            dve.wait_ge(wt_ready, groups + 1)
            dve.tensor_copy(T.rT[:, :], T.pO[:, 0:E]).then_inc(wt_done, 1)
            for ch in range(NCH):
                b = ch * CHUNK // S
                dve.wait_ge(x_loaded[min(ch, 1)], 16)
                if ch:
                    dve.wait_ge(std_ready, ch)
                for t in range(CT):
                    link(dve.bn_stats(T.bn[:, t, :], T.x[:, ch * CT + t, :]))
                for t in range(CT):
                    last = dve.bn_aggr(T.mv[:, t, :], T.bn[:, t, :])
                link(last)
                done(dve.tensor_scalar(T.veps[:, :], T.mv[:, :, 1], EPS, None, ALU.add), var_ready, ch + 1)
                dve.wait_ge(std_ready, ch + 1)
                link(dve.reciprocal(T.rs[:, :], T.std[:, :]))
                link(dve.tensor_tensor(T.rs[:, :], T.rs[:, :], T.veps[:, :], ALU.mult))
                link(dve.tensor_tensor(T.rs[:, :], T.rs[:, :], T.std[:, :], ALU.add))
                link(dve.tensor_scalar(T.rs[:, :], T.rs[:, :], 0.5, None, ALU.mult))
                link(dve.reciprocal(T.rs[:, :], T.rs[:, :]))
                if ch:
                    dve.wait_ge(xt_ready, ch)
                for t in range(CT):
                    last = dve.tensor_scalar(T.xhat[:, t, :], T.x[:, ch * CT + t, :], T.mv[:, t, 0:1],
                                             T.rs[:, t:t + 1], ALU.subtract, ALU.mult)
                last.then_inc(xhat_ready, 1)
                dve.wait_ge(xt_ready, ch + 1)
                if ch:
                    dve.wait_ge(qkv_ready, ch * CT)
                dve.tensor_scalar(T.hT[:, :], T.pO[:, :], T.mod[:, B + b:B + b + 1], T.mod[:, b:b + 1],
                                  ALU.mult, ALU.add).then_inc(ht_ready, 1)
                for t in range(CT):
                    g = ch * CT + t
                    src = T.pA[:, (g % 2) * 512:(g % 2) * 512 + 2 * C]
                    dve.wait_ge(v_done, g + 1)
                    dve.wait_ge(part1, g + 1)
                    done(dve.tensor_tensor(T.rem[:, :], src, T.qkp[:, t, 0, :], ALU.subtract), qkv_used, g + 1)
                    link(dve.tensor_copy(T.qkp[:, t, 1, :], T.rem[:, :]))
                    done(dve.tensor_tensor(T.qkp[:, t, 2, :], T.rem[:, :], T.qkp[:, t, 1, :], ALU.subtract), parts_ready, g + 1)

        @block.tensor
        def _(pe):
            pe.wait_ge(cload, 80)
            pe.wait_ge(silu_done, 1)
            for m in range(6):
                nc.tensor.matmul(T.pO[:, m * B:(m + 1) * B], T.wmod[:, m * C:(m + 1) * C], T.sc[:, :], start=True, stop=True)
            for k, m in enumerate((2, 5)):
                for b in range(B):
                    last = nc.tensor.matmul(T.pM[:, (k * B + b) * C:(k * B + b + 1) * C],
                                            T.sc[:, b:b + 1].broadcast_to([P, P]), T.wmod[:, m * C:(m + 1) * C],
                                            start=True, stop=True)
            last.then_inc(mod_ready, 1)
            pe.wait_ge(mod_done, 1)
            pe.wait_ge(consts, 2)
            for k in range(groups):
                if k == 0:
                    pe.wait_ge(att_loads, 4 * 16)
                else:
                    pe.wait_ge(loads, 7 * 16)
                if k >= 2:
                    pe.wait_ge(wt_done, k - 1)
                dst = T.pO if k % 2 == 0 else T.pM
                for j in range(min(4, NWT - 4 * k)):
                    last = nc.tensor.transpose(dst[:, j * C:(j + 1) * C], nat[:, 4 * k + j, :], T.ident[:, :])
                last.then_inc(wt_ready, 1)
            pe.wait_ge(wt_done, groups)
            nc.tensor.transpose(T.pO[:, 0:E], T.rt_nat[:, :], T.ident[0:E, 0:E]).then_inc(wt_ready, 1)
            pe.wait_ge(wt_done, groups + 1)
            for ch in range(NCH):
                pe.wait_ge(xhat_ready, ch + 1)
                if ch:
                    pe.wait_ge(ht_ready, ch)
                for t in range(CT):
                    last = nc.tensor.transpose(T.pO[:, t * P:(t + 1) * P], T.xhat[:, t, :], T.ident[:, :])
                last.then_inc(xt_ready, 1)
                pe.wait_ge(ht_ready, ch + 1)
                for t in range(CT):
                    g = ch * CT + t
                    if g >= 2:
                        pe.wait_ge(qkv_used, g - 1)
                    nc.tensor.matmul(T.pA[:, (g % 2) * 512:(g % 2) * 512 + 3 * C], T.hT[:, t * P:(t + 1) * P],
                                     T.wT[:, 0:3 * C], start=True, stop=True).then_inc(qkv_ready, 1)
                pe.wait_ge(parts_ready, (ch + 1) * CT)
                for w in range(2):
                    if ch:
                        pe.wait_ge(tp_done, 2 * (ch - 1) + w + 1)
                    for p in range(PARTS):
                        for t in range(CT):
                            o = w * 2048 + p * CHUNK + t * P
                            last = nc.tensor.transpose(T.pUW_b[:, o:o + P], T.qkp[:, t, p, w * C:(w + 1) * C], T.ident_b[:, :])
                    last.then_inc(tp_ready, 1)


def attention(nc, T, qk_aug):
    sem = T.sem
    a_load = [sem(f"a_load{e}") for e in range(2)]
    b_load = [sem(f"b_load{e}") for e in range(2)]
    aux_load = [sem(f"aux_load{e}") for e in range(2)]
    s_load = sem("s_load")
    a_ready = sem("a_ready"); a_copied = sem("a_copied"); a_counted = sem("a_counted")
    u_ready = sem("u_ready"); w_ready = sem("w_ready"); e_ready = sem("e_ready"); p_ready = sem("p_ready")
    pv_done = sem("pv_done"); o_copied = sem("o_copied"); ot_ready = sem("ot_ready"); o_done = sem("o_done")
    o_chain = sem("o_chain"); v_ready = sem("v_ready"); qg_ready = sem("qg_ready")
    st_taken = sem("st_taken"); pos_ready = sem("pos_ready"); pos_used = sem("pos_used"); sel_ready = sem("sel_ready")
    gat_ready = sem("gat_ready"); gat_used = sem("gat_used")
    ss_ready = sem("ss_ready"); ss_copied = sem("ss_copied"); step_t = sem("step_t"); step_c = sem("step_c")
    selT_ready = sem("selT_ready"); selT_copied = sem("selT_copied")
    tp_ready = sem("tparts_ready"); sc_ready = sem("scattered"); flag_ready = sem("flag_ready"); sc_used = sem("scatter_used")
    rows_src = sem("rows_src"); rowsT_ready = sem("rowsT_ready"); rows_copied = sem("rows_copied")
    chain = sem("search_chain")
    fb_ready = sem("fb_ready"); fb_copied = sem("fb_copied"); fb_chain = sem("fb_chain")
    NC_ = SEARCH_LINKS
    FBN = SLOTS * (2 + 5 * BISECT + 4)
    settled = sem("settled")
    K0 = len(DAMP)

    def at_least(i, lo):
        return i >= lo if isinstance(i, int) else lo <= 2

    with nc.Block() as block:
        @block.sync
        def _(sp):
            def load(dst, w, head, s):
                sp.dma_start(dst, qk_aug[w, bass.ds(head, 1), :, :].rearrange("o r n -> (o r) n")).then_inc(s, 16)

            def aux(e):
                sp.dma_start(T.QB[AUX:WROWS, e, :], T.rowsT[e * 48:(e + 1) * 48, :]).then_inc(aux_load[e], 16)
            for e in range(2):
                load(T.QA[0:KROWS, e, :], 0, e, a_load[e])
                load(T.KA[0:KROWS, e, :], 1, e, a_load[e])

            def load_a(i, e):
                sp.wait_ge(a_ready, i * SLOTS + (e + 1) * QT)
                load(T.QA[0:KROWS, e, :], 0, 2 * i + 2 + e, a_load[e])
                load(T.KA[0:KROWS, e, :], 1, 2 * i + 2 + e, a_load[e])

            def body(i, do_a, do_s, do_b, more_a):
                if do_b:
                    if not (isinstance(i, int) and i == 2):
                        sp.wait_ge(p_ready, (i - 2) * SLOTS)
                    load(T.QB[0:KROWS, 1, :], 0, 2 * i - 3, b_load[1])
                    load(T.KB[0:KROWS, 1, :], 1, 2 * i - 3, b_load[1])
                    aux(1)
                if do_s:
                    if do_b:
                        sp.wait_ge(p_ready, (i - 2) * SLOTS + QT)
                    load(T.QB[0:KROWS, 0, :], 0, 2 * i - 2, b_load[0])
                    load(T.KB[0:KROWS, 0, :], 1, 2 * i - 2, b_load[0])
                if more_a:
                    load_a(i, 0)
                if do_a:
                    if do_s:
                        sp.wait_ge(sc_used, i)
                    for e in range(2):
                        load(T.KS[0:KROWS, e, :], 1, 2 * i + e, s_load)
                        load(T.QS[0:KROWS, e, :], 0, 2 * i + e, s_load)
                if do_s:
                    sp.wait_ge(rows_copied, i)
                    aux(0)
                if more_a:
                    load_a(i, 1)
            body(0, True, False, False, True)
            body(1, True, True, False, True)
            body(2, True, True, True, True)
            with sp.Fori(3, PAIRS - 1) as i:
                body(i, True, True, True, True)
            body(PAIRS - 1, True, True, True, False)
            body(PAIRS, False, True, True, False)
            body(PAIRS + 1, False, False, True, False)

        @block.gpsimd
        def _(pool):
            def values(e, pair, first):
                if not first:
                    pool.wait_ge(pv_done, pair * QT - QT + (e + 1) * (QT // 2))
                pool.tensor_copy(T.V32[:, e, :, 0:D],
                                 T.V[:, bass.ds(2 * pair + e, 1), :, :].rearrange("p o t d -> p (o t) d")).then_inc(v_ready, 1)

            def body(i, do_a, do_s, do_b):
                if do_s:
                    if at_least(i, 2):
                        pool.wait_ge(gat_ready, i - 1)
                    for e in range(2):
                        for r in range(PARTS):
                            last = pool.tensor_copy(
                                T.QG[:, e, :, r * PARTS * D:(r + 1) * PARTS * D].rearrange("p t (a d) -> p t a d", a=PARTS),
                                T.Qtok[:, bass.ds(2 * i - 2 + e, 1), :, :, :].rearrange("p o t a d -> p (o t) a d"))
                    last.then_inc(qg_ready, 1)
                if do_b and (not isinstance(i, int) or i < PAIRS + 1):
                    values(0, i - 1, False)
                if do_b and (not isinstance(i, int) or i < PAIRS + 1):
                    values(1, i - 1, False)
                if isinstance(i, int) and i == 1:
                    values(0, 0, True)
                    values(1, 0, True)
            iterations(pool, body)

        @block.scalar
        def _(act):
            def copy_o(i, e):
                head = 2 * (i - 2) + e - 1
                act.wait_ge(pv_done, (head + 1) * (QT // 2))
                if not (isinstance(i, int) and head == 0):
                    act.wait_ge(ot_ready, head)
                act.activation(T.Osb[:, :], T.pO[:, :], ACT.Copy).then_inc(o_copied, 1)

            def body(i, do_a, do_s, do_b):
                for n in range(SLOTS):
                    e, t = n // QT, n % QT
                    if do_b:
                        gb = (i - 2) * SLOTS + n
                        act.wait_ge(w_ready, gb + 1)
                        if not (isinstance(i, int) and i == 2 and n < 4):
                            act.wait_ge(pv_done, (i - 2) * QT + (n - 4) // 2 + 1)
                        act.activation(T.E[:, n % 4, :], T.pW[:, :], ACT.Exp).then_inc(e_ready, 1)
                    if do_a:
                        ga = i * SLOTS + n
                        act.wait_ge(a_copied, ga + 1)
                        if n == 0 and do_s:
                            act.wait_ge(st_taken, i)
                        act.activation(T.junk_a[:, n % 2, :], T.Sc[:, n % 2, :], ACT.Sign, bias=T.negthr[:, 0:1],
                                       accum_out=T.cnt[:, n:n + 1]).then_inc(a_counted, 1)
                    if do_b and t == 1 and not (isinstance(i, int) and i == 2 and e == 0):
                        copy_o(i, e)
                    if do_s:
                        if n in (5, 6):
                            act.wait_ge(ss_ready, 2 * (i - 1) + n - 4)
                            if n == 5 and at_least(i, 2):
                                act.wait_ge(sc_used, i - 1)
                            act.activation(T.Ss[:, (n - 5) * 512:(n - 4) * 512], T.pM[:, :], ACT.Copy).then_inc(ss_copied, 1)
                        if n == 8:
                            act.wait_ge(selT_ready, i)
                            act.activation(T.SelT[:, :], T.pM_b[:, :], ACT.Copy).then_inc(selT_copied, 1)
                        if 7 <= n < 7 + K0:
                            k = n - 7
                            if k == 0:
                                act.wait_ge(ss_copied, 2 * i)
                            act.wait_ge(step_t, (i - 1) * (K0 + 1) + k + 1)
                            act.activation(T.junk_a2[:, :], T.Ss[:, :], ACT.Sign, bias=T.tc[:, k:k + 1], scale=-1.0,
                                           accum_out=T.sg[:, k:k + 1]).then_inc(step_c, 1)
            iterations(act, body)
            act.wait_ge(pv_done, HEADS * QT // 2)
            act.wait_ge(ot_ready, HEADS - 1)
            act.activation(T.Osb[:, :], T.pO[:, :], ACT.Copy).then_inc(o_copied, 1)

        @block.vector
        def _(dve):
            def done(ins, s, value):
                ins.then_inc(s, 1)
                dve.wait_ge(s, value)

            def finish_o(head, first=False):
                dve.wait_ge(ot_ready, head + 1)
                o = T.pM[:, 0:QT * (D + 1)].rearrange("p (t d) -> p t d", d=D + 1)
                if not first:
                    dve.wait_ge(o_done, head)
                dve.reciprocal(T.rl[:, :], o[:, :, D]).then_inc(o_chain, 1)
                dve.wait_ge(o_chain, head + 1)
                dve.tensor_tensor(T.attn[:, bass.ds(head, 1), :, :].rearrange("p o t d -> p (o t) d"), o[:, :, 0:D],
                                  T.rl[:, :].unsqueeze(2).broadcast_to([P, QT, D]), ALU.mult).then_inc(o_done, 1)

            def body(i, do_a, do_s, do_b):
                links = [0]

                def link(ins):
                    links[0] += 1
                    ins.then_inc(chain, 1)
                    dve.wait_ge(chain, (i - 1) * NC_ + links[0])

                def fallback():
                    m = [0]

                    def flink(ins):
                        m[0] += 1
                        ins.then_inc(fb_chain, 1)
                        dve.wait_ge(fb_chain, (i - 1) * FBN + m[0])
                    for n in range(SLOTS):
                        for hf in range(2):
                            dve.wait_ge(fb_ready, (i - 1) * 2 * SLOTS + 2 * n + hf + 1)
                            dve.tensor_copy(T.Ss[:, hf * 512:(hf + 1) * 512], T.pM[:, :]).then_inc(fb_copied, 1)
                        dve.wait_ge(fb_copied, (i - 1) * 2 * SLOTS + 2 * n + 2)
                        flink(dve.tensor_copy(T.lo[:, :], T.thrc[:, :]))
                        flink(dve.tensor_scalar(T.stp[:, :], T.Mp[:, n:n + 1], 0.0, 1.0, ALU.max, ALU.add))
                        dve.sem_inc(settled, 1)
                        with dve.Fori(0, BISECT) as r:
                            base = (i - 1) * FBN + n * (6 + 5 * BISECT) + 2 + 5 * r

                            def rlink(ins, k):
                                ins.then_inc(fb_chain, 1)
                                dve.wait_ge(fb_chain, base + k)
                            rlink(dve.tensor_tensor(T.mid[:, :], T.lo[:, :], T.stp[:, :], ALU.add), 1)
                            rlink(dve.tensor_scalar(T.Wm[:, :], T.Ss[:, :], T.mid[:, 0:1], None, ALU.is_ge, ALU.add,
                                                    accum_out=T.c1[:, :]), 2)
                            rlink(dve.scalar_tensor_tensor(T.mid[:, :], T.c1[:, :], KEEP - 0.5, T.stp[:, :], ALU.is_ge, ALU.mult), 3)
                            rlink(dve.tensor_tensor(T.lo[:, :], T.lo[:, :], T.mid[:, :], ALU.add), 4)
                            rlink(dve.tensor_scalar(T.stp[:, :], T.stp[:, :], 0.5, None, ALU.mult), 5)
                            dve.sem_inc(settled, 1)
                        m[0] += 5 * BISECT
                        flink(dve.tensor_scalar(T.mid[:, :], T.Mp[:, n:n + 1], 0.0, -SLACK, ALU.max, ALU.mult))
                        flink(dve.tensor_tensor(T.lo[:, :], T.lo[:, :], T.mid[:, :], ALU.add))
                        flink(dve.tensor_tensor(T.Tt[:, n:n + 1], T.lo[:, :], T.thrc[:, :], ALU.max))
                        flink(dve.tensor_copy(T.c1[:, :], T.lo[:, :]))
                    dve.sem_inc(settled, 1)
                    assert m[0] == FBN, (m[0], FBN)

                def search(n):
                    if n == 0:
                        dve.wait_ge(a_counted, i * SLOTS)
                        if at_least(i, 2):
                            dve.wait_ge(sc_used, i - 1)
                        dve.tensor_scalar(T.Fb[:, :], T.cnt[:, :], 0.0, None, ALU.is_ge)
                        dve.tensor_copy(T.st[:, :, 0], T.cnt[:, :])
                        dve.tensor_copy(T.st[:, :, 1], T.M[:, :])
                        dve.tensor_copy(T.Mp[:, :], T.M[:, :])
                        dve.tensor_scalar(T.st[:, :, 2], T.cnt[:, :], 0.0, None, ALU.is_ge).then_inc(st_taken, 1)
                        dve.wait_ge(st_taken, i)
                    if n == 1:
                        dve.wait_ge(pos_ready, i)
                        done(dve.tensor_tensor(T.posF[:, :], T.pM[:, 0:SLOTS], T.Fb[:, :], ALU.mult), pos_used, i)
                        done(dve.tensor_tensor(T.Sel[:, :, :, :].rearrange("p t e c -> p e t c"),
                                               T.iota[:, 0:CAP].unsqueeze(1).unsqueeze(1).broadcast_to([P, 2, QT, CAP]),
                                               T.posF[:, :].rearrange("p (e t) -> p e t", e=2).unsqueeze(3).broadcast_to([P, 2, QT, CAP]),
                                               ALU.is_equal), sel_ready, i)
                        link(dve.tensor_reduce(T.bad[:, 1:2], T.posF[:, :], AX.X, ALU.max))
                    if n == 4:
                        dve.wait_ge(gat_ready, i)
                        dve.tensor_copy(T.Qc[:, :], T.pM[0:KROWS, 0:P])
                        done(dve.tensor_copy(T.gs[:, :], T.pM[:, P:P + 3]), gat_used, i)
                        link(dve.tensor_scalar(T.sl[:, :], T.gs[:, 1:2], 0.0, SLOPE, ALU.max, ALU.mult))
                        link(dve.scalar_tensor_tensor(T.dt[:, :], T.gs[:, 0:1], 8.0, T.sl[:, :], ALU.add, ALU.mult))
                        done(dve.tensor_tensor(T.tc[:, 0:1], T.dt[:, :], T.thrc[:, :], ALU.add), step_t, (i - 1) * (K0 + 1) + 1)
                    if 7 <= n < 7 + K0:
                        k = n - 7
                        dve.wait_ge(step_c, (i - 1) * K0 + k + 1)
                        s = T.sg[:, k:k + 1]
                        link(dve.tensor_scalar(T.nd[:, :], s, -1.0, 8.0, ALU.mult, ALU.add))
                        link(dve.tensor_tensor(T.dt[:, :], T.nd[:, :], T.nd[:, :], ALU.mult))
                        link(dve.tensor_scalar(T.dt[:, :], T.dt[:, :], 6.5 * 6.5, DAMP[k], ALU.is_gt, ALU.mult))
                        link(dve.tensor_tensor(T.dt[:, :], T.dt[:, :], T.nd[:, :], ALU.mult))
                        done(dve.scalar_tensor_tensor(T.tc[:, k + 1:k + 2], T.dt[:, :], T.sl[:, 0:1], T.tc[:, k:k + 1],
                                                      ALU.mult, ALU.add), step_t, (i - 1) * (K0 + 1) + k + 2)
                    if n == 12:
                        t = T.tc[:, K0:K0 + 1]
                        link(dve.tensor_scalar(T.Wm[:, :], T.Ss[:, :], t, None, ALU.is_ge, ALU.add, accum_out=T.c1[:, :]))
                        link(dve.scalar_tensor_tensor(T.Wm[:, :], T.Ss[:, :], t, T.Ss[:, :], ALU.is_lt, ALU.mult))
                    if n == 13:
                        link(dve.max(T.W8[:, :], T.Wm[:, :]))
                        link(dve.tensor_scalar(T.ix[:, :], T.c1[:, :], -1.0, float(KEEP), ALU.mult, ALU.add))
                        link(dve.tensor_scalar(T.ix1[:, :], T.ix[:, :], 1.0, None, ALU.add))
                        link(dve.scalar_tensor_tensor(T.h8[:, :], T.iota[:, 0:8], T.ix[:, 0:1], T.W8[:, :], ALU.is_equal, ALU.mult,
                                                      accum_out=T.kth[:, :]))
                        link(dve.scalar_tensor_tensor(T.h8[:, :], T.iota[:, 0:8], T.ix1[:, 0:1], T.W8[:, :], ALU.is_equal, ALU.mult,
                                                      accum_out=T.nxt[:, :]))
                        link(dve.tensor_tensor(T.kth[:, :], T.kth[:, :], T.nxt[:, :], ALU.add))
                        link(dve.tensor_scalar(T.nxt[:, :], T.gs[:, 1:2], 0.0, -2 * SLACK, ALU.max, ALU.mult))
                        link(dve.tensor_tensor(T.kth[:, :], T.kth[:, :], T.nxt[:, :], ALU.add))
                        link(dve.tensor_scalar(T.kth[:, :], T.kth[:, :], 0.5, None, ALU.mult))
                        link(dve.tensor_copy(T.t3[:, 0:1], T.kth[:, :]))
                        link(dve.tensor_tensor(T.dt[:, :], T.kth[:, :], T.t3[:, 0:1], ALU.subtract))
                        link(dve.tensor_copy(T.t3[:, 1:2], T.dt[:, :]))
                        link(dve.tensor_tensor(T.t3[:, 2:3], T.dt[:, :], T.t3[:, 1:2], ALU.subtract))
                        link(dve.tensor_scalar(T.tpm[:, 0, :], T.t3[:, :], T.half[:, 0:1], None, ALU.mult))
                        link(dve.tensor_scalar(T.tpm[:, 1, :], T.t3[:, :], T.half[:, 1:2], None, ALU.mult))
                        link(dve.tensor_scalar(T.nd[:, :], T.ix[:, :], -4.0, None, ALU.add))
                        link(dve.tensor_tensor(T.nd[:, :], T.nd[:, :], T.nd[:, :], ALU.mult))
                        link(dve.scalar_tensor_tensor(T.nd[:, :], T.nd[:, :], 9.5, T.gs[:, 2:3], ALU.is_gt, ALU.mult))
                        dve.scalar_tensor_tensor(T.badb[:, :], T.bad[:, 1:2], CAP + 0.5, T.nd[:, :], ALU.is_gt, ALU.add).then_inc(tp_ready, 1)
                    if n == 14:
                        dve.wait_ge(sc_ready, i)
                        link(dve.tensor_copy(T.flag[0:1, 0:1], T.pM[0:1, 64:65]))
                        done(dve.tensor_reduce(T.Tt[:, :].rearrange("p (e t) -> p t e", e=2),
                                               T.pM[:, 0:48].rearrange("p (t e a) -> p t e a", e=2, a=PARTS), AX.X, ALU.add), flag_ready, i)
                        link(dve.tensor_scalar(T.Tt[:, :], T.Tt[:, :], T.thrc[:, 0:1], None, ALU.max))
                        dve.sem_inc(settled, 1)
                        flag = dve.value_load(T.flag[0:1, 0:1], min_val=0, max_val=P * 2)
                        with dve.If(flag > 0):
                            fallback()
                        with dve.Else():
                            dve.sem_inc(fb_copied, 2 * SLOTS)
                            dve.sem_inc(fb_chain, FBN)
                        if at_least(i, 2):
                            dve.wait_ge(rowsT_ready, i - 1)
                        X = T.X
                        dve.tensor_scalar(X[:, 0, :], T.Tt[:, :], -1.0, None, ALU.mult)
                        done(dve.tensor_tensor(X[:, 1, :], T.Tt[:, :], T.Mp[:, :], ALU.subtract), sc_used, i)
                        r = T.RP[:, :].rearrange("p (e k a t) -> p k a e t", e=2, k=2, a=PARTS)
                        xv = X[:, :, :].rearrange("p k (e t) -> p k e t", e=2)
                        for k in range(2):
                            last = dve.tensor_copy(r[:, k, 0], xv[:, k])
                        link(last)
                        for k in range(2):
                            last = dve.tensor_tensor(xv[:, k], xv[:, k], r[:, k, 0], ALU.subtract)
                        link(last)
                        for k in range(2):
                            last = dve.tensor_copy(r[:, k, 1], xv[:, k])
                        link(last)
                        for k in range(2):
                            last = dve.tensor_tensor(r[:, k, 2], xv[:, k], r[:, k, 1], ALU.subtract)
                        last.then_inc(rows_src, 1)
                    if n == 15:
                        dve.wait_ge(rowsT_ready, i)
                        if at_least(i, 2):
                            for e in range(2):
                                dve.wait_ge(aux_load[e], (i - 1) * 16)
                        dve.tensor_copy(T.rowsT[:, :], T.pM_b[0:96, 0:P]).then_inc(rows_copied, 1)
                        assert links[0] == NC_, links[0]

                for n in range(SLOTS):
                    e, t = n // QT, n % QT
                    if do_s and n == 0:
                        search(0)
                    if do_a:
                        ga = i * SLOTS + n
                        dve.wait_ge(a_ready, ga + 1)
                        if not (isinstance(i, int) and i == 0 and n < 2):
                            dve.wait_ge(a_counted, ga - 1)
                        dve.tensor_scalar(T.Sc[:, n % 2, :], T.pA[:, :], 1.0, None, ALU.mult, ALU.max,
                                          accum_out=T.M[:, n:n + 1]).then_inc(a_copied, 1)
                    if do_b:
                        gb = (i - 2) * SLOTS + n
                        dve.wait_ge(e_ready, gb + 1)
                        dve.wait_ge(u_ready, gb + 1)
                        dve.scalar_tensor_tensor(T.E[:, n % 4, :], T.pU[:, :], 0.0, T.E[:, n % 4, :], ALU.is_ge, ALU.mult).then_inc(p_ready, 1)
                    if do_b and t == 2 and not (isinstance(i, int) and i == 2 and e == 0):
                        finish_o(2 * (i - 2) + e - 1, isinstance(i, int) and i == 2 and e == 1)
                    if do_s and n > 0:
                        search(n)
            iterations(dve, body)
            finish_o(HEADS - 1)

        @block.tensor
        def _(pe):
            def products(i, n):
                k = (n // 2 - 1) % (QT // 2)
                e = ((n - 2) // QT) % 2
                pe.wait_ge(p_ready, (i - 2) * SLOTS + n)
                if k == 0:
                    head = 2 * (i - 2) + e
                    pe.wait_ge(v_ready, head + 1)
                    if not (isinstance(i, int) and i == 2 and e == 0):
                        pe.wait_ge(o_copied, head)
                for par in range(2):
                    for c in range(2):
                        g = 32 * (2 * par + c)
                        last = nc.tensor.matmul(T.pO[g:g + VW, :], T.V32[:, e, 2 * k + par, :],
                                                T.E[:, (n - 2 + par) % 4, c * 512:(c + 1) * 512],
                                                start=(k == 0), stop=(k == QT // 2 - 1))
                last.then_inc(pv_done, 1)

            def gather_o(head):
                pe.wait_ge(o_copied, head + 1)
                for c in range(2):
                    for t in range(QT // 2):
                        o = (c * (QT // 2) + t) * (D + 1)
                        last = nc.tensor.matmul(T.pM[:, o:o + D + 1], T.Osb[:, t * P:(t + 1) * P], T.osel[:, c, :],
                                                start=True, stop=True)
                last.then_inc(ot_ready, 1)

            def body(i, do_a, do_s, do_b):
                for n in range(SLOTS):
                    e, t = n // QT, n % QT
                    if do_b:
                        gb = (i - 2) * SLOTS + n
                        first = isinstance(i, int) and i == 2 and n == 0
                        if t == 0:
                            pe.wait_ge(b_load[e], (i - 1) * 32)
                            pe.wait_ge(aux_load[e], (i - 1) * 16)
                        if not first:
                            pe.wait_ge(e_ready, gb)
                        for c in range(2):
                            last = nc.tensor.matmul(T.pW[:, c * 512:(c + 1) * 512], T.KB[0:WROWS, e, t * P:(t + 1) * P],
                                                    T.QB[0:WROWS, e, c * 512:(c + 1) * 512], start=True, stop=True)
                        last.then_inc(w_ready, 1)
                    if do_a:
                        ga = i * SLOTS + n
                        if t == 0:
                            pe.wait_ge(a_load[e], (i + 1) * 32)
                        if not (isinstance(i, int) and i == 0 and n == 0):
                            pe.wait_ge(a_copied, ga)
                        for c in range(2):
                            last = nc.tensor.matmul(T.pA[:, c * 512:(c + 1) * 512], T.QA[0:KROWS, e, t * P:(t + 1) * P],
                                                    T.KA[0:KROWS, e, c * 512:(c + 1) * 512], start=True, stop=True)
                        last.then_inc(a_ready, 1)
                    if do_b:
                        if not first:
                            pe.wait_ge(p_ready, gb)
                        for c in range(2):
                            last = nc.tensor.matmul(T.pU[:, c * 512:(c + 1) * 512], T.KB[0:UROWS, e, t * P:(t + 1) * P],
                                                    T.QB[0:UROWS, e, c * 512:(c + 1) * 512], start=True, stop=True)
                        last.then_inc(u_ready, 1)
                        if n % 2 == 0 and not first:
                            products(i, n)
                        if t == 2 and not (isinstance(i, int) and i == 2 and e == 0):
                            if do_s:
                                pe.wait_ge(pos_used if n == 2 else selT_copied, i)
                            elif n == 2:
                                pe.wait_ge(rows_copied, PAIRS)
                            else:
                                pe.wait_ge(o_done, 2 * (i - 2))
                            gather_o(2 * (i - 2) + e - 1)
                    if not do_s:
                        continue
                    if n == 1:
                        pe.wait_ge(st_taken, i)
                        if at_least(i, 2):
                            pe.wait_ge(rows_copied, i - 1)
                        F = T.Fb[:, :].rearrange("p (e t) -> p e t", e=2)
                        pos = T.pM[:, 0:SLOTS].rearrange("p (e t) -> p e t", e=2)
                        nc.tensor.matmul(pos, T.zeros_b[:, :], F, start=True, stop=False)
                        for s in range(1, QT):
                            nc.tensor.matmul(pos[:, :, s:QT], T.ones_b[:, :], F[:, :, 0:QT - s], start=False, stop=False)
                        last = nc.tensor.matmul(pos, T.tri[:, :], F, start=False, stop=True)
                        last.then_inc(pos_ready, 1)
                    if n == 4:
                        pe.wait_ge(sel_ready, i)
                        pe.wait_ge(qg_ready, i)
                        if do_b and not (isinstance(i, int) and i == 2):
                            pe.wait_ge(o_done, 2 * (i - 2))
                        for e2 in range(2):
                            for t2 in range(QT):
                                nc.tensor.matmul(T.pM[0:KROWS, e2 * CAP:(e2 + 1) * CAP], T.QG[:, e2, t2, :],
                                                 T.Sel[:, t2, e2, :], start=(t2 == 0), stop=(t2 == QT - 1))
                        for e2 in range(2):
                            for t2 in range(QT):
                                last = nc.tensor.matmul(T.pM[e2 * CAP:(e2 + 1) * CAP, P:P + 3], T.Sel[:, t2, e2, :],
                                                        T.st[:, e2 * QT + t2, :], start=(t2 == 0), stop=(t2 == QT - 1))
                        last.then_inc(gat_ready, 1)
                    if n in (5, 6):
                        pe.wait_ge(gat_used, i)
                        if n == 5:
                            pe.wait_ge(s_load, i * 64)
                        else:
                            pe.wait_ge(ss_copied, 2 * (i - 1) + 1)
                        for e2 in range(2):
                            last = nc.tensor.matmul(T.pM[e2 * CAP:(e2 + 1) * CAP, :], T.Qc[0:KROWS, e2 * CAP:(e2 + 1) * CAP],
                                                    T.KS[0:KROWS, e2, (n - 5) * 512:(n - 4) * 512], start=True, stop=True)
                        last.then_inc(ss_ready, 1)
                    if n == 8:
                        pe.wait_ge(ss_copied, 2 * i)
                        for t2 in range(QT):
                            last = nc.tensor.transpose(T.pM_b[:, t2 * P:(t2 + 1) * P], T.Sel[:, t2, :, :].rearrange("p e c -> p (e c)"), T.ident_b[:, :])
                        last.then_inc(selT_ready, 1)
                    if n == 14:
                        pe.wait_ge(tp_ready, i)
                        pe.wait_ge(selT_copied, i)
                        if do_b:
                            pe.wait_ge(o_done, 2 * (i - 2) + 1)
                        for t2 in range(QT):
                            nc.tensor.matmul(T.pM[:, t2 * 6:(t2 + 1) * 6], T.SelT[:, t2 * P:(t2 + 1) * P],
                                             T.tpm[:, :, :].rearrange("p e a -> p (e a)"), start=True, stop=True)
                        nc.tensor.matmul(T.pM[0:1, 64:65], T.badb[:, 0:1], T.ones_b[:, 0:1], start=True, stop=True).then_inc(sc_ready, 1)
                        pe.wait_ge(flag_ready, i)
                        pe.sem_inc(settled, 1)
                        flag = pe.value_load(T.flag[0:1, 0:1], min_val=0, max_val=P * 2)
                        with pe.If(flag > 0):
                            for m in range(SLOTS):
                                for hf in range(2):
                                    if m + hf:
                                        pe.wait_ge(fb_copied, (i - 1) * 2 * SLOTS + 2 * m + hf)
                                    nc.tensor.matmul(T.pM[:, :], T.QS[0:KROWS, m // QT, (m % QT) * P:(m % QT + 1) * P],
                                                     T.KS[0:KROWS, m // QT, hf * 512:(hf + 1) * 512], start=True, stop=True).then_inc(fb_ready, 1)
                        with pe.Else():
                            pe.sem_inc(fb_ready, 2 * SLOTS)
                        pe.wait_ge(fb_copied, i * 2 * SLOTS)
                        pe.wait_ge(rows_src, i)
                        nc.tensor.transpose(T.pM_b[0:96, 0:P], T.RP[:, :], T.ident_b[:, :]).then_inc(rowsT_ready, 1)
            iterations(pe, body)
            products(PAIRS + 1, SLOTS)
            pe.wait_ge(o_done, HEADS - 1)
            gather_o(HEADS - 1)


def iterations(eng, body):
    body(0, True, False, False)
    body(1, True, True, False)
    body(2, True, True, True)
    with eng.Fori(3, PAIRS) as i:
        body(i, True, True, True)
    body(PAIRS, False, True, True)
    body(PAIRS + 1, False, False, True)


def feed_forward(nc, T, out):
    sem = T.sem
    at_ready = sem("ff_attn"); att_ready = sem("ff_attnT_ready"); att_copied = sem("ff_attnT")
    pr_ready = sem("ff_proj"); x1_ready = sem("ff_x1"); var_ready = sem("ff_var"); std_ready = sem("ff_std")
    xhat_ready = sem("ff_xhat"); xt_ready = sem("ff_xt"); ht_ready = sem("ff_ht")
    lg_ready = sem("ff_logits"); oh_ready = sem("ff_onehot"); ohT_ready = sem("ff_ohT"); ohT_done = sem("ff_ohT_done")
    ohb_ready = sem("ff_ohb_ready"); mask_done = sem("ff_mask_done")
    xe_ready = sem("ff_xe"); xe_used = sem("ff_xe_used"); gu_ready = sem("ff_gu"); silu_done = sem("ff_silu")
    h_ready = sem("ff_h"); hm_ready = sem("ff_hm"); y_ready = sem("ff_y"); y_done = sem("ff_y_done")
    out_done = sem("ff_out"); chain = sem("ff_chain")
    NCH = B * S // CHUNK
    LN = FF_LINKS

    def loop(eng, body):
        body(0)
        with eng.Fori(1, NCH) as c:
            body(c)

    with nc.Block() as block:
        @block.sync
        def _(sp):
            def body(c):
                sp.wait_ge(y_done, c + 1)
                sp.dma_start(out[bass.ds(c * CHUNK, CHUNK), :].rearrange("(t p) c -> p t c", p=P), T.x2[:, :, :]).then_inc(out_done, 16)
            loop(sp, body)
            sp.wait_ge(out_done, NCH * 16)

        @block.gpsimd
        def _(pool):
            for c in range(NCH):
                b, t0 = c // 2, (c % 2) * CT
                if c:
                    pool.wait_ge(att_ready, c)
                for t in range(CT):
                    last = pool.tensor_copy(T.ast[:, t, :].rearrange("p (h d) -> p h d", d=D),
                                            T.attn[:, b * H:(b + 1) * H, t0 + t, :])
                last.then_inc(at_ready, 1)

        @block.scalar
        def _(act):
            for c in range(NCH):
                act.wait_ge(att_ready, c + 1)
                if c:
                    act.wait_ge(pr_ready, c)
                act.activation(T.attT[:, :], T.pO[:, :], ACT.Copy).then_inc(att_copied, 1)
                act.wait_ge(var_ready, c + 1)
                act.activation(T.std[:, :], T.mv[:, :, 1], ACT.Sqrt, bias=T.epsc[:, 0:1]).then_inc(std_ready, 1)
                act.wait_ge(ohT_ready, c + 1)
                if c:
                    act.wait_ge(ohb_ready, c * E)
                act.activation(T.ohT[:, :], T.pM[0:E, :], ACT.Copy).then_inc(ohT_done, 1)
                for e in range(E):
                    act.wait_ge(ohb_ready, c * E + e + 1)
                    if c and e == 0:
                        act.wait_ge(hm_ready, c)
                    act.activation(T.mask[:, e, :], (T.pM if e % 2 else T.pO)[:, :], ACT.Copy).then_inc(mask_done, 1)
                for k in range(2):
                    act.wait_ge(gu_ready, 2 * c + k + 1)
                    if c and k == 0:
                        act.wait_ge(h_ready, 2 * c)
                    act.activation(T.sg2[:, k, :], T.pA[:, :], ACT.Silu).then_inc(silu_done, 1)

        @block.vector
        def _(dve):
            def done(ins, s, value):
                ins.then_inc(s, 1)
                dve.wait_ge(s, value)

            for c in range(NCH):
                b = c // 2
                n = [c * LN]

                def link(ins):
                    n[0] += 1
                    ins.then_inc(chain, 1)
                    dve.wait_ge(chain, n[0])
                dve.wait_ge(pr_ready, c + 1)
                pr = T.pM[:, :].rearrange("p (t c) -> p t c", c=C)
                if c:
                    dve.wait_ge(y_done, c)
                link(dve.tensor_tensor(T.x1[:, :, :], pr, T.gates[:, b * C:(b + 1) * C].unsqueeze(1).broadcast_to([P, CT, C]), ALU.mult))
                done(dve.tensor_tensor(T.x1[:, :, :], T.x1[:, :, :], T.x[:, c * CT:(c + 1) * CT, :], ALU.add), x1_ready, c + 1)
                for t in range(CT):
                    link(dve.bn_stats(T.bn[:, t, :], T.x1[:, t, :]))
                for t in range(CT):
                    last = dve.bn_aggr(T.mv[:, t, :], T.bn[:, t, :])
                link(last)
                done(dve.tensor_scalar(T.veps[:, :], T.mv[:, :, 1], EPS, None, ALU.add), var_ready, c + 1)
                dve.wait_ge(std_ready, c + 1)
                link(dve.reciprocal(T.rs[:, :], T.std[:, :]))
                link(dve.tensor_tensor(T.rs[:, :], T.rs[:, :], T.veps[:, :], ALU.mult))
                link(dve.tensor_tensor(T.rs[:, :], T.rs[:, :], T.std[:, :], ALU.add))
                link(dve.tensor_scalar(T.rs[:, :], T.rs[:, :], 0.5, None, ALU.mult))
                link(dve.reciprocal(T.rs[:, :], T.rs[:, :]))
                for t in range(CT):
                    last = dve.tensor_scalar(T.xhat[:, t, :], T.x1[:, t, :], T.mv[:, t, 0:1], T.rs[:, t:t + 1], ALU.subtract, ALU.mult)
                last.then_inc(xhat_ready, 1)
                dve.wait_ge(xt_ready, c + 1)
                dve.tensor_scalar(T.hT[:, :], T.pO[:, :], T.mod[:, 4 * B + b:4 * B + b + 1], T.mod[:, 3 * B + b:3 * B + b + 1],
                                       ALU.mult, ALU.add).then_inc(ht_ready, 1)
                dve.wait_ge(lg_ready, c + 1)
                lg = T.pM[:, 0:CT * E].rearrange("p (t e) -> p t e", e=E)
                link(dve.tensor_copy(T.lg[:, :, :], lg))
                link(dve.tensor_reduce(T.mx[:, :], T.lg[:, :, :], AX.X, ALU.max))
                link(dve.tensor_tensor(T.lg[:, :, :], T.lg[:, :, :], T.mx[:, :].unsqueeze(2).broadcast_to([P, CT, E]), ALU.is_ge))
                link(dve.tensor_tensor(T.lg[:, :, :], T.lg[:, :, :], T.down_count[:, :].unsqueeze(1).broadcast_to([P, CT, E]), ALU.mult))
                link(dve.tensor_reduce(T.mx[:, :], T.lg[:, :, :], AX.X, ALU.max))
                dve.tensor_tensor(T.oh[:, :, :], T.lg[:, :, :], T.mx[:, :].unsqueeze(2).broadcast_to([P, CT, E]), ALU.is_equal).then_inc(oh_ready, 1)
                for e in range(E):
                    dve.wait_ge(mask_done, c * E + e + 1)
                    if e >= 2:
                        dve.wait_ge(xe_used, c * (E - 1) + e - 1)
                    elif c:
                        dve.wait_ge(xe_used, c * (E - 1))
                    dve.tensor_tensor(T.xe[:, e % 2, :], T.hT[:, :], T.mask[:, e, :], ALU.mult).then_inc(xe_ready, 1)
                for k in range(2):
                    dve.wait_ge(silu_done, 2 * c + k + 1)
                    done(dve.tensor_tensor(T.h[:, k, :], T.sg2[:, k, :], T.pU[:, :], ALU.mult), h_ready, 2 * c + k + 1)
                    if k == 0:
                        if c:
                            dve.wait_ge(y_ready, c)
                        for e in range(E):
                            last = dve.tensor_tensor(T.hm[:, e, :, :], T.h[:, 0, :].rearrange("p (f n) -> p f n", f=FB),
                                                     T.mask[:, e, :].unsqueeze(1).broadcast_to([P, FB, CHUNK]), ALU.mult)
                        last.then_inc(hm_ready, 1)
                dve.wait_ge(y_ready, c + 1)
                y = T.pW[:, 0:512].rearrange("p (t c) -> p t c", c=C)
                if c:
                    dve.wait_ge(out_done, 16 * c)
                link(dve.tensor_tensor(T.x2[:, :, :], y, T.gates[:, (B + b) * C:(B + b + 1) * C].unsqueeze(1).broadcast_to([P, CT, C]), ALU.mult))
                dve.tensor_tensor(T.x2[:, :, :], T.x2[:, :, :], T.x1[:, :, :], ALU.add).then_inc(y_done, 1)
                assert n[0] == (c + 1) * LN, n[0]

        @block.tensor
        def _(pe):
            wT = T.wT[:, 4 * C:].rearrange("p (k e f n) -> p k e f n", k=3, e=E + 1, f=FB)
            woT = T.wT[:, 3 * C:4 * C]
            for c in range(NCH):
                pe.wait_ge(at_ready, c + 1)
                for t in range(CT):
                    last = nc.tensor.transpose(T.pO[:, t * P:(t + 1) * P], T.ast[:, t, :], T.ident[:, :])
                last.then_inc(att_ready, 1)
                pe.wait_ge(att_copied, c + 1)
                for t in range(CT):
                    nc.tensor.matmul(T.pM[:, t * C:(t + 1) * C], T.attT[:, t * P:(t + 1) * P], woT, start=True, stop=False)
                    last = nc.tensor.matmul(T.pM[:, t * C:(t + 1) * C], T.ones_f[0:1, :], T.borow[0:1, :], start=False, stop=True)
                last.then_inc(pr_ready, 1)
                pe.wait_ge(xhat_ready, c + 1)
                for t in range(CT):
                    last = nc.tensor.transpose(T.pO[:, t * P:(t + 1) * P], T.xhat[:, t, :], T.ident[:, :])
                last.then_inc(xt_ready, 1)
                pe.wait_ge(ht_ready, c + 1)
                for t in range(CT):
                    last = nc.tensor.matmul(T.pM[:, t * E:(t + 1) * E], T.hT[:, t * P:(t + 1) * P], T.rT[:, :], start=True, stop=True)
                last.then_inc(lg_ready, 1)
                pe.wait_ge(oh_ready, c + 1)
                for t in range(CT):
                    last = nc.tensor.transpose(T.pM[0:E, t * P:(t + 1) * P], T.oh[:, t, :], T.ident[:, :])
                last.then_inc(ohT_ready, 1)
                pe.wait_ge(ohT_done, c + 1)

                def spread(e):
                    if e >= 2:
                        pe.wait_ge(mask_done, c * E + e - 1)
                    nc.tensor.matmul((T.pM if e % 2 else T.pO)[:, :], T.ident_b[0:E, e:e + 1].broadcast_to([E, P]), T.ohT[:, :],
                                     start=True, stop=True).then_inc(ohb_ready, 1)
                spread(0)
                spread(1)
                for e in range(E):
                    if e + 2 < E:
                        spread(e + 2)
                    pe.wait_ge(xe_ready, c * E + e + 1)
                    for k, ps in ((0, T.pA), (1, T.pU)):
                        for f in range(FB):
                            last = nc.tensor.matmul(ps[:, f * 512:(f + 1) * 512], wT[:, k, e, f, :], T.xe[:, e % 2, :],
                                                    start=(e == 0), stop=(e == E - 1))
                    last.then_inc(xe_used if e < E - 1 else gu_ready, 1)
                pe.wait_ge(h_ready, 2 * c + 1)
                for k, ps in ((0, T.pA), (1, T.pU)):
                    for f in range(FB):
                        last = nc.tensor.matmul(ps[:, f * 512:(f + 1) * 512], wT[:, k, E, f, :], T.hT[:, :], start=True, stop=True)
                last.then_inc(gu_ready, 1)
                pe.wait_ge(hm_ready, c + 1)
                pe.wait_ge(h_ready, 2 * c + 2)
                for t in range(CT):
                    for e in range(E + 1):
                        for f in range(FB):
                            lhs = T.hm[:, e, f, t * P:(t + 1) * P] if e < E else T.h[:, 1, f * 512 + t * P:f * 512 + (t + 1) * P]
                            last = nc.tensor.matmul(T.pW[:, t * C:(t + 1) * C], lhs, wT[:, 2, e, f, :],
                                                    start=(e == 0 and f == 0), stop=(e == E and f == FB - 1))
                last.then_inc(y_ready, 1)



class Places:

    def __init__(self, nc, ctx):
        def sb(name, shape, dt):
            return ctx.enter_context(nc.sbuf_tensor(name, shape, dt))

        self.ident = sb("ident", [P, P], F32)
        self.ident_b = sb("ident_b", [P, P], BF16)
        self.tri = sb("tri", [P, P], BF16)
        self.ones_b = sb("ones_b", [P, P], BF16)
        self.zeros_b = sb("zeros_b", [P, P], BF16)
        self.ones_f = sb("ones_f", [P, P], F32)
        self.iota_i = sb("iota_i", [P, P], I32)
        self.iota = sb("iota", [P, P], F32)
        self.down_count = sb("down_count", [P, E], F32)
        self.epsc = sb("epsc", [P, 1], F32)
        self.half = sb("half", [P, 2], F32)
        self.osel = sb("osel", [P, 2, D + 1], F32)
        self.thr0 = sb("thr0", [P, 1], F32)
        self.thrc = sb("thrc", [P, 1], F32)
        self.negthr = sb("negthr", [P, 1], F32)
        self.mod = sb("mod", [P, 6 * B], F32)
        self.gates = sb("gates", [P, 2 * B * C], F32)
        self.wT = sb("wT", [P, NWT * C], F32)
        self.rT = sb("rT", [P, E], F32)
        self.x = sb("x", [P, B * QT, C], F32)
        self.V = sb("V", [P, HEADS, QT, D], F32)
        self.Qtok = sb("Qtok", [P, HEADS, QT, PARTS, D], BF16)
        self.attn = sb("attn", [P, HEADS, QT, D], F32)
        self.QB = sb("QB", [P, 2, S], BF16)
        self.KB = sb("KB", [P, 2, S], BF16)
        self.V32 = sb("V32", [P, 2, QT, VW], F32)
        self.tpm = sb("tpm", [P, 2, PARTS], BF16)
        self.bn = sb("bn", [P, CT, 6], F32)
        self.mv = sb("mv", [P, CT, 2], F32)
        self.veps = sb("veps", [P, CT], F32)
        self.std = sb("std", [P, CT], F32)
        self.rs = sb("rs", [P, CT], F32)
        self.xhat = sb("xhat", [P, CT, C], F32)
        self.hT = sb("hT", [P, CHUNK], F32)
        self.borow = sb("borow", [1, C], F32)
        ps = ctx.enter_context(nc.psum_tensor("ps", [P, 4096], F32))
        self.pA, self.pU, self.pW = ps[:, 0:1024], ps[:, 1024:2048], ps[:, 2048:3072]
        self.pO, self.pM = ps[:, 3072:3584], ps[:, 3584:4096]
        self.pUW_b, self.pM_b = ps[:, 1024:3072].bitcast(BF16), ps[:, 3584:4096].bitcast(BF16)
        self.sem = lambda name: ctx.enter_context(nc.semaphore(name))


def place_prepare(T, nc, ctx):
    def sb(name, shape, dt):
        return ctx.enter_context(nc.sbuf_tensor(name, shape, dt))

    T.nat = sb("nat", [P, NWT, C], F32)
    T.cT = sb("cT", [P, B], F32)
    T.sc = sb("sc", [P, B], F32)
    T.wmod = sb("wmod", [P, 6 * C], F32)
    T.gabs = sb("gabs", [P, 2 * B * C], F32)
    T.qkp = sb("qkp", [P, CT, PARTS, 2 * C], BF16)
    T.rem = sb("rem", [P, 2 * C], F32)
    T.qkT = sb("qkT", [P, 2 * PARTS, CHUNK], BF16)
    T.rt_nat = sb("rt_nat", [E, C], F32)


def place_attention(T, nc, ctx):
    def sb(name, shape, dt):
        return ctx.enter_context(nc.sbuf_tensor(name, shape, dt))

    T.QA = sb("QA", [P, 2, S], BF16)
    T.KA = sb("KA", [P, 2, S], BF16)
    T.QS = sb("QS", [P, 2, S], BF16)
    T.KS = sb("KS", [P, 2, S], BF16)
    T.E = sb("E", [P, 4, S], F32)
    T.Sc = sb("Sc", [P, 2, S], F32)
    T.Ss = sb("Ss", [P, S], F32)
    T.Wm = sb("Wm", [P, S], F32)
    T.junk_a = sb("junk_a", [P, 2, S], BF16)
    T.junk_a2 = sb("junk_a2", [P, S], BF16)
    T.M = sb("M", [P, SLOTS], F32)
    T.Mp = sb("Mp", [P, SLOTS], F32)
    T.cnt = sb("cnt", [P, SLOTS], F32)
    T.Fb = sb("Fb", [P, SLOTS], BF16)
    T.st = sb("st", [P, SLOTS, 3], BF16)
    T.posF = sb("posF", [P, SLOTS], F32)
    T.Sel = sb("Sel", [P, QT, 2, CAP], BF16)
    T.SelT = sb("SelT", [P, S], BF16)
    T.QG = sb("QG", [P, 2, QT, KROWS], BF16)
    T.gs = sb("gs", [P, 3], F32)
    T.sl = sb("sl", [P, 1], F32)
    T.dt = sb("dt", [P, 1], F32)
    T.nd = sb("nd", [P, 1], F32)
    T.tc = sb("tc", [P, len(DAMP) + 1], F32)
    T.sg = sb("sg", [P, len(DAMP)], F32)
    T.c1 = sb("c1", [P, 1], F32)
    T.W8 = sb("W8", [P, 8], F32)
    T.h8 = sb("h8", [P, 8], F32)
    T.ix = sb("ix", [P, 1], F32)
    T.ix1 = sb("ix1", [P, 1], F32)
    T.kth = sb("kth", [P, 1], F32)
    T.nxt = sb("nxt", [P, 1], F32)
    T.t3 = sb("t3", [P, PARTS], BF16)
    T.bad = sb("bad", [P, 2], F32)
    T.badb = sb("badb", [P, 1], BF16)
    T.flag = sb("flag", [P, 1], I32)
    T.Tt = sb("Tt", [P, SLOTS], F32)
    T.X = sb("X", [P, 2, SLOTS], F32)
    T.RP = sb("RP", [P, 2 * 2 * PARTS * QT], BF16)
    T.Osb = sb("Osb", [P, CHUNK], F32)
    T.rl = sb("rl", [P, QT], F32)
    T.lo = sb("lo", [P, 1], F32)
    T.mid = sb("mid", [P, 1], F32)
    T.stp = sb("stp", [P, 1], F32)
    T.Qc = sb("Qc", [KROWS, P], BF16)
    T.rowsT = sb("rowsT", [2 * 2 * PARTS * QT, P], BF16)


def place_feed_forward(T, nc, ctx):
    def sb(name, shape, dt):
        return ctx.enter_context(nc.sbuf_tensor(name, shape, dt))

    T.ast = sb("ast", [P, CT, C], F32)
    T.attT = sb("attT", [P, CHUNK], F32)
    T.x1 = sb("x1", [P, CT, C], F32)
    T.x2 = sb("x2", [P, CT, C], F32)
    T.lg = sb("lg", [P, CT, E], F32)
    T.mx = sb("mx", [P, CT], F32)
    T.oh = sb("oh", [P, CT, E], F32)
    T.mask = sb("mask", [P, E, CHUNK], BF16)
    T.xe = sb("xe", [P, 2, CHUNK], F32)
    T.sg2 = sb("sg2", [P, 2, FB * CHUNK], F32)
    T.h = sb("h", [P, 2, FB * CHUNK], F32)
    T.hm = sb("hm", [P, E, FB, CHUNK], F32)
    T.ohT = sb("ohT", [E, CHUNK], BF16)


def build(nc, x, wq, wk, wv, wo, bo, thr, up, gate, down, router, up_s, gate_s, down_s, c_in, wmod, out, qk_aug):
    with ExitStack() as kept:
        T = Places(nc, kept)
        with ExitStack() as ctx:
            place_prepare(T, nc, ctx)
            prepare(nc, T, x.rearrange("b s c -> (b s) c"), wq, wk, wv, wo, bo, thr, up, gate, down, router,
                    up_s, gate_s, down_s, c_in, wmod, qk_aug)
        with ExitStack() as ctx:
            place_attention(T, nc, ctx)
            attention(nc, T, qk_aug)
        with ExitStack() as ctx:
            place_feed_forward(T, nc, ctx)
            feed_forward(nc, T, out.rearrange("b s c -> (b s) c"))


def kernel(**inputs):
    import numpy as np
    import concourse.bacc as bacc
    from concourse.bass_utils import run_bass_kernel_spmd

    nc = bacc.Bacc("TRN2", target_bir_lowering=False, num_devices=1)
    names = ["attn_x", "attn_Wq", "attn_Wk", "attn_Wv", "attn_Wo", "attn_bo", "attn_adaptive_threshold", "ffn_up", "ffn_gate",
             "ffn_down", "ffn_router", "ffn_w_up_s", "ffn_w_gate_s", "ffn_w_down_s", "c", "wmod"]
    arrays, args = {}, []
    for name in names:
        a = np.ascontiguousarray(inputs["L0_" + name])
        arrays["in_" + name] = a
        args.append(nc.dram_tensor("in_" + name, a.shape, mybir.dt.from_np(a.dtype), kind="ExternalInput").ap())
    out = nc.dram_tensor("out_0", (B, S, C), F32, kind="ExternalOutput").ap()
    qk_aug = nc.dram_tensor("qk_aug", (2, HEADS, KROWS, S), BF16).ap()
    build(nc, *args, out, qk_aug)
    return run_bass_kernel_spmd(nc, [arrays], core_ids=[0]).results[0]["out_0"]
```

```python
import concourse.bass as bass
from concourse import mybir
from contextlib import ExitStack

F32 = mybir.dt.float32
BF16 = mybir.dt.bfloat16
I32 = mybir.dt.int32
ACT = mybir.ActivationFunctionType
ALU = mybir.AluOpType
AX = mybir.AxisListType

P = 128
B, S, C = 2, 1024, 128
H, D = 16, 8
QT = S // P
HEADS = B * H
PAIRS = HEADS // 2
SLOTS = 2 * QT
KEEP = S // 2
E, F = 8, 256
FB = F // P
PARTS = 3
REP = PARTS * PARTS
KROWS = REP * D
AUX = 96
UROWS = AUX + PARTS
WROWS = AUX + 2 * PARTS
CAP = P // 2
VW = 32
CHUNK = 512
CT = CHUNK // P
EPS = 1e-5
NWT = 4 + 3 * (E + 1) * FB
POOL_LINKS = 35
LAG = 4
FF_LINKS = 17
DAMP = [1.0, 1.0, 0.6, 0.9, 0.5]
SLOPE = 2.5066 / S / 4.5 / 2
SLACK = 2.0 ** -21
BISECT = 36


def prepare(nc, T, x, wq, wk, wv, wo, bo, thr, up, gate, down, router, up_s, gate_s, down_s, c_in, wmod, qk_aug):
    sem = T.sem
    loads = sem("prep_loads"); att_loads = sem("prep_att_loads"); cload = sem("prep_c_load"); consts = sem("prep_consts")
    chain_p = sem("prep_chain_pool")
    silu_done = sem("prep_silu"); mod_ready = sem("prep_mod_ready"); mod_done = sem("prep_mod_done")
    wt_ready = sem("prep_wt_ready"); wt_done = sem("prep_wt_done")
    chain = sem("prep_chain_dve"); chain_a = sem("prep_chain_act")
    x_loaded = [sem(f"prep_x_loaded{n}") for n in range(2)]
    var_ready = sem("prep_var"); std_ready = sem("prep_std"); xhat_ready = sem("prep_xhat")
    xt_ready = sem("prep_xt"); ht_ready = sem("prep_ht")
    qkv_ready = sem("prep_qkv"); v_done = sem("prep_v_done"); part1 = sem("prep_part1")
    qkv_used = sem("prep_qkv_used"); parts_ready = sem("prep_parts")
    tp_ready = sem("prep_tp_ready"); tp_done = sem("prep_tp_done"); qtok_done = sem("prep_qtok_done")
    stored = [sem(f"prep_stored{w}") for w in range(2)]
    nat = T.nat
    groups = (NWT + 3) // 4
    NCH = B * S // CHUNK

    with nc.Block() as block:
        @block.sync
        def _(sp):
            for b in range(B):
                sp.dma_start(T.cT[:, b:b + 1], c_in[b, :].rearrange("(c o) -> c o", o=1)).then_inc(cload, 16)
            sp.dma_start(T.wmod[:, :], wmod).then_inc(cload, 16)
            sp.dma_start(T.borow[:, :], bo.rearrange("(a n) -> a n", a=1)).then_inc(cload, 16)
            sp.dma_start(T.thr0[:, :], thr.partition_broadcast(P)).then_inc(cload, 16)
            sp.dma_start(T.x[:, 0:CT, :], x[0:CHUNK, :].rearrange("(t p) c -> p t c", p=P)).then_inc(x_loaded[0], 16)
            for n, w in enumerate((wq, wk, wv, wo)):
                sp.dma_start(nat[:, n, :], w).then_inc(att_loads, 16)
            sp.dma_start(T.x[:, CT:, :], x[CHUNK:, :].rearrange("(t p) c -> p t c", p=P)).then_inc(x_loaded[1], 16)
            n = 4
            for w, ws in ((gate, gate_s), (up, up_s)):
                sp.dma_start(nat[:, n:n + E * FB, :], w.rearrange("e (f p) c -> p (e f) c", p=P)).then_inc(loads, 16)
                sp.dma_start(nat[:, n + E * FB:n + (E + 1) * FB, :], ws.rearrange("(f p) c -> p f c", p=P)).then_inc(loads, 16)
                n += (E + 1) * FB
            sp.dma_start(nat[:, n:n + E * FB, :].rearrange("p (e f) n -> p e (f n)", e=E), down.rearrange("e c h -> c e h")).then_inc(loads, 16)
            sp.dma_start(nat[:, n + E * FB:n + (E + 1) * FB, :].rearrange("p f n -> p (f n)"), down_s).then_inc(loads, 16)
            sp.dma_start(T.rt_nat[:, :], router).then_inc(loads, 16)
            for ch in range(NCH):
                for w in range(2):
                    sp.wait_ge(tp_done, ch * 2 + w + 1)
                    for j in range(REP):
                        part = j // PARTS if w else j % PARTS
                        dst = qk_aug[w, (ch * CHUNK // S) * H:(ch * CHUNK // S + 1) * H, j * D:(j + 1) * D,
                                     ch * CHUNK % S:ch * CHUNK % S + CHUNK]
                        sp.dma_start(dst, T.qkT[:, w * PARTS + part, :]).then_inc(stored[w], 16)
            for w in range(2):
                sp.wait_ge(stored[w], NCH * REP * 16)

        @block.gpsimd
        def _(pool):
            n = [0]

            def link(ins):
                n[0] += 1
                ins.then_inc(chain_p, 1)
                pool.wait_ge(chain_p, n[0])
            link(pool.memset(T.ident[:, :], 0.0))
            link(pool.affine_select(out=T.ident[:, :], in_=T.ident[:, :], compare_op=ALU.not_equal, fill=1.0,
                                    base=0, pattern=[[-1, P]], channel_multiplier=1))
            pool.tensor_copy(T.ident_b[:, :], T.ident[:, :]).then_inc(consts, 1)
            link(pool.memset(T.tri[:, :], 1.0))
            link(pool.affine_select(out=T.tri[:, :], in_=T.tri[:, :], compare_op=ALU.is_ge, fill=0.0,
                                    base=0, pattern=[[1, P]], channel_multiplier=-1))
            link(pool.memset(T.ones_b[:, :], 1.0))
            link(pool.memset(T.zeros_b[:, :], 0.0))
            link(pool.memset(T.ones_f[:, :], 1.0))
            link(pool.iota(T.iota_i[:, :], pattern=[[1, P]], base=1, channel_multiplier=0))
            link(pool.tensor_copy(T.iota[:, :], T.iota_i[:, :]))
            for e in range(2):
                link(pool.memset(T.QB[64:P, e, :], 0.0))
                link(pool.memset(T.KB[64:P, e, :], 0.0))
                link(pool.memset(T.KB[AUX:P, e, :], 1.0))
                link(pool.memset(T.V32[:, e, :, :], 0.0))
                link(pool.memset(T.V32[:, e, :, D:D + 1], 1.0))
            link(pool.memset(T.tpm[:, :, :], 0.0))
            link(pool.memset(T.half[:, :], 0.0))
            link(pool.memset(T.half[0:CAP, 0:1], 1.0))
            link(pool.memset(T.half[CAP:P, 1:2], 1.0))
            link(pool.memset(T.osel[:, :, :], 0.0))
            for c in range(2):
                for par in range(2):
                    link(pool.affine_select(out=T.osel[:, c, :], in_=T.osel[:, c, :], compare_op=ALU.not_equal, fill=1.0,
                                            base=-32 * (2 * par + c), pattern=[[-1, D + 1]], channel_multiplier=1))
            link(pool.iota(T.iota_i[:, 0:E], pattern=[[-1, E]], base=E, channel_multiplier=0))
            link(pool.tensor_copy(T.down_count[:, :], T.iota_i[:, 0:E]))
            pool.memset(T.epsc[:, :], EPS).then_inc(consts, 1)
            for ch in range(NCH):
                pool.wait_ge(parts_ready, (ch + 1) * CT)
                b, t0 = ch * CHUNK // S, (ch % (S // CHUNK)) * CT
                for t in range(CT):
                    for p in range(PARTS):
                        last = pool.tensor_copy(T.Qtok[:, b * H:(b + 1) * H, t0 + t, p, :],
                                                T.qkp[:, t, p, 0:C].rearrange("p (h d) -> p h d", d=D))
                last.then_inc(qtok_done, 1)

        @block.scalar
        def _(act):
            act.wait_ge(cload, 80)
            act.activation(T.sc[:, :], T.cT[:, :], ACT.Silu).then_inc(silu_done, 1)
            act.wait_ge(consts, 2)
            for ch in range(NCH):
                act.wait_ge(var_ready, ch + 1)
                act.activation(T.std[:, :], T.mv[:, :, 1], ACT.Sqrt, bias=T.epsc[:, 0:1]).then_inc(std_ready, 1)
                for t in range(CT):
                    g = ch * CT + t
                    b, tt = g // QT, g % QT
                    act.wait_ge(qkv_ready, g + 1)
                    if g >= CT:
                        act.wait_ge(qtok_done, ch)
                        act.wait_ge(tp_ready, 2 * ch)
                    act.activation(T.qkp[:, t, 0, :], T.pA[:, (g % 2) * 512:(g % 2) * 512 + 2 * C], ACT.Copy).then_inc(part1, 1)
                    act.activation(T.V[:, b * H:(b + 1) * H, tt, :],
                                   T.pA[:, (g % 2) * 512 + 2 * C:(g % 2) * 512 + 3 * C].rearrange("p (h d) -> p h d", d=D),
                                   ACT.Copy).then_inc(v_done, 1)
                for w in range(2):
                    act.wait_ge(tp_ready, ch * 2 + w + 1)
                    if ch:
                        act.wait_ge(stored[w], ch * REP * 16)
                    act.activation(T.qkT[:, w * PARTS:(w + 1) * PARTS, :],
                                   T.pUW_b[:, w * 2048:w * 2048 + PARTS * CHUNK].rearrange("p (a n) -> p a n", a=PARTS),
                                   ACT.Copy).then_inc(tp_done, 1)

        @block.vector
        def _(dve):
            def done(ins, s, value):
                ins.then_inc(s, 1)
                dve.wait_ge(s, value)

            n = [0]

            def link(ins):
                n[0] += 1
                ins.then_inc(chain, 1)
                dve.wait_ge(chain, n[0])
            dve.wait_ge(cload, 80)
            link(dve.tensor_scalar(T.thrc[:, :], T.thr0[:, :], 0.0, 1.0, ALU.max, ALU.min))
            link(dve.tensor_scalar(T.negthr[:, :], T.thrc[:, :], -1.0, None, ALU.mult))
            dve.wait_ge(mod_ready, 1)
            link(dve.tensor_copy(T.mod[:, :], T.pO[:, 0:6 * B]))
            for m in (1, 4):
                link(dve.tensor_scalar(T.mod[:, m * B:(m + 1) * B], T.mod[:, m * B:(m + 1) * B], 1.0, None, ALU.add))
            g = T.gates[:, :]
            link(dve.tensor_copy(g, T.pM[:, 0:2 * B * C]))
            link(dve.scalar_tensor_tensor(T.gabs[:, :], g, -1.0, g, ALU.mult, ALU.max))
            link(dve.tensor_scalar(g, g, 0.0, 2.0, ALU.is_ge, ALU.mult))
            link(dve.tensor_scalar(T.gabs[:, :], T.gabs[:, :], 0.25, None, ALU.max))
            link(dve.tensor_scalar(g, g, -1.0, None, ALU.add))
            dve.tensor_tensor(g, g, T.gabs[:, :], ALU.mult).then_inc(mod_done, 1)
            for k in range(groups):
                dve.wait_ge(wt_ready, k + 1)
                m = min(4, NWT - 4 * k)
                src = T.pO if k % 2 == 0 else T.pM
                if k == 0:
                    dve.tensor_scalar(T.wT[:, 0:C], src[:, 0:C], float(D) ** -0.5, None, ALU.mult)
                    dve.tensor_copy(T.wT[:, C:4 * C], src[:, C:4 * C]).then_inc(wt_done, 1)
                else:
                    dve.tensor_copy(T.wT[:, 4 * k * C:(4 * k + m) * C], src[:, 0:m * C]).then_inc(wt_done, 1)
            dve.wait_ge(wt_ready, groups + 1)
            dve.tensor_copy(T.rT[:, :], T.pO[:, 0:E]).then_inc(wt_done, 1)
            for ch in range(NCH):
                b = ch * CHUNK // S
                dve.wait_ge(x_loaded[min(ch, 1)], 16)
                if ch:
                    dve.wait_ge(std_ready, ch)
                for t in range(CT):
                    link(dve.bn_stats(T.bn[:, t, :], T.x[:, ch * CT + t, :]))
                for t in range(CT):
                    last = dve.bn_aggr(T.mv[:, t, :], T.bn[:, t, :])
                link(last)
                done(dve.tensor_scalar(T.veps[:, :], T.mv[:, :, 1], EPS, None, ALU.add), var_ready, ch + 1)
                dve.wait_ge(std_ready, ch + 1)
                link(dve.reciprocal(T.rs[:, :], T.std[:, :]))
                link(dve.tensor_tensor(T.rs[:, :], T.rs[:, :], T.veps[:, :], ALU.mult))
                link(dve.tensor_tensor(T.rs[:, :], T.rs[:, :], T.std[:, :], ALU.add))
                link(dve.tensor_scalar(T.rs[:, :], T.rs[:, :], 0.5, None, ALU.mult))
                link(dve.reciprocal(T.rs[:, :], T.rs[:, :]))
                if ch:
                    dve.wait_ge(xt_ready, ch)
                for t in range(CT):
                    last = dve.tensor_scalar(T.xhat[:, t, :], T.x[:, ch * CT + t, :], T.mv[:, t, 0:1],
                                             T.rs[:, t:t + 1], ALU.subtract, ALU.mult)
                last.then_inc(xhat_ready, 1)
                dve.wait_ge(xt_ready, ch + 1)
                if ch:
                    dve.wait_ge(qkv_ready, ch * CT)
                dve.tensor_scalar(T.hT[:, :], T.pO[:, :], T.mod[:, B + b:B + b + 1], T.mod[:, b:b + 1],
                                  ALU.mult, ALU.add).then_inc(ht_ready, 1)
                for t in range(CT):
                    g = ch * CT + t
                    src = T.pA[:, (g % 2) * 512:(g % 2) * 512 + 2 * C]
                    dve.wait_ge(v_done, g + 1)
                    dve.wait_ge(part1, g + 1)
                    done(dve.tensor_tensor(T.rem[:, :], src, T.qkp[:, t, 0, :], ALU.subtract), qkv_used, g + 1)
                    link(dve.tensor_copy(T.qkp[:, t, 1, :], T.rem[:, :]))
                    done(dve.tensor_tensor(T.qkp[:, t, 2, :], T.rem[:, :], T.qkp[:, t, 1, :], ALU.subtract), parts_ready, g + 1)

        @block.tensor
        def _(pe):
            pe.wait_ge(cload, 80)
            pe.wait_ge(silu_done, 1)
            for m in range(6):
                nc.tensor.matmul(T.pO[:, m * B:(m + 1) * B], T.wmod[:, m * C:(m + 1) * C], T.sc[:, :], start=True, stop=True)
            for k, m in enumerate((2, 5)):
                for b in range(B):
                    last = nc.tensor.matmul(T.pM[:, (k * B + b) * C:(k * B + b + 1) * C],
                                            T.sc[:, b:b + 1].broadcast_to([P, P]), T.wmod[:, m * C:(m + 1) * C],
                                            start=True, stop=True)
            last.then_inc(mod_ready, 1)
            pe.wait_ge(mod_done, 1)
            pe.wait_ge(consts, 2)
            for k in range(groups):
                if k == 0:
                    pe.wait_ge(att_loads, 4 * 16)
                else:
                    pe.wait_ge(loads, 7 * 16)
                if k >= 2:
                    pe.wait_ge(wt_done, k - 1)
                dst = T.pO if k % 2 == 0 else T.pM
                for j in range(min(4, NWT - 4 * k)):
                    last = nc.tensor.transpose(dst[:, j * C:(j + 1) * C], nat[:, 4 * k + j, :], T.ident[:, :])
                last.then_inc(wt_ready, 1)
            pe.wait_ge(wt_done, groups)
            nc.tensor.transpose(T.pO[:, 0:E], T.rt_nat[:, :], T.ident[0:E, 0:E]).then_inc(wt_ready, 1)
            pe.wait_ge(wt_done, groups + 1)
            for ch in range(NCH):
                pe.wait_ge(xhat_ready, ch + 1)
                if ch:
                    pe.wait_ge(ht_ready, ch)
                for t in range(CT):
                    last = nc.tensor.transpose(T.pO[:, t * P:(t + 1) * P], T.xhat[:, t, :], T.ident[:, :])
                last.then_inc(xt_ready, 1)
                pe.wait_ge(ht_ready, ch + 1)
                for t in range(CT):
                    g = ch * CT + t
                    if g >= 2:
                        pe.wait_ge(qkv_used, g - 1)
                    nc.tensor.matmul(T.pA[:, (g % 2) * 512:(g % 2) * 512 + 3 * C], T.hT[:, t * P:(t + 1) * P],
                                     T.wT[:, 0:3 * C], start=True, stop=True).then_inc(qkv_ready, 1)
                pe.wait_ge(parts_ready, (ch + 1) * CT)
                for w in range(2):
                    if ch:
                        pe.wait_ge(tp_done, 2 * (ch - 1) + w + 1)
                    for p in range(PARTS):
                        for t in range(CT):
                            o = w * 2048 + p * CHUNK + t * P
                            last = nc.tensor.transpose(T.pUW_b[:, o:o + P], T.qkp[:, t, p, w * C:(w + 1) * C], T.ident_b[:, :])
                    last.then_inc(tp_ready, 1)


def attention(nc, T, qk_aug):
    sem = T.sem
    a_load = [sem(f"a_load{e}") for e in range(2)]
    b_load = [sem(f"b_load{e}") for e in range(2)]
    aux_load = [sem(f"aux_load{e}") for e in range(2)]
    s_load = sem("s_load")
    a_ready, a_copied, a_counted = sem("a_ready"), sem("a_copied"), sem("a_counted")
    u_ready, w_ready, e_ready, p_ready = sem("u_ready"), sem("w_ready"), sem("e_ready"), sem("p_ready")
    pv_done, o_copied, ot_ready, o_done, o_chain = sem("pv_done"), sem("o_copied"), sem("ot_ready"), sem("o_done"), sem("o_chain")
    v_ready, qg_ready = sem("v_ready"), sem("qg_ready")
    m_taken, m_kept, st_taken, flagged = sem("m_taken"), sem("m_kept"), sem("st_taken"), sem("flagged")
    pos_ready, pos_used, sel_ready = sem("pos_ready"), sem("pos_used"), sem("sel_ready")
    gat_ready, gat_used = sem("gat_ready"), sem("gat_used")
    ss_ready, ss_copied, step_t, step_c = sem("ss_ready"), sem("ss_copied"), sem("step_t"), sem("step_c")
    selT_ready, selT_copied = sem("selT_ready"), sem("selT_copied")
    cnt_ready, w8_ready, z_ready, kth_ready = sem("cnt_ready"), sem("w8_ready"), sem("z_ready"), sem("kth_ready")
    tp_ready, sc_ready, flag_ready, t_ready, t_final = (sem("tparts_ready"), sem("scattered"), sem("flag_ready"),
                                                        sem("t_ready"), sem("t_final"))
    rows_src, rowsT_ready, rows_copied = sem("rows_src"), sem("rowsT_ready"), sem("rows_copied")
    chain, chain_p = sem("search_chain"), sem("search_chain_pool")
    fb_ready, fb_copied, fb_chain = sem("fb_ready"), sem("fb_copied"), sem("fb_chain")
    settled = sem("settled")
    FBN = SLOTS * (2 + 5 * BISECT + 4)
    K0 = len(DAMP)
    last_i = PAIRS + 2

    def static(i):
        return isinstance(i, int)

    def iterations(eng, body):
        for i in range(3):
            body(i)
        with eng.Fori(3, PAIRS - 1) as i:
            body(i)
        for i in range(PAIRS - 1, last_i + 1):
            body(i)

    def scores(i):
        return not static(i) or i < PAIRS

    def searches(i):
        return not static(i) or 1 <= i <= PAIRS

    def b_tile(i, n):
        g = (i - 2) * SLOTS + n - LAG
        if static(i) and not 0 <= g < PAIRS * SLOTS:
            return None
        k = (n - LAG) % SLOTS
        return g, k // QT, k % QT

    def head_before(i, n):
        return 2 * (i - 2) + (n - LAG) // QT - 1

    with nc.Block() as block:
        @block.sync
        def _(sp):
            def load(dst, w, head, s):
                sp.dma_start(dst, qk_aug[w, bass.ds(head, 1), :, :].rearrange("o r n -> (o r) n")).then_inc(s, 16)

            def aux(e):
                sp.dma_start(T.QB[AUX:WROWS, e, :], T.rowsT[e * 48:(e + 1) * 48, :]).then_inc(aux_load[e], 16)

            def load_a(i, e):
                sp.wait_ge(a_ready, i * SLOTS + (e + 1) * QT)
                load(T.QA[0:KROWS, e, :], 0, 2 * i + 2 + e, a_load[e])
                load(T.KA[0:KROWS, e, :], 1, 2 * i + 2 + e, a_load[e])

            def body(i):
                more_a = not static(i) or i < PAIRS - 1
                if b_tile(i, LAG):
                    if not (static(i) and i == 2):
                        sp.wait_ge(p_ready, (i - 2) * SLOTS)
                    load(T.QB[0:KROWS, 1, :], 0, 2 * i - 3, b_load[1])
                    load(T.KB[0:KROWS, 1, :], 1, 2 * i - 3, b_load[1])
                    aux(1)
                if more_a:
                    load_a(i, 0)
                if searches(i):
                    if b_tile(i, LAG):
                        sp.wait_ge(p_ready, (i - 2) * SLOTS + QT)
                    load(T.QB[0:KROWS, 0, :], 0, 2 * i - 2, b_load[0])
                    load(T.KB[0:KROWS, 0, :], 1, 2 * i - 2, b_load[0])
                if scores(i):
                    if searches(i):
                        sp.wait_ge(t_final, i)
                    for w, dst in ((1, T.KS), (0, T.QS)):
                        for e in range(2):
                            load(dst[0:KROWS, e, :], w, 2 * i + e, s_load)
                if searches(i):
                    sp.wait_ge(rows_copied, i)
                    aux(0)
                if more_a:
                    load_a(i, 1)

            for e in range(2):
                load(T.QA[0:KROWS, e, :], 0, e, a_load[e])
                load(T.KA[0:KROWS, e, :], 1, e, a_load[e])
            iterations(sp, body)

        @block.gpsimd
        def _(pool):
            def gate():
                pool.sem_inc(settled, 1)

            def values(e, pair):
                if not (static(pair) and pair == 0):
                    pool.wait_ge(pv_done, pair * QT - QT + (e + 1) * (QT // 2))
                gate()
                pool.tensor_copy(T.V32[:, e, :, 0:D],
                                 T.V[:, bass.ds(2 * pair + e, 1), :, :].rearrange("p o t d -> p (o t) d")).then_inc(v_ready, 1)

            def query(i, k):
                if k == 0 and searches(i):
                    pool.wait_ge(gat_ready, i)
                    gate()
                e, r = k // PARTS, k % PARTS
                copy = pool.tensor_copy(
                    T.QG[:, e, :, r * PARTS * D:(r + 1) * PARTS * D].rearrange("p t (a d) -> p t a d", a=PARTS),
                    T.Qtok[:, bass.ds(2 * i + e, 1), :, :, :].rearrange("p o t a d -> p (o t) a d"))
                if k == 2 * PARTS - 1:
                    copy.then_inc(qg_ready, 1)

            def body(i):
                links = [0]

                def link(ins):
                    links[0] += 1
                    ins.then_inc(chain_p, 1)
                    pool.wait_ge(chain_p, (i - 1) * POOL_LINKS + links[0])
                if searches(i):
                    pool.wait_ge(a_counted, i * SLOTS)
                    gate()
                    pool.tensor_scalar(T.Fb[:, :], T.cnt[:, :], 0.0, None, ALU.is_ge).then_inc(flagged, 1)
                    pool.tensor_copy(T.st[:, :, 0], T.cnt[:, :])
                    pool.tensor_scalar(T.st[:, :, 2], T.cnt[:, :], 0.0, None, ALU.is_ge)
                    pool.wait_ge(m_taken, i)
                    gate()
                    pool.tensor_copy(T.st[:, :, 1], T.Mp[:, :]).then_inc(st_taken, 1)
                    pool.tensor_copy(T.Mq[:, :], T.Mp[:, :]).then_inc(m_kept, 1)
                    pool.wait_ge(gat_used, i)
                    gate()
                    link(pool.tensor_scalar(T.mp0[:, :], T.gs[:, 1:2], 0.0, None, ALU.max))
                    gate()
                    pool.tensor_scalar(T.sk[:, :], T.mp0[:, :], -SLACK, None, ALU.mult)
                    pool.tensor_scalar(T.nd[:, :], T.gs[:, 0:1], 1.0, 8.0, ALU.mult, ALU.add)
                    link(pool.tensor_scalar(T.sl[:, :], T.mp0[:, :], SLOPE, None, ALU.mult))
                    link(pool.tensor_tensor(T.dt[:, :], T.nd[:, :], T.sl[:, :], ALU.mult))
                    pool.tensor_tensor(T.tc[:, 0:1], T.dt[:, :], T.thrc[:, :], ALU.add).then_inc(step_t, 1)
                    for k in range(K0):
                        pool.wait_ge(step_c, (i - 1) * K0 + k + 1)
                        gate()
                        link(pool.tensor_scalar(T.nd[:, :], T.sg[:, k:k + 1], -1.0, 8.0, ALU.mult, ALU.add))
                        pool.tensor_tensor(T.ns[:, :], T.nd[:, :], T.sl[:, :], ALU.mult)
                        link(pool.tensor_tensor(T.dt[:, :], T.nd[:, :], T.nd[:, :], ALU.mult))
                        gate()
                        link(pool.tensor_scalar(T.dt[:, :], T.dt[:, :], 6.5 * 6.5, DAMP[k], ALU.is_gt, ALU.mult))
                        gate()
                        pool.tensor_scalar(T.tc[:, k + 1:k + 2], T.dt[:, :], T.ns[:, 0:1], T.tc[:, k:k + 1],
                                           ALU.mult, ALU.add).then_inc(step_t, 1)
                        if scores(i):
                            query(i, k)
                if b_tile(i, LAG):
                    values(1, i - 2)
                if searches(i):
                    pool.wait_ge(cnt_ready, i)
                    gate()
                    link(pool.tensor_scalar(T.ix[:, :], T.c1[:, :], -1.0, KEEP + 0.5, ALU.mult, ALU.add))
                    gate()
                    link(pool.tensor_scalar(T.z8[:, :], T.iota[:, 0:8], T.ix[:, 0:1], None, ALU.subtract))
                    pool.tensor_tensor(T.z8[:, :], T.z8[:, :], T.z8[:, :], ALU.mult).then_inc(z_ready, 1)
                    pool.tensor_scalar(T.bad[:, 2:3], T.bad[:, 1:2], CAP + 0.5, None, ALU.is_gt)
                    link(pool.tensor_scalar(T.nd[:, :], T.ix[:, :], -4.5, None, ALU.add))
                    link(pool.tensor_tensor(T.nd[:, :], T.nd[:, :], T.nd[:, :], ALU.mult))
                    gate()
                    link(pool.tensor_scalar(T.nd[:, :], T.nd[:, :], 9.5, None, ALU.is_gt))
                    link(pool.tensor_tensor(T.nd[:, :], T.nd[:, :], T.gs[:, 2:3], ALU.mult))
                    link(pool.tensor_tensor(T.badb[:, :], T.nd[:, :], T.bad[:, 2:3], ALU.add))
                    pool.wait_ge(kth_ready, i)
                    gate()
                    link(pool.tensor_scalar(T.kth[:, :], T.kth[:, :], 0.5, None, ALU.mult))
                    link(pool.tensor_tensor(T.kth[:, :], T.kth[:, :], T.sk[:, :], ALU.add))
                    gate()
                    link(pool.tensor_copy(T.t3[:, 0:1], T.kth[:, :]))
                    link(pool.tensor_tensor(T.dt[:, :], T.kth[:, :], T.t3[:, 0:1], ALU.subtract))
                    gate()
                    link(pool.tensor_copy(T.t3[:, 1:2], T.dt[:, :]))
                    link(pool.tensor_tensor(T.t3[:, 2:3], T.dt[:, :], T.t3[:, 1:2], ALU.subtract))
                    pool.tensor_tensor(T.tpm[:, :, :], T.t3[:, :].unsqueeze(1).broadcast_to([P, 2, PARTS]),
                                       T.half[:, :].unsqueeze(2).broadcast_to([P, 2, PARTS]), ALU.mult).then_inc(tp_ready, 1)
                    pool.wait_ge(t_final, i)
                    r = T.RP[:, :].rearrange("p (e k a t) -> p k a e t", e=2, k=2, a=PARTS)
                    xv = T.X[:, :, :].rearrange("p k (e t) -> p k e t", e=2)
                    gate()
                    pool.tensor_scalar(T.X[:, 0, :], T.Tt[:, :], -1.0, None, ALU.mult)
                    link(pool.tensor_tensor(T.X[:, 1, :], T.Tt[:, :], T.Mq[:, :], ALU.subtract))
                    gate()
                    link(pool.tensor_copy(r[:, :, 0], xv))
                    link(pool.tensor_tensor(xv, xv, r[:, :, 0], ALU.subtract))
                    gate()
                    link(pool.tensor_copy(r[:, :, 1], xv))
                    pool.tensor_tensor(r[:, :, 2], xv, r[:, :, 1], ALU.subtract).then_inc(rows_src, 1)
                    pool.wait_ge(rows_src, i)
                    assert links[0] == POOL_LINKS, links[0]
                    values(0, i - 1)
                if scores(i):
                    for k in range(K0 if searches(i) else 0, 2 * PARTS):
                        query(i, k)
            iterations(pool, body)

        @block.scalar
        def _(act):
            def copy_o(head):
                act.wait_ge(pv_done, (head + 1) * (QT // 2))
                if not (static(head) and head == 0):
                    act.wait_ge(ot_ready, head)
                act.activation(T.Osb[:, :], T.pO[:, :], ACT.Copy).then_inc(o_copied, 1)

            def body(i):
                for n in range(SLOTS):
                    ahead = b_tile(i, n + 1)
                    if ahead:
                        g, e, t = ahead
                        act.wait_ge(w_ready, g + 1)
                        if not (static(i) and g < 4):
                            act.wait_ge(pv_done, (i - 2) * QT + (n + 1 - LAG - 4) // 2 + 1)
                        act.activation(T.E[:, (n + 1) % 4, :], T.pW[:, :], ACT.Exp).then_inc(e_ready, 1)
                    if scores(i) if n else searches(i):
                        m = (n - 1) % SLOTS
                        act.wait_ge(a_copied, i * SLOTS + n)
                        if n == 1 and searches(i):
                            act.wait_ge(st_taken, i)
                        act.activation(T.junk_a[:, m % 4, :], T.Sc[:, m % 4, :], ACT.Sign, bias=T.negthr[:, 0:1],
                                       accum_out=T.cnt[:, m:m + 1]).then_inc(a_counted, 1)
                    bt = b_tile(i, n)
                    if bt and bt[2] == 1 and not (static(i) and bt[0] < QT):
                        copy_o(head_before(i, n))
                    if not searches(i):
                        continue
                    if n in (3, 4):
                        act.wait_ge(ss_ready, 2 * (i - 1) + n - 2)
                        if n == 3 and not (static(i) and i == 1):
                            act.wait_ge(t_final, i - 1)
                        act.activation(T.Ss[:, (n - 3) * 512:(n - 2) * 512], T.pM[:, :], ACT.Copy).then_inc(ss_copied, 1)
                    if 5 <= n < 5 + K0:
                        k = n - 5
                        if k == 0:
                            act.wait_ge(ss_copied, 2 * i)
                        act.wait_ge(step_t, (i - 1) * (K0 + 1) + k + 1)
                        act.activation(T.junk_a2[:, :], T.Ss[:, :], ACT.Sign, bias=T.tc[:, k:k + 1], scale=-1.0,
                                       accum_out=T.sg[:, k:k + 1]).then_inc(step_c, 1)
                    if n == 11:
                        act.wait_ge(selT_ready, i)
                        act.activation(T.SelT[:, :], T.pM_b[:, :], ACT.Copy).then_inc(selT_copied, 1)
            iterations(act, body)
            copy_o(HEADS - 1)

        @block.vector
        def _(dve):
            def done(ins, s, value):
                ins.then_inc(s, 1)
                dve.wait_ge(s, value)

            def finish_o(head):
                dve.wait_ge(ot_ready, head + 1)
                o = T.pM[:, 0:QT * (D + 1)].rearrange("p (t c d) -> p c t d", c=2, d=D + 1)
                rl = T.rl[:, :].rearrange("p (c t) -> p c t", c=2)
                if not (static(head) and head == 0):
                    dve.wait_ge(o_done, head)
                done(dve.reciprocal(rl, o[:, :, :, D]), o_chain, head + 1)
                dve.tensor_tensor(T.attn[:, bass.ds(head, 1), :, :].rearrange("p o (c t) d -> p (o c) t d", c=2), o[:, :, :, 0:D],
                                  rl.unsqueeze(3).broadcast_to([P, 2, QT // 2, D]), ALU.mult).then_inc(o_done, 1)

            def exhaustive(i):
                m = [0]

                def flink(ins):
                    m[0] += 1
                    done(ins, fb_chain, (i - 1) * FBN + m[0])
                for n in range(SLOTS):
                    for hf in range(2):
                        dve.wait_ge(fb_ready, (i - 1) * 2 * SLOTS + 2 * n + hf + 1)
                        dve.tensor_copy(T.Ss[:, hf * 512:(hf + 1) * 512], T.pM[:, :]).then_inc(fb_copied, 1)
                    dve.wait_ge(fb_copied, (i - 1) * 2 * SLOTS + 2 * n + 2)
                    flink(dve.tensor_copy(T.lo[:, :], T.thrc[:, :]))
                    flink(dve.tensor_scalar(T.stp[:, :], T.Mp[:, n:n + 1], 0.0, 1.0, ALU.max, ALU.add))
                    dve.sem_inc(settled, 1)
                    with dve.Fori(0, BISECT) as r:
                        base = (i - 1) * FBN + n * (6 + 5 * BISECT) + 2 + 5 * r
                        done(dve.tensor_tensor(T.mid[:, :], T.lo[:, :], T.stp[:, :], ALU.add), fb_chain, base + 1)
                        done(dve.tensor_scalar(T.Wm[:, :], T.Ss[:, :], T.mid[:, 0:1], None, ALU.is_ge, ALU.add,
                                               accum_out=T.cf[:, :]), fb_chain, base + 2)
                        done(dve.scalar_tensor_tensor(T.mid[:, :], T.cf[:, :], KEEP - 0.5, T.stp[:, :], ALU.is_ge, ALU.mult),
                             fb_chain, base + 3)
                        done(dve.tensor_tensor(T.lo[:, :], T.lo[:, :], T.mid[:, :], ALU.add), fb_chain, base + 4)
                        done(dve.tensor_scalar(T.stp[:, :], T.stp[:, :], 0.5, None, ALU.mult), fb_chain, base + 5)
                        dve.sem_inc(settled, 1)
                    m[0] += 5 * BISECT
                    flink(dve.tensor_scalar(T.mid[:, :], T.Mp[:, n:n + 1], 0.0, -SLACK, ALU.max, ALU.mult))
                    flink(dve.tensor_tensor(T.lo[:, :], T.lo[:, :], T.mid[:, :], ALU.add))
                    flink(dve.tensor_tensor(T.Tt[:, n:n + 1], T.lo[:, :], T.thrc[:, :], ALU.max))
                    flink(dve.tensor_copy(T.cf[:, :], T.lo[:, :]))
                dve.sem_inc(settled, 1)
                assert m[0] == FBN, (m[0], FBN)

            def search(i, n, place):
                at = (n, place)
                if at == (0, 0):
                    dve.wait_ge(a_copied, i * SLOTS)
                    if not (static(i) and i == 1):
                        dve.wait_ge(m_kept, i - 1)
                    done(dve.tensor_copy(T.Mp[:, :], T.M[:, :]), m_taken, i)
                if at == (1, 1):
                    dve.wait_ge(pos_ready, i)
                    if not (static(i) and i == 1):
                        dve.wait_ge(tp_ready, i - 1)
                    dve.tensor_tensor(T.posF[:, :], T.pM[:, 0:SLOTS], T.Fb[:, :], ALU.mult).then_inc(pos_used, 1)
                if at == (1, 2):
                    dve.wait_ge(pos_used, i)
                    dve.tensor_tensor(T.Sel[:, :, :, :].rearrange("p t e c -> p e t c"),
                                      T.iota[:, 0:CAP].unsqueeze(1).unsqueeze(1).broadcast_to([P, 2, QT, CAP]),
                                      T.posF[:, :].rearrange("p (e t) -> p e t", e=2).unsqueeze(3).broadcast_to([P, 2, QT, CAP]),
                                      ALU.is_equal).then_inc(sel_ready, 1)
                    dve.tensor_reduce(T.bad[:, 1:2], T.posF[:, :], AX.X, ALU.max)
                if at == (2, 2):
                    dve.wait_ge(gat_ready, i)
                    dve.tensor_copy(T.Qc[:, :], T.pM[0:KROWS, 0:P])
                    dve.tensor_copy(T.gs[:, :], T.pM[:, P:P + 3]).then_inc(gat_used, 1)
                t = T.tc[:, K0:K0 + 1]
                if at == (10, 2):
                    dve.wait_ge(step_t, i * (K0 + 1))
                    dve.tensor_scalar(T.junk_d[:, :], T.Ss[:, :], t, None, ALU.is_ge, ALU.add, accum_out=T.c1[:, :]).then_inc(cnt_ready, 1)
                if at == (11, 1):
                    done(dve.scalar_tensor_tensor(T.Wm[:, :], T.Ss[:, :], t, T.Ss[:, :], ALU.is_lt, ALU.mult), chain, i)
                if at == (11, 2):
                    dve.max(T.W8[:, :], T.Wm[:, :]).then_inc(w8_ready, 1)
                if at == (12, 1):
                    dve.wait_ge(z_ready, i)
                    dve.wait_ge(w8_ready, i)
                    dve.scalar_tensor_tensor(T.h8[:, :], T.z8[:, :], 0.5, T.W8[:, :], ALU.is_lt, ALU.mult,
                                             accum_out=T.kth[:, :]).then_inc(kth_ready, 1)
                if at == (14, 0):
                    dve.wait_ge(sc_ready, i)
                    dve.tensor_copy(T.flag[0:1, 0:1], T.pM[0:1, 64:65])
                    done(dve.tensor_reduce(T.Tt[:, :].rearrange("p (e t) -> p t e", e=2),
                                           T.pM[:, 0:48].rearrange("p (t e a) -> p t e a", e=2, a=PARTS), AX.X, ALU.add),
                         flag_ready, i)
                if at == (14, 1):
                    dve.tensor_scalar(T.Tt[:, :], T.Tt[:, :], T.thrc[:, 0:1], None, ALU.max).then_inc(t_ready, 1)
                if at == (15, 2):
                    dve.wait_ge(t_ready, i)
                    dve.sem_inc(settled, 1)
                    flag = dve.value_load(T.flag[0:1, 0:1], min_val=0, max_val=P * 2)
                    with dve.If(flag > 0):
                        exhaustive(i)
                    with dve.Else():
                        dve.sem_inc(fb_copied, 2 * SLOTS)
                        dve.sem_inc(fb_chain, FBN)
                    dve.sem_inc(t_final, 1)

            def take_rows(i):
                dve.wait_ge(rowsT_ready, i)
                if not (static(i) and i == 1):
                    for e in range(2):
                        dve.wait_ge(aux_load[e], (i - 1) * 16)
                dve.tensor_copy(T.rowsT[:, :], T.pM_b[0:96, 0:P]).then_inc(rows_copied, 1)

            def body(i):
                for n in range(SLOTS):
                    if searches(i):
                        search(i, n, 0)
                    if scores(i):
                        g = i * SLOTS + n
                        dve.wait_ge(a_ready, g + 1)
                        if not (static(i) and g < 4):
                            dve.wait_ge(a_counted, g - 3)
                        dve.tensor_scalar(T.Sc[:, n % 4, :], T.pA[:, :], 1.0, None, ALU.mult, ALU.max,
                                          accum_out=T.M[:, n:n + 1]).then_inc(a_copied, 1)
                    bt = b_tile(i, n)
                    if bt and bt[2] == 3 and not (static(i) and bt[0] < QT):
                        finish_o(head_before(i, n))
                    if searches(i):
                        search(i, n, 1)
                    if bt:
                        g, e, t = bt
                        dve.wait_ge(e_ready, g + 1)
                        dve.wait_ge(u_ready, g + 1)
                        dve.scalar_tensor_tensor(T.E[:, n % 4, :], T.pU[:, :], 0.0, T.E[:, n % 4, :],
                                                 ALU.is_ge, ALU.mult).then_inc(p_ready, 1)
                    if n == 0 and searches(i - 1):
                        take_rows(i - 1)
                    if searches(i):
                        search(i, n, 2)
            iterations(dve, body)
            finish_o(HEADS - 1)

        @block.tensor
        def _(pe):
            def products(i, n):
                m = (n - LAG) // 2 - 1
                k, e = m % (QT // 2), (m // (QT // 2)) % 2
                pe.wait_ge(p_ready, (i - 2) * SLOTS + n - LAG)
                if k == 0:
                    head = 2 * (i - 2) + m // (QT // 2)
                    pe.wait_ge(v_ready, head + 1)
                    if not (static(i) and head == 0):
                        pe.wait_ge(o_copied, head)
                for par in range(2):
                    for c in range(2):
                        g = 32 * (2 * par + c)
                        last = nc.tensor.matmul(T.pO[g:g + VW, :], T.V32[:, e, 2 * k + par, :],
                                                T.E[:, (n - 2 + par) % 4, c * 512:(c + 1) * 512],
                                                start=(k == 0), stop=(k == QT // 2 - 1))
                last.then_inc(pv_done, 1)

            def gather_o(head):
                pe.wait_ge(o_copied, head + 1)
                if not (static(head) and head == 0):
                    pe.wait_ge(o_done, head)
                for t in range(QT // 2):
                    o = t * 2 * (D + 1)
                    last = nc.tensor.matmul(T.pM[:, o:o + 2 * (D + 1)], T.Osb[:, t * P:(t + 1) * P],
                                            T.osel[:, :, :].rearrange("p c d -> p (c d)"), start=True, stop=True)
                last.then_inc(ot_ready, 1)

            def search(i, n):
                if n == 1:
                    pe.wait_ge(flagged, i)
                    if not (static(i) and i == 1):
                        pe.wait_ge(rows_copied, i - 1)
                    F = T.Fb[:, :].rearrange("p (e t) -> p e t", e=2)
                    pos = T.pM[:, 0:SLOTS].rearrange("p (e t) -> p e t", e=2)
                    nc.tensor.matmul(pos, T.zeros_b[:, :], F, start=True, stop=False)
                    for s in range(1, QT):
                        nc.tensor.matmul(pos[:, :, s:QT], T.ones_b[:, :], F[:, :, 0:QT - s], start=False, stop=False)
                    nc.tensor.matmul(pos, T.tri[:, :], F, start=False, stop=True).then_inc(pos_ready, 1)
                if n == 2:
                    pe.wait_ge(sel_ready, i)
                    pe.wait_ge(st_taken, i)
                    pe.wait_ge(qg_ready, i)
                    for e in range(2):
                        for t in range(QT):
                            nc.tensor.matmul(T.pM[0:KROWS, e * CAP:(e + 1) * CAP], T.QG[:, e, t, :], T.Sel[:, t, e, :],
                                             start=(t == 0), stop=(t == QT - 1))
                    for e in range(2):
                        for t in range(QT):
                            last = nc.tensor.matmul(T.pM[e * CAP:(e + 1) * CAP, P:P + 3], T.Sel[:, t, e, :],
                                                    T.st[:, e * QT + t, :], start=(t == 0), stop=(t == QT - 1))
                    last.then_inc(gat_ready, 1)
                if n in (3, 4):
                    if n == 3:
                        pe.wait_ge(gat_used, i)
                        pe.wait_ge(s_load, i * 64)
                    else:
                        pe.wait_ge(ss_copied, 2 * (i - 1) + 1)
                    for e in range(2):
                        last = nc.tensor.matmul(T.pM[e * CAP:(e + 1) * CAP, :], T.Qc[0:KROWS, e * CAP:(e + 1) * CAP],
                                                T.KS[0:KROWS, e, (n - 3) * 512:(n - 2) * 512], start=True, stop=True)
                    last.then_inc(ss_ready, 1)
                if n == 8:
                    pe.wait_ge(ss_copied, 2 * i)
                    if b_tile(i, 6) and not (static(i) and i == 2):
                        pe.wait_ge(o_done, 2 * (i - 2))
                    for t in range(QT):
                        last = nc.tensor.transpose(T.pM_b[:, t * P:(t + 1) * P], T.Sel[:, t, :, :].rearrange("p e c -> p (e c)"),
                                                   T.ident_b[:, :])
                    last.then_inc(selT_ready, 1)
                if n == 13:
                    pe.wait_ge(tp_ready, i)
                    pe.wait_ge(selT_copied, i)
                    for t in range(QT):
                        nc.tensor.matmul(T.pM[:, t * 6:(t + 1) * 6], T.SelT[:, t * P:(t + 1) * P],
                                         T.tpm[:, :, :].rearrange("p e a -> p (e a)"), start=True, stop=True)
                    nc.tensor.matmul(T.pM[0:1, 64:65], T.badb[:, 0:1], T.ones_b[:, 0:1], start=True, stop=True).then_inc(sc_ready, 1)
                if n == 15:
                    pe.wait_ge(t_ready, i)
                    pe.sem_inc(settled, 1)
                    flag = pe.value_load(T.flag[0:1, 0:1], min_val=0, max_val=P * 2)
                    with pe.If(flag > 0):
                        if b_tile(i, 14):
                            pe.wait_ge(o_done, 2 * (i - 2) + 1)
                            pe.sem_inc(settled, 1)
                        for m in range(SLOTS):
                            for hf in range(2):
                                if m + hf:
                                    pe.wait_ge(fb_copied, (i - 1) * 2 * SLOTS + 2 * m + hf)
                                nc.tensor.matmul(T.pM[:, :], T.QS[0:KROWS, m // QT, (m % QT) * P:(m % QT + 1) * P],
                                                 T.KS[0:KROWS, m // QT, hf * 512:(hf + 1) * 512], start=True, stop=True).then_inc(fb_ready, 1)
                    with pe.Else():
                        pe.sem_inc(fb_ready, 2 * SLOTS)

            def transpose_rows(i):
                if b_tile(i, 14):
                    pe.wait_ge(o_done, 2 * (i - 2) + 1)
                pe.wait_ge(fb_copied, i * 2 * SLOTS)
                pe.wait_ge(rows_src, i)
                nc.tensor.transpose(T.pM_b[0:96, 0:P], T.RP[:, :], T.ident_b[:, :]).then_inc(rowsT_ready, 1)

            def body(i):
                for n in range(SLOTS):
                    if scores(i):
                        ga = i * SLOTS + n
                        ea, ta = n // QT, n % QT
                        if ta == 0:
                            pe.wait_ge(a_load[ea], (i + 1) * 32)
                        if not (static(i) and ga == 0):
                            pe.wait_ge(a_copied, ga)
                        for c in range(2):
                            last = nc.tensor.matmul(T.pA[:, c * 512:(c + 1) * 512], T.QA[0:KROWS, ea, ta * P:(ta + 1) * P],
                                                    T.KA[0:KROWS, ea, c * 512:(c + 1) * 512], start=True, stop=True)
                        last.then_inc(a_ready, 1)
                    ahead = b_tile(i, n + 1)
                    if ahead:
                        gb, e, t = ahead
                        if t == 0:
                            pe.wait_ge(b_load[e], (i - 1) * 32)
                            pe.wait_ge(aux_load[e], (i - 1) * 16)
                        if not (static(i) and gb == 0):
                            pe.wait_ge(e_ready, gb)
                        for c in range(2):
                            last = nc.tensor.matmul(T.pW[:, c * 512:(c + 1) * 512], T.KB[0:WROWS, e, t * P:(t + 1) * P],
                                                    T.QB[0:WROWS, e, c * 512:(c + 1) * 512], start=True, stop=True)
                        last.then_inc(w_ready, 1)
                    bt = b_tile(i, n)
                    if bt:
                        gb, e, t = bt
                        first = static(i) and gb == 0
                        if not first:
                            pe.wait_ge(p_ready, gb)
                        for c in range(2):
                            last = nc.tensor.matmul(T.pU[:, c * 512:(c + 1) * 512], T.KB[0:UROWS, e, t * P:(t + 1) * P],
                                                    T.QB[0:UROWS, e, c * 512:(c + 1) * 512], start=True, stop=True)
                        last.then_inc(u_ready, 1)
                        if n % 2 == 0 and not first:
                            products(i, n)
                        if t == 2 and not (static(i) and gb < QT):
                            if searches(i):
                                pe.wait_ge(ss_copied if n == 6 else flag_ready, 2 * i if n == 6 else i)
                            elif n == 6:
                                pe.wait_ge(rows_copied, PAIRS)
                            gather_o(head_before(i, n))
                    if n == 0 and searches(i - 1):
                        transpose_rows(i - 1)
                    if searches(i):
                        search(i, n)
            iterations(pe, body)
            products(last_i, LAG)
            gather_o(HEADS - 1)


def feed_forward(nc, T, out):
    sem = T.sem
    at_ready = sem("ff_attn"); att_ready = sem("ff_attnT_ready"); att_copied = sem("ff_attnT")
    pr_ready = sem("ff_proj"); x1_ready = sem("ff_x1"); var_ready = sem("ff_var"); std_ready = sem("ff_std")
    xhat_ready = sem("ff_xhat"); xt_ready = sem("ff_xt"); ht_ready = sem("ff_ht")
    lg_ready = sem("ff_logits"); oh_ready = sem("ff_onehot"); ohT_ready = sem("ff_ohT"); ohT_done = sem("ff_ohT_done")
    ohb_ready = sem("ff_ohb_ready"); mask_done = sem("ff_mask_done")
    xe_ready = sem("ff_xe"); xe_used = sem("ff_xe_used"); gu_ready = sem("ff_gu"); silu_done = sem("ff_silu")
    h_ready = sem("ff_h"); hm_ready = sem("ff_hm"); y_ready = sem("ff_y"); y_done = sem("ff_y_done")
    out_done = sem("ff_out"); chain = sem("ff_chain")
    NCH = B * S // CHUNK
    LN = FF_LINKS

    def loop(eng, body):
        body(0)
        with eng.Fori(1, NCH) as c:
            body(c)

    with nc.Block() as block:
        @block.sync
        def _(sp):
            def body(c):
                sp.wait_ge(y_done, c + 1)
                sp.dma_start(out[bass.ds(c * CHUNK, CHUNK), :].rearrange("(t p) c -> p t c", p=P), T.x2[:, :, :]).then_inc(out_done, 16)
            loop(sp, body)
            sp.wait_ge(out_done, NCH * 16)

        @block.gpsimd
        def _(pool):
            for c in range(NCH):
                b, t0 = c // 2, (c % 2) * CT
                if c:
                    pool.wait_ge(att_ready, c)
                for t in range(CT):
                    last = pool.tensor_copy(T.ast[:, t, :].rearrange("p (h d) -> p h d", d=D),
                                            T.attn[:, b * H:(b + 1) * H, t0 + t, :])
                last.then_inc(at_ready, 1)

        @block.scalar
        def _(act):
            for c in range(NCH):
                act.wait_ge(att_ready, c + 1)
                if c:
                    act.wait_ge(pr_ready, c)
                act.activation(T.attT[:, :], T.pO[:, :], ACT.Copy).then_inc(att_copied, 1)
                act.wait_ge(var_ready, c + 1)
                act.activation(T.std[:, :], T.mv[:, :, 1], ACT.Sqrt, bias=T.epsc[:, 0:1]).then_inc(std_ready, 1)
                act.wait_ge(ohT_ready, c + 1)
                if c:
                    act.wait_ge(ohb_ready, c * E)
                act.activation(T.ohT[:, :], T.pM[0:E, :], ACT.Copy).then_inc(ohT_done, 1)
                for e in range(E):
                    act.wait_ge(ohb_ready, c * E + e + 1)
                    if c and e == 0:
                        act.wait_ge(hm_ready, c)
                    act.activation(T.mask[:, e, :], (T.pM if e % 2 else T.pO)[:, :], ACT.Copy).then_inc(mask_done, 1)
                for k in range(2):
                    act.wait_ge(gu_ready, 2 * c + k + 1)
                    if c and k == 0:
                        act.wait_ge(h_ready, 2 * c)
                    act.activation(T.sg2[:, k, :], T.pA[:, :], ACT.Silu).then_inc(silu_done, 1)

        @block.vector
        def _(dve):
            def done(ins, s, value):
                ins.then_inc(s, 1)
                dve.wait_ge(s, value)

            for c in range(NCH):
                b = c // 2
                n = [c * LN]

                def link(ins):
                    n[0] += 1
                    ins.then_inc(chain, 1)
                    dve.wait_ge(chain, n[0])
                dve.wait_ge(pr_ready, c + 1)
                pr = T.pM[:, :].rearrange("p (t c) -> p t c", c=C)
                if c:
                    dve.wait_ge(y_done, c)
                link(dve.tensor_tensor(T.x1[:, :, :], pr, T.gates[:, b * C:(b + 1) * C].unsqueeze(1).broadcast_to([P, CT, C]), ALU.mult))
                done(dve.tensor_tensor(T.x1[:, :, :], T.x1[:, :, :], T.x[:, c * CT:(c + 1) * CT, :], ALU.add), x1_ready, c + 1)
                for t in range(CT):
                    link(dve.bn_stats(T.bn[:, t, :], T.x1[:, t, :]))
                for t in range(CT):
                    last = dve.bn_aggr(T.mv[:, t, :], T.bn[:, t, :])
                link(last)
                done(dve.tensor_scalar(T.veps[:, :], T.mv[:, :, 1], EPS, None, ALU.add), var_ready, c + 1)
                dve.wait_ge(std_ready, c + 1)
                link(dve.reciprocal(T.rs[:, :], T.std[:, :]))
                link(dve.tensor_tensor(T.rs[:, :], T.rs[:, :], T.veps[:, :], ALU.mult))
                link(dve.tensor_tensor(T.rs[:, :], T.rs[:, :], T.std[:, :], ALU.add))
                link(dve.tensor_scalar(T.rs[:, :], T.rs[:, :], 0.5, None, ALU.mult))
                link(dve.reciprocal(T.rs[:, :], T.rs[:, :]))
                for t in range(CT):
                    last = dve.tensor_scalar(T.xhat[:, t, :], T.x1[:, t, :], T.mv[:, t, 0:1], T.rs[:, t:t + 1], ALU.subtract, ALU.mult)
                last.then_inc(xhat_ready, 1)
                dve.wait_ge(xt_ready, c + 1)
                dve.tensor_scalar(T.hT[:, :], T.pO[:, :], T.mod[:, 4 * B + b:4 * B + b + 1], T.mod[:, 3 * B + b:3 * B + b + 1],
                                       ALU.mult, ALU.add).then_inc(ht_ready, 1)
                dve.wait_ge(lg_ready, c + 1)
                lg = T.pM[:, 0:CT * E].rearrange("p (t e) -> p t e", e=E)
                link(dve.tensor_copy(T.lg[:, :, :], lg))
                link(dve.tensor_reduce(T.mx[:, :], T.lg[:, :, :], AX.X, ALU.max))
                link(dve.tensor_tensor(T.lg[:, :, :], T.lg[:, :, :], T.mx[:, :].unsqueeze(2).broadcast_to([P, CT, E]), ALU.is_ge))
                link(dve.tensor_tensor(T.lg[:, :, :], T.lg[:, :, :], T.down_count[:, :].unsqueeze(1).broadcast_to([P, CT, E]), ALU.mult))
                link(dve.tensor_reduce(T.mx[:, :], T.lg[:, :, :], AX.X, ALU.max))
                dve.tensor_tensor(T.oh[:, :, :], T.lg[:, :, :], T.mx[:, :].unsqueeze(2).broadcast_to([P, CT, E]), ALU.is_equal).then_inc(oh_ready, 1)
                for e in range(E):
                    dve.wait_ge(mask_done, c * E + e + 1)
                    if e >= 2:
                        dve.wait_ge(xe_used, c * (E - 1) + e - 1)
                    elif c:
                        dve.wait_ge(xe_used, c * (E - 1))
                    dve.tensor_tensor(T.xe[:, e % 2, :], T.hT[:, :], T.mask[:, e, :], ALU.mult).then_inc(xe_ready, 1)
                for k in range(2):
                    dve.wait_ge(silu_done, 2 * c + k + 1)
                    done(dve.tensor_tensor(T.h[:, k, :], T.sg2[:, k, :], T.pU[:, :], ALU.mult), h_ready, 2 * c + k + 1)
                    if k == 0:
                        if c:
                            dve.wait_ge(y_ready, c)
                        for e in range(E):
                            last = dve.tensor_tensor(T.hm[:, e, :, :], T.h[:, 0, :].rearrange("p (f n) -> p f n", f=FB),
                                                     T.mask[:, e, :].unsqueeze(1).broadcast_to([P, FB, CHUNK]), ALU.mult)
                        last.then_inc(hm_ready, 1)
                dve.wait_ge(y_ready, c + 1)
                y = T.pW[:, 0:512].rearrange("p (t c) -> p t c", c=C)
                if c:
                    dve.wait_ge(out_done, 16 * c)
                link(dve.tensor_tensor(T.x2[:, :, :], y, T.gates[:, (B + b) * C:(B + b + 1) * C].unsqueeze(1).broadcast_to([P, CT, C]), ALU.mult))
                dve.tensor_tensor(T.x2[:, :, :], T.x2[:, :, :], T.x1[:, :, :], ALU.add).then_inc(y_done, 1)
                assert n[0] == (c + 1) * LN, n[0]

        @block.tensor
        def _(pe):
            wT = T.wT[:, 4 * C:].rearrange("p (k e f n) -> p k e f n", k=3, e=E + 1, f=FB)
            woT = T.wT[:, 3 * C:4 * C]
            for c in range(NCH):
                pe.wait_ge(at_ready, c + 1)
                for t in range(CT):
                    last = nc.tensor.transpose(T.pO[:, t * P:(t + 1) * P], T.ast[:, t, :], T.ident[:, :])
                last.then_inc(att_ready, 1)
                pe.wait_ge(att_copied, c + 1)
                for t in range(CT):
                    nc.tensor.matmul(T.pM[:, t * C:(t + 1) * C], T.attT[:, t * P:(t + 1) * P], woT, start=True, stop=False)
                    last = nc.tensor.matmul(T.pM[:, t * C:(t + 1) * C], T.ones_f[0:1, :], T.borow[0:1, :], start=False, stop=True)
                last.then_inc(pr_ready, 1)
                pe.wait_ge(xhat_ready, c + 1)
                for t in range(CT):
                    last = nc.tensor.transpose(T.pO[:, t * P:(t + 1) * P], T.xhat[:, t, :], T.ident[:, :])
                last.then_inc(xt_ready, 1)
                pe.wait_ge(ht_ready, c + 1)
                for t in range(CT):
                    last = nc.tensor.matmul(T.pM[:, t * E:(t + 1) * E], T.hT[:, t * P:(t + 1) * P], T.rT[:, :], start=True, stop=True)
                last.then_inc(lg_ready, 1)
                pe.wait_ge(oh_ready, c + 1)
                for t in range(CT):
                    last = nc.tensor.transpose(T.pM[0:E, t * P:(t + 1) * P], T.oh[:, t, :], T.ident[:, :])
                last.then_inc(ohT_ready, 1)
                pe.wait_ge(ohT_done, c + 1)

                def spread(e):
                    if e >= 2:
                        pe.wait_ge(mask_done, c * E + e - 1)
                    nc.tensor.matmul((T.pM if e % 2 else T.pO)[:, :], T.ident_b[0:E, e:e + 1].broadcast_to([E, P]), T.ohT[:, :],
                                     start=True, stop=True).then_inc(ohb_ready, 1)
                spread(0)
                spread(1)
                for e in range(E):
                    if e + 2 < E:
                        spread(e + 2)
                    pe.wait_ge(xe_ready, c * E + e + 1)
                    for k, ps in ((0, T.pA), (1, T.pU)):
                        for f in range(FB):
                            last = nc.tensor.matmul(ps[:, f * 512:(f + 1) * 512], wT[:, k, e, f, :], T.xe[:, e % 2, :],
                                                    start=(e == 0), stop=(e == E - 1))
                    last.then_inc(xe_used if e < E - 1 else gu_ready, 1)
                pe.wait_ge(h_ready, 2 * c + 1)
                for k, ps in ((0, T.pA), (1, T.pU)):
                    for f in range(FB):
                        last = nc.tensor.matmul(ps[:, f * 512:(f + 1) * 512], wT[:, k, E, f, :], T.hT[:, :], start=True, stop=True)
                last.then_inc(gu_ready, 1)
                pe.wait_ge(hm_ready, c + 1)
                pe.wait_ge(h_ready, 2 * c + 2)
                for t in range(CT):
                    for e in range(E + 1):
                        for f in range(FB):
                            lhs = T.hm[:, e, f, t * P:(t + 1) * P] if e < E else T.h[:, 1, f * 512 + t * P:f * 512 + (t + 1) * P]
                            last = nc.tensor.matmul(T.pW[:, t * C:(t + 1) * C], lhs, wT[:, 2, e, f, :],
                                                    start=(e == 0 and f == 0), stop=(e == E and f == FB - 1))
                last.then_inc(y_ready, 1)



class Places:

    def __init__(self, nc, ctx):
        def sb(name, shape, dt):
            return ctx.enter_context(nc.sbuf_tensor(name, shape, dt))

        self.ident = sb("ident", [P, P], F32)
        self.ident_b = sb("ident_b", [P, P], BF16)
        self.tri = sb("tri", [P, P], BF16)
        self.ones_b = sb("ones_b", [P, P], BF16)
        self.zeros_b = sb("zeros_b", [P, P], BF16)
        self.ones_f = sb("ones_f", [P, P], F32)
        self.iota_i = sb("iota_i", [P, P], I32)
        self.iota = sb("iota", [P, P], F32)
        self.down_count = sb("down_count", [P, E], F32)
        self.epsc = sb("epsc", [P, 1], F32)
        self.half = sb("half", [P, 2], F32)
        self.osel = sb("osel", [P, 2, D + 1], F32)
        self.thr0 = sb("thr0", [P, 1], F32)
        self.thrc = sb("thrc", [P, 1], F32)
        self.negthr = sb("negthr", [P, 1], F32)
        self.mod = sb("mod", [P, 6 * B], F32)
        self.gates = sb("gates", [P, 2 * B * C], F32)
        self.wT = sb("wT", [P, NWT * C], F32)
        self.rT = sb("rT", [P, E], F32)
        self.x = sb("x", [P, B * QT, C], F32)
        self.V = sb("V", [P, HEADS, QT, D], F32)
        self.Qtok = sb("Qtok", [P, HEADS, QT, PARTS, D], BF16)
        self.attn = sb("attn", [P, HEADS, QT, D], F32)
        self.QB = sb("QB", [P, 2, S], BF16)
        self.KB = sb("KB", [P, 2, S], BF16)
        self.V32 = sb("V32", [P, 2, QT, VW], F32)
        self.tpm = sb("tpm", [P, 2, PARTS], BF16)
        self.bn = sb("bn", [P, CT, 6], F32)
        self.mv = sb("mv", [P, CT, 2], F32)
        self.veps = sb("veps", [P, CT], F32)
        self.std = sb("std", [P, CT], F32)
        self.rs = sb("rs", [P, CT], F32)
        self.xhat = sb("xhat", [P, CT, C], F32)
        self.hT = sb("hT", [P, CHUNK], F32)
        self.borow = sb("borow", [1, C], F32)
        ps = ctx.enter_context(nc.psum_tensor("ps", [P, 4096], F32))
        self.pA, self.pU, self.pW = ps[:, 0:1024], ps[:, 1024:2048], ps[:, 2048:3072]
        self.pO, self.pM = ps[:, 3072:3584], ps[:, 3584:4096]
        self.pUW_b, self.pM_b = ps[:, 1024:3072].bitcast(BF16), ps[:, 3584:4096].bitcast(BF16)
        self.sem = lambda name: ctx.enter_context(nc.semaphore(name))


def place_prepare(T, nc, ctx):
    def sb(name, shape, dt):
        return ctx.enter_context(nc.sbuf_tensor(name, shape, dt))

    T.nat = sb("nat", [P, NWT, C], F32)
    T.cT = sb("cT", [P, B], F32)
    T.sc = sb("sc", [P, B], F32)
    T.wmod = sb("wmod", [P, 6 * C], F32)
    T.gabs = sb("gabs", [P, 2 * B * C], F32)
    T.qkp = sb("qkp", [P, CT, PARTS, 2 * C], BF16)
    T.rem = sb("rem", [P, 2 * C], F32)
    T.qkT = sb("qkT", [P, 2 * PARTS, CHUNK], BF16)
    T.rt_nat = sb("rt_nat", [E, C], F32)


def place_attention(T, nc, ctx):
    def sb(name, shape, dt):
        return ctx.enter_context(nc.sbuf_tensor(name, shape, dt))

    T.QA = sb("QA", [P, 2, S], BF16)
    T.KA = sb("KA", [P, 2, S], BF16)
    T.QS = sb("QS", [P, 2, S], BF16)
    T.KS = sb("KS", [P, 2, S], BF16)
    T.E = sb("E", [P, 4, S], F32)
    T.Sc = sb("Sc", [P, 4, S], F32)
    T.Ss = sb("Ss", [P, S], F32)
    T.Wm = sb("Wm", [P, S], F32)
    T.junk_a = sb("junk_a", [P, 4, S], BF16)
    T.junk_a2 = sb("junk_a2", [P, S], BF16)
    T.M = sb("M", [P, SLOTS], F32)
    T.Mp = sb("Mp", [P, SLOTS], F32)
    T.cnt = sb("cnt", [P, SLOTS], F32)
    T.Fb = sb("Fb", [P, SLOTS], BF16)
    T.st = sb("st", [P, SLOTS, 3], BF16)
    T.posF = sb("posF", [P, SLOTS], F32)
    T.Sel = sb("Sel", [P, QT, 2, CAP], BF16)
    T.SelT = sb("SelT", [P, S], BF16)
    T.QG = sb("QG", [P, 2, QT, KROWS], BF16)
    T.gs = sb("gs", [P, 3], F32)
    T.sl = sb("sl", [P, 1], F32)
    T.dt = sb("dt", [P, 1], F32)
    T.nd = sb("nd", [P, 1], F32)
    T.ns = sb("ns", [P, 1], F32)
    T.Mq = sb("Mq", [P, SLOTS], F32)
    T.tc = sb("tc", [P, len(DAMP) + 1], F32)
    T.sg = sb("sg", [P, len(DAMP)], F32)
    T.c1 = sb("c1", [P, 1], F32)
    T.W8 = sb("W8", [P, 8], F32)
    T.h8 = sb("h8", [P, 8], F32)
    T.ix = sb("ix", [P, 1], F32)
    T.kth = sb("kth", [P, 1], F32)
    T.t3 = sb("t3", [P, PARTS], BF16)
    T.bad = sb("bad", [P, 3], F32)
    T.badb = sb("badb", [P, 1], BF16)
    T.flag = sb("flag", [P, 1], I32)
    T.Tt = sb("Tt", [P, SLOTS], F32)
    T.X = sb("X", [P, 2, SLOTS], F32)
    T.RP = sb("RP", [P, 2 * 2 * PARTS * QT], BF16)
    T.Osb = sb("Osb", [P, CHUNK], F32)
    T.rl = sb("rl", [P, QT], F32)
    T.mp0 = sb("mp0", [P, 1], F32)
    T.sk = sb("sk", [P, 1], F32)
    T.z8 = sb("z8", [P, 8], F32)
    T.cf = sb("cf", [P, 1], F32)
    T.junk_d = sb("junk_d", [P, S], BF16)
    T.lo = sb("lo", [P, 1], F32)
    T.mid = sb("mid", [P, 1], F32)
    T.stp = sb("stp", [P, 1], F32)
    T.Qc = sb("Qc", [KROWS, P], BF16)
    T.rowsT = sb("rowsT", [2 * 2 * PARTS * QT, P], BF16)


def place_feed_forward(T, nc, ctx):
    def sb(name, shape, dt):
        return ctx.enter_context(nc.sbuf_tensor(name, shape, dt))

    T.ast = sb("ast", [P, CT, C], F32)
    T.attT = sb("attT", [P, CHUNK], F32)
    T.x1 = sb("x1", [P, CT, C], F32)
    T.x2 = sb("x2", [P, CT, C], F32)
    T.lg = sb("lg", [P, CT, E], F32)
    T.mx = sb("mx", [P, CT], F32)
    T.oh = sb("oh", [P, CT, E], F32)
    T.mask = sb("mask", [P, E, CHUNK], BF16)
    T.xe = sb("xe", [P, 2, CHUNK], F32)
    T.sg2 = sb("sg2", [P, 2, FB * CHUNK], F32)
    T.h = sb("h", [P, 2, FB * CHUNK], F32)
    T.hm = sb("hm", [P, E, FB, CHUNK], F32)
    T.ohT = sb("ohT", [E, CHUNK], BF16)


def build(nc, x, wq, wk, wv, wo, bo, thr, up, gate, down, router, up_s, gate_s, down_s, c_in, wmod, out, qk_aug):
    with ExitStack() as kept:
        T = Places(nc, kept)
        with ExitStack() as ctx:
            place_prepare(T, nc, ctx)
            prepare(nc, T, x.rearrange("b s c -> (b s) c"), wq, wk, wv, wo, bo, thr, up, gate, down, router,
                    up_s, gate_s, down_s, c_in, wmod, qk_aug)
        with ExitStack() as ctx:
            place_attention(T, nc, ctx)
            attention(nc, T, qk_aug)
        with ExitStack() as ctx:
            place_feed_forward(T, nc, ctx)
            feed_forward(nc, T, out.rearrange("b s c -> (b s) c"))


def kernel(**inputs):
    import numpy as np
    import concourse.bacc as bacc
    from concourse.bass_utils import run_bass_kernel_spmd

    nc = bacc.Bacc("TRN2", target_bir_lowering=False, num_devices=1)
    names = ["attn_x", "attn_Wq", "attn_Wk", "attn_Wv", "attn_Wo", "attn_bo", "attn_adaptive_threshold", "ffn_up", "ffn_gate",
             "ffn_down", "ffn_router", "ffn_w_up_s", "ffn_w_gate_s", "ffn_w_down_s", "c", "wmod"]
    arrays, args = {}, []
    for name in names:
        a = np.ascontiguousarray(inputs["L0_" + name])
        arrays["in_" + name] = a
        args.append(nc.dram_tensor("in_" + name, a.shape, mybir.dt.from_np(a.dtype), kind="ExternalInput").ap())
    out = nc.dram_tensor("out_0", (B, S, C), F32, kind="ExternalOutput").ap()
    qk_aug = nc.dram_tensor("qk_aug", (2, HEADS, KROWS, S), BF16).ap()
    build(nc, *args, out, qk_aug)
    return run_bass_kernel_spmd(nc, [arrays], core_ids=[0]).results[0]["out_0"]
```

```python
import concourse.bass as bass
from concourse import mybir
from contextlib import ExitStack

F32 = mybir.dt.float32
BF16 = mybir.dt.bfloat16
I32 = mybir.dt.int32
ACT = mybir.ActivationFunctionType
ALU = mybir.AluOpType
AX = mybir.AxisListType

P = 128
B, S, C = 2, 1024, 128
H, D = 16, 8
QT = S // P
HEADS = B * H
PAIRS = HEADS // 2
SLOTS = 2 * QT
KEEP = S // 2
E, F = 8, 256
FB = F // P
PARTS = 3
REP = PARTS * PARTS
KROWS = REP * D
AUX = 96
UROWS = AUX + PARTS
WROWS = AUX + 2 * PARTS
CAP = P // 2
VW = 32
CHUNK = 512
CT = CHUNK // P
EPS = 1e-5
NWT = 4 + 3 * (E + 1) * FB
POOL_LINKS = 35
COUNTED = [[SLOTS - 1]] + [[n - 1] for n in range(1, 7)] + [[], [6], [], [7], [8, 9], [10, 11], [12], [13], [14]]
LAG = 4
DAMP = [1.0, 1.0, 0.6, 0.9, 0.5]
SLOPE = 2.5066 / S / 4.5 / 2
SLACK = 2.0 ** -21
BISECT = 36


def prepare(nc, T, x, wq, wk, wv, wo, bo, thr, up, gate, down, router, up_s, gate_s, down_s, c_in, wmod, qk_aug):
    sem = T.sem
    loads = sem("prep_loads"); att_loads = sem("prep_att_loads"); cload = sem("prep_c_load"); consts = sem("prep_consts")
    chain_p = sem("prep_chain_pool")
    silu_done = sem("prep_silu"); mod_ready = sem("prep_mod_ready"); mod_done = sem("prep_mod_done")
    wt_ready = sem("prep_wt_ready"); wt_even = sem("prep_wt_even"); wt_odd = sem("prep_wt_odd")
    chain = sem("prep_chain_dve"); chain_a = sem("prep_chain_act")
    x_loaded = [sem(f"prep_x_loaded{n}") for n in range(2)]
    var_ready = sem("prep_var"); std_ready = sem("prep_std"); xhat_ready = sem("prep_xhat")
    xt_ready = sem("prep_xt"); ht_ready = sem("prep_ht")
    qkv_ready = sem("prep_qkv"); v_done = sem("prep_v_done"); part1 = sem("prep_part1")
    qkv_used = sem("prep_qkv_used"); parts_ready = sem("prep_parts")
    tp_ready = sem("prep_tp_ready"); tp_done = sem("prep_tp_done"); qtok_done = sem("prep_qtok_done")
    stored = [sem(f"prep_stored{w}") for w in range(2)]
    nat = T.nat
    groups = (NWT + 3) // 4
    NCH = B * S // CHUNK

    with nc.Block() as block:
        @block.sync
        def _(sp):
            for b in range(B):
                sp.dma_start(T.cT[:, b:b + 1], c_in[b, :].rearrange("(c o) -> c o", o=1)).then_inc(cload, 16)
            sp.dma_start(T.wmod[:, :], wmod).then_inc(cload, 16)
            sp.dma_start(T.borow[:, :], bo.rearrange("(a n) -> a n", a=1)).then_inc(cload, 16)
            sp.dma_start(T.thr0[:, :], thr.partition_broadcast(P)).then_inc(cload, 16)
            sp.dma_start(T.x[:, 0:CT, :], x[0:CHUNK, :].rearrange("(t p) c -> p t c", p=P)).then_inc(x_loaded[0], 16)
            for n, w in enumerate((wq, wk, wv, wo)):
                sp.dma_start(nat[:, n, :], w).then_inc(att_loads, 16)
            sp.dma_start(T.x[:, CT:, :], x[CHUNK:, :].rearrange("(t p) c -> p t c", p=P)).then_inc(x_loaded[1], 16)
            n = 4
            for w, ws in ((gate, gate_s), (up, up_s)):
                sp.dma_start(nat[:, n:n + E * FB, :], w.rearrange("e (f p) c -> p (e f) c", p=P)).then_inc(loads, 16)
                sp.dma_start(nat[:, n + E * FB:n + (E + 1) * FB, :], ws.rearrange("(f p) c -> p f c", p=P)).then_inc(loads, 16)
                n += (E + 1) * FB
            sp.dma_start(nat[:, n:n + E * FB, :].rearrange("p (e f) n -> p e (f n)", e=E), down.rearrange("e c h -> c e h")).then_inc(loads, 16)
            sp.dma_start(nat[:, n + E * FB:n + (E + 1) * FB, :].rearrange("p f n -> p (f n)"), down_s).then_inc(loads, 16)
            sp.dma_start(T.rt_nat[:, :], router).then_inc(loads, 16)
            for ch in range(NCH):
                for w in range(2):
                    sp.wait_ge(tp_done, ch * 2 + w + 1)
                    b, n0 = ch * CHUNK // S, ch * CHUNK % S
                    for part in range(PARTS):
                        rows = slice(part * PARTS, (part + 1) * PARTS) if w else slice(part, REP, PARTS)
                        sp.dma_start(qk_aug[w, rows, b * C:(b + 1) * C, n0:n0 + CHUNK].rearrange("r p n -> p r n"),
                                     T.qkT[:, w * PARTS + part, :].unsqueeze(1).broadcast_to([P, PARTS, CHUNK])).then_inc(stored[w], 16)
            for w in range(2):
                sp.wait_ge(stored[w], NCH * PARTS * 16)

        @block.gpsimd
        def _(pool):
            n = [0]

            def link(ins):
                n[0] += 1
                ins.then_inc(chain_p, 1)
                pool.wait_ge(chain_p, n[0])
            link(pool.memset(T.ident[:, :], 0.0))
            link(pool.affine_select(out=T.ident[:, :], in_=T.ident[:, :], compare_op=ALU.not_equal, fill=1.0,
                                    base=0, pattern=[[-1, P]], channel_multiplier=1))
            pool.tensor_copy(T.ident_b[:, :], T.ident[:, :]).then_inc(consts, 1)
            link(pool.memset(T.tri[:, :], 1.0))
            link(pool.affine_select(out=T.tri[:, :], in_=T.tri[:, :], compare_op=ALU.is_ge, fill=0.0,
                                    base=0, pattern=[[1, P]], channel_multiplier=-1))
            link(pool.memset(T.ones_b[:, :], 1.0))
            link(pool.memset(T.zeros_b[:, :], 0.0))
            link(pool.memset(T.ones_f[:, :], 1.0))
            link(pool.iota(T.iota_i[:, :], pattern=[[1, P]], base=1, channel_multiplier=0))
            link(pool.tensor_copy(T.iota[:, :], T.iota_i[:, :]))
            for e in range(2):
                link(pool.memset(T.QB[64:P, e, :], 0.0))
                link(pool.memset(T.KB[64:P, e, :], 0.0))
                link(pool.memset(T.KB[AUX:P, e, :], 1.0))
                link(pool.memset(T.V32[:, e, :, :], 0.0))
                link(pool.memset(T.V32[:, e, :, D:D + 1], 1.0))
            link(pool.memset(T.tpm[:, :, :], 0.0))
            link(pool.memset(T.half[:, :], 0.0))
            link(pool.memset(T.half[0:CAP, 0:1], 1.0))
            link(pool.memset(T.half[CAP:P, 1:2], 1.0))
            link(pool.memset(T.osel[:, :, :], 0.0))
            for c in range(2):
                for par in range(2):
                    link(pool.affine_select(out=T.osel[:, c, :], in_=T.osel[:, c, :], compare_op=ALU.not_equal, fill=1.0,
                                            base=-32 * (2 * par + c), pattern=[[-1, D + 1]], channel_multiplier=1))
            link(pool.iota(T.iota_i[:, 0:E], pattern=[[-1, E]], base=E, channel_multiplier=0))
            link(pool.tensor_copy(T.down_count[:, :], T.iota_i[:, 0:E]))
            pool.memset(T.epsc[:, :], EPS).then_inc(consts, 1)
            for ch in range(NCH):
                pool.wait_ge(parts_ready, (ch + 1) * CT)
                b, t0 = ch * CHUNK // S, (ch % (S // CHUNK)) * CT
                for t in range(CT):
                    for p in range(PARTS):
                        last = pool.tensor_copy(T.Qtok[:, b * H:(b + 1) * H, t0 + t, p, :],
                                                T.qkp[:, ch % 2, t, p, 0:C].rearrange("p (h d) -> p h d", d=D))
                last.then_inc(qtok_done, 1)

        @block.scalar
        def _(act):
            act.wait_ge(cload, 80)
            act.activation(T.sc[:, :], T.cT[:, :], ACT.Silu).then_inc(silu_done, 1)
            act.wait_ge(consts, 2)
            act.wait_ge(var_ready, 1)
            act.activation(T.stdx[:, :], T.mvx[:, :, 1], ACT.Sqrt, bias=T.epsc[:, 0:1]).then_inc(std_ready, 1)

            def copy_parts(ch):
                for w in range(2):
                    act.wait_ge(tp_ready, ch * 2 + w + 1)
                    if ch:
                        act.wait_ge(stored[w], ch * PARTS * 16)
                    act.activation(T.qkT[:, w * PARTS:(w + 1) * PARTS, :],
                                   T.pUW_b[:, w * 2048:w * 2048 + PARTS * CHUNK].rearrange("p (a n) -> p a n", a=PARTS),
                                   ACT.Copy).then_inc(tp_done, 1)

            for ch in range(NCH):
                for t in range(CT):
                    g = ch * CT + t
                    b, tt = g // QT, g % QT
                    act.wait_ge(qkv_ready, g + 1)
                    if ch >= 2:
                        act.wait_ge(qtok_done, ch - 1)
                        act.wait_ge(tp_ready, 2 * (ch - 1))
                    act.activation(T.qkp[:, ch % 2, t, 0, :], T.pA[:, (g % 2) * 512:(g % 2) * 512 + 2 * C], ACT.Copy).then_inc(part1, 1)
                    act.activation(T.V[:, b * H:(b + 1) * H, tt, :],
                                   T.pA[:, (g % 2) * 512 + 2 * C:(g % 2) * 512 + 3 * C].rearrange("p (h d) -> p h d", d=D),
                                   ACT.Copy).then_inc(v_done, 1)
                copy_parts(ch)
            for k in range(1, groups, 2):
                m = min(4, NWT - 4 * k)
                act.wait_ge(wt_ready, k + 1)
                act.activation(T.wT[:, 4 * k * C:(4 * k + m) * C], T.pM[:, 0:m * C], ACT.Copy).then_inc(wt_odd, 1)

        @block.vector
        def _(dve):
            def done(ins, s, value):
                ins.then_inc(s, 1)
                dve.wait_ge(s, value)

            n = [0]

            def link(ins):
                n[0] += 1
                ins.then_inc(chain, 1)
                dve.wait_ge(chain, n[0])
            dve.wait_ge(cload, 80)
            link(dve.tensor_scalar(T.thrc[:, :], T.thr0[:, :], 0.0, 1.0, ALU.max, ALU.min))
            link(dve.tensor_scalar(T.negthr[:, :], T.thrc[:, :], -1.0, None, ALU.mult))
            for h in range(2):
                dve.wait_ge(x_loaded[h], 16)
                for g in range(CT if h else 0, B * QT if h else CT):
                    last = dve.bn_stats(T.bnx[:, g, :], T.x[:, g, :])
                link(last)
            dve.wait_ge(mod_ready, 1)
            dve.tensor_copy(T.mod[:, :], T.pO[:, 0:6 * B])
            link(dve.tensor_copy(T.gates[:, :], T.pM[:, 0:B * C]))
            dve.sem_inc(mod_done, 1)
            for g in range(B * QT):
                last = dve.bn_aggr(T.mvx[:, g, :], T.bnx[:, g, :])
            link(last)
            link(dve.tensor_scalar(T.vepsx[:, :], T.mvx[:, :, 1], EPS, None, ALU.add))
            dve.sem_inc(var_ready, 1)
            for m in (1, 4):
                link(dve.tensor_scalar(T.mod[:, m * B:(m + 1) * B], T.mod[:, m * B:(m + 1) * B], 1.0, None, ALU.add))
            pairs = ((T.mod[:, 5 * B:6 * B], T.gabs[:, 0:B]), (T.gates[:, :], T.gabs[:, B:B + B * C]))
            for g, size in pairs:
                last = dve.scalar_tensor_tensor(size, g, -1.0, g, ALU.mult, ALU.max)
            link(last)
            for g, size in pairs:
                dve.tensor_scalar(g, g, 0.0, 2.0, ALU.is_ge, ALU.mult)
                last = dve.tensor_scalar(size, size, 0.25, None, ALU.max)
            link(last)
            for g, size in pairs:
                last = dve.tensor_scalar(g, g, -1.0, None, ALU.add)
            link(last)
            for g, size in pairs:
                last = dve.tensor_tensor(g, g, size, ALU.mult)
            link(last)
            dve.wait_ge(wt_ready, 1)
            dve.tensor_scalar(T.wT[:, 0:C], T.pO[:, 0:C], float(D) ** -0.5, None, ALU.mult)
            dve.tensor_copy(T.wT[:, C:4 * C], T.pO[:, C:4 * C]).then_inc(wt_even, 1)

            def normalise(ch):
                for t in range(CT):
                    g = ch * CT + t
                    last = dve.tensor_scalar(T.xhatx[:, g, :], T.x[:, g, :], T.mvx[:, g, 0:1], T.rsx[:, g:g + 1],
                                             ALU.subtract, ALU.mult)
                last.then_inc(xhat_ready, 1)

            dve.wait_ge(std_ready, 1)
            link(dve.reciprocal(T.rsx[:, :], T.stdx[:, :]))
            link(dve.tensor_tensor(T.rsx[:, :], T.rsx[:, :], T.vepsx[:, :], ALU.mult))
            link(dve.tensor_tensor(T.rsx[:, :], T.rsx[:, :], T.stdx[:, :], ALU.add))
            link(dve.tensor_scalar(T.rsx[:, :], T.rsx[:, :], 0.5, None, ALU.mult))
            link(dve.reciprocal(T.rsx[:, :], T.rsx[:, :]))
            normalise(0)
            for ch in range(NCH):
                b = ch * CHUNK // S
                dve.wait_ge(xt_ready, ch + 1)
                if ch:
                    dve.wait_ge(qkv_ready, ch * CT)
                dve.tensor_scalar(T.hT[:, :], T.pO[:, :], T.mod[:, B + b:B + b + 1], T.mod[:, b:b + 1],
                                  ALU.mult, ALU.add).then_inc(ht_ready, 1)
                if ch + 1 < NCH:
                    normalise(ch + 1)
                for t in range(CT):
                    g = ch * CT + t
                    src = T.pA[:, (g % 2) * 512:(g % 2) * 512 + 2 * C]
                    qkp = T.qkp[:, ch % 2, t, :, :]
                    dve.wait_ge(v_done, g + 1)
                    dve.wait_ge(part1, g + 1)
                    done(dve.tensor_tensor(T.rem[:, :], src, qkp[:, 0, :], ALU.subtract), qkv_used, g + 1)
                    link(dve.tensor_copy(qkp[:, 1, :], T.rem[:, :]))
                    done(dve.tensor_tensor(qkp[:, 2, :], T.rem[:, :], qkp[:, 1, :], ALU.subtract), parts_ready, g + 1)
            for k in range(2, groups, 2):
                m = min(4, NWT - 4 * k)
                dve.wait_ge(wt_ready, k + 1)
                dve.tensor_copy(T.wT[:, 4 * k * C:(4 * k + m) * C], T.pO[:, 0:m * C]).then_inc(wt_even, 1)
            dve.wait_ge(wt_ready, groups + 1)
            dve.tensor_copy(T.rT[:, :], T.pA[:, 0:E]).then_inc(wt_even, 1)

        @block.tensor
        def _(pe):
            pe.wait_ge(cload, 80)
            pe.wait_ge(silu_done, 1)
            for m in range(6):
                nc.tensor.matmul(T.pO[:, m * B:(m + 1) * B], T.wmod[:, m * C:(m + 1) * C], T.sc[:, :], start=True, stop=True)
            for b in range(B):
                last = nc.tensor.matmul(T.pM[:, b * C:(b + 1) * C], T.sc[:, b:b + 1].broadcast_to([P, P]),
                                        T.wmod[:, 2 * C:3 * C], start=True, stop=True)
            last.then_inc(mod_ready, 1)
            pe.wait_ge(mod_done, 1)
            pe.wait_ge(consts, 1)

            def weights(k):
                dst = T.pM if k % 2 else T.pO
                for j in range(min(4, NWT - 4 * k)):
                    last = nc.tensor.transpose(dst[:, j * C:(j + 1) * C], nat[:, 4 * k + j, :], T.ident[:, :])
                last.then_inc(wt_ready, 1)

            def transpose_xhat(ch):
                pe.wait_ge(xhat_ready, ch + 1)
                if ch:
                    pe.wait_ge(ht_ready, ch)
                for t in range(CT):
                    last = nc.tensor.transpose(T.pO[:, t * P:(t + 1) * P], T.xhatx[:, ch * CT + t, :], T.ident[:, :])
                last.then_inc(xt_ready, 1)

            def transpose_parts(ch):
                pe.wait_ge(parts_ready, (ch + 1) * CT)
                for w in range(2):
                    if ch:
                        pe.wait_ge(tp_done, 2 * (ch - 1) + w + 1)
                    for p in range(PARTS):
                        for t in range(CT):
                            o = w * 2048 + p * CHUNK + t * P
                            last = nc.tensor.transpose(T.pUW_b[:, o:o + P], T.qkp[:, ch % 2, t, p, w * C:(w + 1) * C], T.ident_b[:, :])
                    last.then_inc(tp_ready, 1)

            pe.wait_ge(att_loads, 4 * 16)
            weights(0)
            pe.wait_ge(wt_even, 1)
            transpose_xhat(0)
            for ch in range(NCH):
                pe.wait_ge(ht_ready, ch + 1)
                for t in range(CT):
                    g = ch * CT + t
                    if g >= 2:
                        pe.wait_ge(qkv_used, g - 1)
                    nc.tensor.matmul(T.pA[:, (g % 2) * 512:(g % 2) * 512 + 3 * C], T.hT[:, t * P:(t + 1) * P],
                                     T.wT[:, 0:3 * C], start=True, stop=True).then_inc(qkv_ready, 1)
                if ch + 1 < NCH:
                    transpose_xhat(ch + 1)
                transpose_parts(ch)
            pe.wait_ge(loads, 7 * 16)
            for k in range(1, groups):
                if k >= 3:
                    pe.wait_ge(*((wt_odd, (k - 1) // 2) if k % 2 else (wt_even, k // 2)))
                weights(k)
            nc.tensor.transpose(T.pA[:, 0:E], T.rt_nat[:, :], T.ident[0:E, 0:E]).then_inc(wt_ready, 1)


def attention(nc, T, qk_aug):
    sem = T.sem
    a_load = [sem(f"a_load{e}") for e in range(2)]
    b_load = [sem(f"b_load{e}") for e in range(2)]
    aux_load = [sem(f"aux_load{e}") for e in range(2)]
    s_load = sem("s_load")
    a_ready, a_copied, a_counted = sem("a_ready"), sem("a_copied"), sem("a_counted")
    u_ready, w_ready, e_ready, p_ready = sem("u_ready"), sem("w_ready"), sem("e_ready"), sem("p_ready")
    pv_done, o_copied, ot_ready, o_done, o_chain = sem("pv_done"), sem("o_copied"), sem("ot_ready"), sem("o_done"), sem("o_chain")
    v_ready, qg_ready = sem("v_ready"), sem("qg_ready")
    m_taken, m_kept, st_taken, flagged = sem("m_taken"), sem("m_kept"), sem("st_taken"), sem("flagged")
    pos_ready, pos_used, sel_ready = sem("pos_ready"), sem("pos_used"), sem("sel_ready")
    gat_ready, gat_used = sem("gat_ready"), sem("gat_used")
    ss_ready, ss_copied, step_t, step_c = sem("ss_ready"), sem("ss_copied"), sem("step_t"), sem("step_c")
    selT_ready, selT_copied = sem("selT_ready"), sem("selT_copied")
    cnt_ready, w8_ready, z_ready, kth_ready = sem("cnt_ready"), sem("w8_ready"), sem("z_ready"), sem("kth_ready")
    tp_ready, sc_ready, flag_ready, t_ready, t_final = (sem("tparts_ready"), sem("scattered"), sem("flag_ready"),
                                                        sem("t_ready"), sem("t_final"))
    rows_src, rowsT_ready, rows_copied = sem("rows_src"), sem("rowsT_ready"), sem("rows_copied")
    chain, chain_p = sem("search_chain"), sem("search_chain_pool")
    fb_ready, fb_copied, fb_chain = sem("fb_ready"), sem("fb_copied"), sem("fb_chain")
    settled = sem("settled")
    FBN = SLOTS * (2 + 5 * BISECT + 4)
    K0 = len(DAMP)
    last_i = PAIRS + 2

    def static(i):
        return isinstance(i, int)

    def iterations(eng, body):
        for i in range(3):
            body(i)
        with eng.Fori(3, PAIRS - 1) as i:
            body(i)
        for i in range(PAIRS - 1, last_i + 1):
            body(i)

    def scores(i):
        return not static(i) or i < PAIRS

    def searches(i):
        return not static(i) or 1 <= i <= PAIRS

    def b_tile(i, n):
        g = (i - 2) * SLOTS + n - LAG
        if static(i) and not 0 <= g < PAIRS * SLOTS:
            return None
        k = (n - LAG) % SLOTS
        return g, k // QT, k % QT

    def a_alone(i):
        return static(i) and i < 2

    def b_alone(i):
        return not scores(i)

    def a_bank(i, n):
        return T.pW if a_alone(i) and n % 2 else T.pA

    def u_bank(i, n):
        return T.pA if b_alone(i) and n % 2 else T.pU

    def head_before(i, n):
        return 2 * (i - 2) + (n - LAG) // QT - 1

    with nc.Block() as block:
        @block.sync
        def _(sp):
            def load(dst, w, head, s):
                sp.dma_start(dst, qk_aug[w, :, bass.ds(head * D, D), :]).then_inc(s, 16)

            def aux(e):
                sp.dma_start(T.QB[AUX:WROWS, e, :], T.rowsT[e * 48:(e + 1) * 48, :]).then_inc(aux_load[e], 16)

            def load_a(i, e):
                sp.wait_ge(a_ready, i * SLOTS + (e + 1) * QT)
                load(T.QA[0:KROWS, e, :], 0, 2 * i + 2 + e, a_load[e])
                load(T.KA[0:KROWS, e, :], 1, 2 * i + 2 + e, a_load[e])

            def body(i):
                more_a = not static(i) or i < PAIRS - 1
                if b_tile(i, LAG):
                    if not (static(i) and i == 2):
                        sp.wait_ge(p_ready, (i - 2) * SLOTS)
                    load(T.QB[0:KROWS, 1, :], 0, 2 * i - 3, b_load[1])
                    load(T.KB[0:KROWS, 1, :], 1, 2 * i - 3, b_load[1])
                    aux(1)
                if more_a:
                    load_a(i, 0)
                if searches(i):
                    if b_tile(i, LAG):
                        sp.wait_ge(p_ready, (i - 2) * SLOTS + QT)
                    load(T.QB[0:KROWS, 0, :], 0, 2 * i - 2, b_load[0])
                    load(T.KB[0:KROWS, 0, :], 1, 2 * i - 2, b_load[0])
                if scores(i):
                    if searches(i):
                        sp.wait_ge(t_final, i)
                    for w, dst in ((1, T.KS), (0, T.QS)):
                        for e in range(2):
                            load(dst[0:KROWS, e, :], w, 2 * i + e, s_load)
                if searches(i):
                    sp.wait_ge(rows_copied, i)
                    aux(0)
                if more_a:
                    load_a(i, 1)

            for e in range(2):
                load(T.QA[0:KROWS, e, :], 0, e, a_load[e])
                load(T.KA[0:KROWS, e, :], 1, e, a_load[e])
            iterations(sp, body)

        @block.gpsimd
        def _(pool):
            def gate():
                pool.sem_inc(settled, 1)

            def values(e, pair):
                if not (static(pair) and pair == 0):
                    pool.wait_ge(pv_done, pair * QT - QT + (e + 1) * (QT // 2))
                gate()
                pool.tensor_copy(T.V32[:, e, :, 0:D],
                                 T.V[:, bass.ds(2 * pair + e, 1), :, :].rearrange("p o t d -> p (o t) d")).then_inc(v_ready, 1)

            def query(i, k):
                if k == 0 and searches(i):
                    pool.wait_ge(gat_ready, i)
                    gate()
                e, r = k // PARTS, k % PARTS
                copy = pool.tensor_copy(
                    T.QG[:, e, :, r * PARTS * D:(r + 1) * PARTS * D].rearrange("p t (a d) -> p t a d", a=PARTS),
                    T.Qtok[:, bass.ds(2 * i + e, 1), :, :, :].rearrange("p o t a d -> p (o t) a d"))
                if k == 2 * PARTS - 1:
                    copy.then_inc(qg_ready, 1)

            def body(i):
                links = [0]

                def link(ins):
                    links[0] += 1
                    ins.then_inc(chain_p, 1)
                    pool.wait_ge(chain_p, (i - 1) * POOL_LINKS + links[0])
                if searches(i):
                    pool.wait_ge(a_counted, i * SLOTS)
                    gate()
                    pool.tensor_scalar(T.Fb[:, :], T.cnt[:, :], 0.0, None, ALU.is_ge).then_inc(flagged, 1)
                    pool.tensor_copy(T.st[:, :, 0], T.cnt[:, :])
                    pool.tensor_scalar(T.st[:, :, 2], T.cnt[:, :], 0.0, None, ALU.is_ge)
                    pool.wait_ge(m_taken, i)
                    gate()
                    pool.tensor_copy(T.st[:, :, 1], T.Mp[:, :]).then_inc(st_taken, 1)
                    pool.tensor_copy(T.Mq[:, :], T.Mp[:, :]).then_inc(m_kept, 1)
                    pool.wait_ge(gat_used, i)
                    gate()
                    link(pool.tensor_scalar(T.mp0[:, :], T.gs[:, 1:2], 0.0, None, ALU.max))
                    gate()
                    pool.tensor_scalar(T.sk[:, :], T.mp0[:, :], -SLACK, None, ALU.mult)
                    pool.tensor_scalar(T.nd[:, :], T.gs[:, 0:1], 1.0, 8.0, ALU.mult, ALU.add)
                    link(pool.tensor_scalar(T.sl[:, :], T.mp0[:, :], SLOPE, None, ALU.mult))
                    link(pool.tensor_tensor(T.dt[:, :], T.nd[:, :], T.sl[:, :], ALU.mult))
                    pool.tensor_tensor(T.tc[:, 0:1], T.dt[:, :], T.thrc[:, :], ALU.add).then_inc(step_t, 1)
                    for k in range(K0):
                        pool.wait_ge(step_c, (i - 1) * K0 + k + 1)
                        gate()
                        link(pool.tensor_scalar(T.nd[:, :], T.sg[:, k:k + 1], -1.0, 8.0, ALU.mult, ALU.add))
                        pool.tensor_tensor(T.ns[:, :], T.nd[:, :], T.sl[:, :], ALU.mult)
                        link(pool.tensor_tensor(T.dt[:, :], T.nd[:, :], T.nd[:, :], ALU.mult))
                        gate()
                        link(pool.tensor_scalar(T.dt[:, :], T.dt[:, :], 6.5 * 6.5, DAMP[k], ALU.is_gt, ALU.mult))
                        gate()
                        pool.tensor_scalar(T.tc[:, k + 1:k + 2], T.dt[:, :], T.ns[:, 0:1], T.tc[:, k:k + 1],
                                           ALU.mult, ALU.add).then_inc(step_t, 1)
                        if scores(i):
                            query(i, k)
                if b_tile(i, LAG):
                    values(1, i - 2)
                if searches(i):
                    pool.wait_ge(cnt_ready, i)
                    gate()
                    link(pool.tensor_scalar(T.ix[:, :], T.c1[:, :], -1.0, KEEP + 0.5, ALU.mult, ALU.add))
                    gate()
                    link(pool.tensor_scalar(T.z8[:, :], T.iota[:, 0:8], T.ix[:, 0:1], None, ALU.subtract))
                    pool.tensor_tensor(T.z8[:, :], T.z8[:, :], T.z8[:, :], ALU.mult).then_inc(z_ready, 1)
                    pool.tensor_scalar(T.bad[:, 2:3], T.bad[:, 1:2], CAP + 0.5, None, ALU.is_gt)
                    link(pool.tensor_scalar(T.nd[:, :], T.ix[:, :], -4.5, None, ALU.add))
                    link(pool.tensor_tensor(T.nd[:, :], T.nd[:, :], T.nd[:, :], ALU.mult))
                    gate()
                    link(pool.tensor_scalar(T.nd[:, :], T.nd[:, :], 9.5, None, ALU.is_gt))
                    link(pool.tensor_tensor(T.nd[:, :], T.nd[:, :], T.gs[:, 2:3], ALU.mult))
                    link(pool.tensor_tensor(T.badb[:, :], T.nd[:, :], T.bad[:, 2:3], ALU.add))
                    pool.wait_ge(kth_ready, i)
                    gate()
                    link(pool.tensor_scalar(T.kth[:, :], T.kth[:, :], 0.5, None, ALU.mult))
                    link(pool.tensor_tensor(T.kth[:, :], T.kth[:, :], T.sk[:, :], ALU.add))
                    gate()
                    link(pool.tensor_copy(T.t3[:, 0:1], T.kth[:, :]))
                    link(pool.tensor_tensor(T.dt[:, :], T.kth[:, :], T.t3[:, 0:1], ALU.subtract))
                    gate()
                    link(pool.tensor_copy(T.t3[:, 1:2], T.dt[:, :]))
                    link(pool.tensor_tensor(T.t3[:, 2:3], T.dt[:, :], T.t3[:, 1:2], ALU.subtract))
                    pool.tensor_tensor(T.tpm[:, :, :], T.t3[:, :].unsqueeze(1).broadcast_to([P, 2, PARTS]),
                                       T.half[:, :].unsqueeze(2).broadcast_to([P, 2, PARTS]), ALU.mult).then_inc(tp_ready, 1)
                    pool.wait_ge(t_final, i)
                    r = T.RP[:, :].rearrange("p (e k a t) -> p k a e t", e=2, k=2, a=PARTS)
                    xv = T.X[:, :, :].rearrange("p k (e t) -> p k e t", e=2)
                    gate()
                    pool.tensor_scalar(T.X[:, 0, :], T.Tt[:, :], -1.0, None, ALU.mult)
                    link(pool.tensor_tensor(T.X[:, 1, :], T.Tt[:, :], T.Mq[:, :], ALU.subtract))
                    gate()
                    link(pool.tensor_copy(r[:, :, 0], xv))
                    link(pool.tensor_tensor(xv, xv, r[:, :, 0], ALU.subtract))
                    gate()
                    link(pool.tensor_copy(r[:, :, 1], xv))
                    pool.tensor_tensor(r[:, :, 2], xv, r[:, :, 1], ALU.subtract).then_inc(rows_src, 1)
                    pool.wait_ge(rows_src, i)
                    assert links[0] == POOL_LINKS, links[0]
                    values(0, i - 1)
                if scores(i):
                    for k in range(K0 if searches(i) else 0, 2 * PARTS):
                        query(i, k)
            iterations(pool, body)

        @block.scalar
        def _(act):
            def copy_o(head):
                act.wait_ge(pv_done, (head + 1) * (QT // 2))
                if not (static(head) and head == 0):
                    act.wait_ge(ot_ready, head)
                act.activation(T.Osb[:, :], T.pO[:, :], ACT.Copy).then_inc(o_copied, 1)

            def body(i):
                for n in range(SLOTS):
                    ahead = b_tile(i, n + 1)
                    if ahead:
                        g, e, t = ahead
                        act.wait_ge(w_ready, g + 1)
                        if not (static(i) and g < 4):
                            act.wait_ge(pv_done, (i - 2) * QT + (n + 1 - LAG - 4) // 2 + 1)
                        act.activation(T.E[:, (n + 1) % 4, :], T.pW[:, :], ACT.Exp).then_inc(e_ready, 1)
                    for m in COUNTED[n] if (scores(i) if n else searches(i)) else ():
                        act.wait_ge(a_copied, i * SLOTS + m + 1 if n else i * SLOTS)
                        if m == 0 and searches(i):
                            act.wait_ge(st_taken, i)
                        act.activation(T.junk_a[:, m % 4, :], T.Sc[:, m % 4, :], ACT.Sign, bias=T.negthr[:, 0:1],
                                       accum_out=T.cnt[:, m:m + 1]).then_inc(a_counted, 1)
                    bt = b_tile(i, n)
                    if bt and bt[2] == 0 and not (static(i) and bt[0] < QT):
                        copy_o(head_before(i, n))
                    if not searches(i):
                        continue
                    if n in (3, 4):
                        act.wait_ge(ss_ready, 2 * (i - 1) + n - 2)
                        if n == 3 and not (static(i) and i == 1):
                            act.wait_ge(t_final, i - 1)
                        act.activation(T.Ss[:, (n - 3) * 512:(n - 2) * 512], T.pM[:, :], ACT.Copy).then_inc(ss_copied, 1)
                    if 5 <= n < 5 + K0:
                        k = n - 5
                        if k == 0:
                            act.wait_ge(ss_copied, 2 * i)
                        act.wait_ge(step_t, (i - 1) * (K0 + 1) + k + 1)
                        act.activation(T.junk_a2[:, :], T.Ss[:, :], ACT.Sign, bias=T.tc[:, k:k + 1], scale=-1.0,
                                       accum_out=T.sg[:, k:k + 1]).then_inc(step_c, 1)
                    if n == 11:
                        act.wait_ge(selT_ready, i)
                        act.activation(T.SelT[:, :], T.pM_b[:, :], ACT.Copy).then_inc(selT_copied, 1)
            iterations(act, body)
            copy_o(HEADS - 1)

        @block.vector
        def _(dve):
            def done(ins, s, value):
                ins.then_inc(s, 1)
                dve.wait_ge(s, value)

            def finish_o(head):
                dve.wait_ge(ot_ready, head + 1)
                o = T.pM[:, 0:QT * (D + 1)].rearrange("p (t c d) -> p c t d", c=2, d=D + 1)
                rl = T.rl[:, :].rearrange("p (c t) -> p c t", c=2)
                if not (static(head) and head == 0):
                    dve.wait_ge(o_done, head)
                done(dve.reciprocal(rl, o[:, :, :, D]), o_chain, head + 1)
                dve.tensor_tensor(T.attn[:, bass.ds(head, 1), :, :].rearrange("p o (c t) d -> p (o c) t d", c=2), o[:, :, :, 0:D],
                                  rl.unsqueeze(3).broadcast_to([P, 2, QT // 2, D]), ALU.mult).then_inc(o_done, 1)

            def exhaustive(i):
                m = [0]

                def flink(ins):
                    m[0] += 1
                    done(ins, fb_chain, (i - 1) * FBN + m[0])
                for n in range(SLOTS):
                    for hf in range(2):
                        dve.wait_ge(fb_ready, (i - 1) * 2 * SLOTS + 2 * n + hf + 1)
                        dve.tensor_copy(T.Ss[:, hf * 512:(hf + 1) * 512], T.pM[:, :]).then_inc(fb_copied, 1)
                    dve.wait_ge(fb_copied, (i - 1) * 2 * SLOTS + 2 * n + 2)
                    flink(dve.tensor_copy(T.lo[:, :], T.thrc[:, :]))
                    flink(dve.tensor_scalar(T.stp[:, :], T.Mp[:, n:n + 1], 0.0, 1.0, ALU.max, ALU.add))
                    dve.sem_inc(settled, 1)
                    with dve.Fori(0, BISECT) as r:
                        base = (i - 1) * FBN + n * (6 + 5 * BISECT) + 2 + 5 * r
                        done(dve.tensor_tensor(T.mid[:, :], T.lo[:, :], T.stp[:, :], ALU.add), fb_chain, base + 1)
                        done(dve.tensor_scalar(T.Wm[:, :], T.Ss[:, :], T.mid[:, 0:1], None, ALU.is_ge, ALU.add,
                                               accum_out=T.cf[:, :]), fb_chain, base + 2)
                        done(dve.scalar_tensor_tensor(T.mid[:, :], T.cf[:, :], KEEP - 0.5, T.stp[:, :], ALU.is_ge, ALU.mult),
                             fb_chain, base + 3)
                        done(dve.tensor_tensor(T.lo[:, :], T.lo[:, :], T.mid[:, :], ALU.add), fb_chain, base + 4)
                        done(dve.tensor_scalar(T.stp[:, :], T.stp[:, :], 0.5, None, ALU.mult), fb_chain, base + 5)
                        dve.sem_inc(settled, 1)
                    m[0] += 5 * BISECT
                    flink(dve.tensor_scalar(T.mid[:, :], T.Mp[:, n:n + 1], 0.0, -SLACK, ALU.max, ALU.mult))
                    flink(dve.tensor_tensor(T.lo[:, :], T.lo[:, :], T.mid[:, :], ALU.add))
                    flink(dve.tensor_tensor(T.Tt[:, n:n + 1], T.lo[:, :], T.thrc[:, :], ALU.max))
                    flink(dve.tensor_copy(T.cf[:, :], T.lo[:, :]))
                dve.sem_inc(settled, 1)
                assert m[0] == FBN, (m[0], FBN)

            def search(i, n, place):
                at = (n, place)
                if at == (0, 0):
                    dve.wait_ge(a_copied, i * SLOTS)
                    if not (static(i) and i == 1):
                        dve.wait_ge(m_kept, i - 1)
                    done(dve.tensor_copy(T.Mp[:, :], T.M[:, :]), m_taken, i)
                if at == (1, 1):
                    dve.wait_ge(pos_ready, i)
                    if not (static(i) and i == 1):
                        dve.wait_ge(tp_ready, i - 1)
                    dve.tensor_tensor(T.posF[:, :], T.pM[:, 0:SLOTS], T.Fb[:, :], ALU.mult).then_inc(pos_used, 1)
                if at == (1, 2):
                    dve.wait_ge(pos_used, i)
                    dve.tensor_tensor(T.Sel[:, :, :, :].rearrange("p t e c -> p e t c"),
                                      T.iota[:, 0:CAP].unsqueeze(1).unsqueeze(1).broadcast_to([P, 2, QT, CAP]),
                                      T.posF[:, :].rearrange("p (e t) -> p e t", e=2).unsqueeze(3).broadcast_to([P, 2, QT, CAP]),
                                      ALU.is_equal).then_inc(sel_ready, 1)
                    dve.tensor_reduce(T.bad[:, 1:2], T.posF[:, :], AX.X, ALU.max)
                if at == (2, 2):
                    dve.wait_ge(gat_ready, i)
                    dve.tensor_copy(T.Qc[:, :], T.pM[0:KROWS, 0:P])
                    dve.tensor_copy(T.gs[:, :], T.pM[:, P:P + 3]).then_inc(gat_used, 1)
                t = T.tc[:, K0:K0 + 1]
                if at == (10, 2):
                    dve.wait_ge(step_t, i * (K0 + 1))
                    dve.tensor_scalar(T.junk_d[:, :], T.Ss[:, :], t, None, ALU.is_ge, ALU.add, accum_out=T.c1[:, :]).then_inc(cnt_ready, 1)
                if at == (11, 1):
                    done(dve.scalar_tensor_tensor(T.Wm[:, :], T.Ss[:, :], t, T.Ss[:, :], ALU.is_lt, ALU.mult), chain, i)
                if at == (12, 1):
                    dve.max(T.W8[:, :], T.Wm[:, :]).then_inc(w8_ready, 1)
                if at == (12, 2):
                    dve.wait_ge(z_ready, i)
                    dve.wait_ge(w8_ready, i)
                    dve.scalar_tensor_tensor(T.h8[:, :], T.z8[:, :], 0.5, T.W8[:, :], ALU.is_lt, ALU.mult,
                                             accum_out=T.kth[:, :]).then_inc(kth_ready, 1)
                if at == (15, 0):
                    dve.wait_ge(sc_ready, i)
                    dve.tensor_copy(T.flag[0:1, 0:1], T.pM[0:1, 64:65])
                    done(dve.tensor_reduce(T.Tt[:, :].rearrange("p (e t) -> p t e", e=2),
                                           T.pM[:, 0:48].rearrange("p (t e a) -> p t e a", e=2, a=PARTS), AX.X, ALU.add),
                         flag_ready, i)
                if at == (15, 1):
                    dve.tensor_scalar(T.Tt[:, :], T.Tt[:, :], T.thrc[:, 0:1], None, ALU.max).then_inc(t_ready, 1)
                if at == (15, 2):
                    dve.wait_ge(t_ready, i)
                    dve.sem_inc(settled, 1)
                    flag = dve.value_load(T.flag[0:1, 0:1], min_val=0, max_val=P * 2)
                    with dve.If(flag > 0):
                        exhaustive(i)
                    with dve.Else():
                        dve.sem_inc(fb_copied, 2 * SLOTS)
                        dve.sem_inc(fb_chain, FBN)
                    dve.sem_inc(t_final, 1)

            def take_rows(i):
                dve.wait_ge(rowsT_ready, i)
                if not (static(i) and i == 1):
                    for e in range(2):
                        dve.wait_ge(aux_load[e], (i - 1) * 16)
                dve.tensor_copy(T.rowsT[:, :], T.pM_b[0:96, 0:P]).then_inc(rows_copied, 1)

            def body(i):
                for n in range(SLOTS):
                    if searches(i):
                        search(i, n, 0)
                    if scores(i):
                        g = i * SLOTS + n
                        dve.wait_ge(a_ready, g + 1)
                        if not (static(i) and g < 4):
                            dve.wait_ge(a_counted, g - 3)
                        dve.tensor_scalar(T.Sc[:, n % 4, :], a_bank(i, n), 1.0, None, ALU.mult, ALU.max,
                                          accum_out=T.M[:, n:n + 1]).then_inc(a_copied, 1)
                    bt = b_tile(i, n)
                    if searches(i):
                        search(i, n, 1)
                    if bt:
                        g, e, t = bt
                        dve.wait_ge(e_ready, g + 1)
                        dve.wait_ge(u_ready, g + 1)
                        dve.scalar_tensor_tensor(T.E[:, n % 4, :], u_bank(i, n), 0.0, T.E[:, n % 4, :],
                                                 ALU.is_ge, ALU.mult).then_inc(p_ready, 1)
                    if bt and bt[2] == 1 and not (static(i) and bt[0] < QT):
                        finish_o(head_before(i, n))
                    if n == 0 and searches(i - 1):
                        take_rows(i - 1)
                    if searches(i):
                        search(i, n, 2)
            iterations(dve, body)
            finish_o(HEADS - 1)

        @block.tensor
        def _(pe):
            def products(i, n):
                m = (n - LAG) // 2 - 1
                k, e = m % (QT // 2), (m // (QT // 2)) % 2
                pe.wait_ge(p_ready, (i - 2) * SLOTS + n - LAG)
                if k == 0:
                    head = 2 * (i - 2) + m // (QT // 2)
                    pe.wait_ge(v_ready, head + 1)
                    if not (static(i) and head == 0):
                        pe.wait_ge(o_copied, head)
                for par in range(2):
                    for c in range(2):
                        g = 32 * (2 * par + c)
                        last = nc.tensor.matmul(T.pO[g:g + VW, :], T.V32[:, e, 2 * k + par, :],
                                                T.E[:, (n - 2 + par) % 4, c * 512:(c + 1) * 512],
                                                start=(k == 0), stop=(k == QT // 2 - 1))
                last.then_inc(pv_done, 1)

            def gather_o(head):
                pe.wait_ge(o_copied, head + 1)
                if not (static(head) and head == 0):
                    pe.wait_ge(o_done, head)
                for t in range(QT // 2):
                    o = t * 2 * (D + 1)
                    last = nc.tensor.matmul(T.pM[:, o:o + 2 * (D + 1)], T.Osb[:, t * P:(t + 1) * P],
                                            T.osel[:, :, :].rearrange("p c d -> p (c d)"), start=True, stop=True)
                last.then_inc(ot_ready, 1)

            def search(i, n):
                if n == 1:
                    pe.wait_ge(flagged, i)
                    if not (static(i) and i == 1):
                        pe.wait_ge(rows_copied, i - 1)
                    F = T.Fb[:, :].rearrange("p (e t) -> p e t", e=2)
                    pos = T.pM[:, 0:SLOTS].rearrange("p (e t) -> p e t", e=2)
                    nc.tensor.matmul(pos, T.zeros_b[:, :], F, start=True, stop=False)
                    for s in range(1, QT):
                        nc.tensor.matmul(pos[:, :, s:QT], T.ones_b[:, :], F[:, :, 0:QT - s], start=False, stop=False)
                    nc.tensor.matmul(pos, T.tri[:, :], F, start=False, stop=True).then_inc(pos_ready, 1)
                if n == 2:
                    pe.wait_ge(sel_ready, i)
                    pe.wait_ge(st_taken, i)
                    pe.wait_ge(qg_ready, i)
                    for e in range(2):
                        for t in range(QT):
                            nc.tensor.matmul(T.pM[0:KROWS, e * CAP:(e + 1) * CAP], T.QG[:, e, t, :], T.Sel[:, t, e, :],
                                             start=(t == 0), stop=(t == QT - 1))
                    for e in range(2):
                        for t in range(QT):
                            last = nc.tensor.matmul(T.pM[e * CAP:(e + 1) * CAP, P:P + 3], T.Sel[:, t, e, :],
                                                    T.st[:, e * QT + t, :], start=(t == 0), stop=(t == QT - 1))
                    last.then_inc(gat_ready, 1)
                if n in (3, 4):
                    if n == 3:
                        pe.wait_ge(gat_used, i)
                        pe.wait_ge(s_load, i * 64)
                    else:
                        pe.wait_ge(ss_copied, 2 * (i - 1) + 1)
                    for e in range(2):
                        last = nc.tensor.matmul(T.pM[e * CAP:(e + 1) * CAP, :], T.Qc[0:KROWS, e * CAP:(e + 1) * CAP],
                                                T.KS[0:KROWS, e, (n - 3) * 512:(n - 2) * 512], start=True, stop=True)
                    last.then_inc(ss_ready, 1)
                if n == 9:
                    pe.wait_ge(ss_copied, 2 * i)
                    if b_tile(i, 6) and not (static(i) and i == 2):
                        pe.wait_ge(o_done, 2 * (i - 2))
                    for t in range(QT):
                        last = nc.tensor.transpose(T.pM_b[:, t * P:(t + 1) * P], T.Sel[:, t, :, :].rearrange("p e c -> p (e c)"),
                                                   T.ident_b[:, :])
                    last.then_inc(selT_ready, 1)
                if n == 14:
                    pe.wait_ge(tp_ready, i)
                    pe.wait_ge(selT_copied, i)
                    if b_tile(i, 13):
                        pe.wait_ge(o_done, 2 * (i - 2) + 1)
                    for t in range(QT):
                        nc.tensor.matmul(T.pM[:, t * 6:(t + 1) * 6], T.SelT[:, t * P:(t + 1) * P],
                                         T.tpm[:, :, :].rearrange("p e a -> p (e a)"), start=True, stop=True)
                    nc.tensor.matmul(T.pM[0:1, 64:65], T.badb[:, 0:1], T.ones_b[:, 0:1], start=True, stop=True).then_inc(sc_ready, 1)
                if n == 15:
                    pe.wait_ge(t_ready, i)
                    pe.sem_inc(settled, 1)
                    flag = pe.value_load(T.flag[0:1, 0:1], min_val=0, max_val=P * 2)
                    with pe.If(flag > 0):
                        if b_tile(i, 14):
                            pe.wait_ge(o_done, 2 * (i - 2) + 1)
                            pe.sem_inc(settled, 1)
                        for m in range(SLOTS):
                            for hf in range(2):
                                if m + hf:
                                    pe.wait_ge(fb_copied, (i - 1) * 2 * SLOTS + 2 * m + hf)
                                nc.tensor.matmul(T.pM[:, :], T.QS[0:KROWS, m // QT, (m % QT) * P:(m % QT + 1) * P],
                                                 T.KS[0:KROWS, m // QT, hf * 512:(hf + 1) * 512], start=True, stop=True).then_inc(fb_ready, 1)
                    with pe.Else():
                        pe.sem_inc(fb_ready, 2 * SLOTS)

            def transpose_rows(i):
                if b_tile(i, 14):
                    pe.wait_ge(o_done, 2 * (i - 2) + 1)
                pe.wait_ge(fb_copied, i * 2 * SLOTS)
                pe.wait_ge(rows_src, i)
                nc.tensor.transpose(T.pM_b[0:96, 0:P], T.RP[:, :], T.ident_b[:, :]).then_inc(rowsT_ready, 1)

            def body(i):
                for n in range(SLOTS):
                    if scores(i):
                        ga = i * SLOTS + n
                        ea, ta = n // QT, n % QT
                        if ta == 0:
                            pe.wait_ge(a_load[ea], (i + 1) * 32)
                        turns = int(a_alone(i))
                        if not (static(i) and ga <= turns):
                            pe.wait_ge(a_copied, ga - turns)
                        for c in range(2):
                            last = nc.tensor.matmul(a_bank(i, n)[:, c * 512:(c + 1) * 512], T.QA[0:KROWS, ea, ta * P:(ta + 1) * P],
                                                    T.KA[0:KROWS, ea, c * 512:(c + 1) * 512], start=True, stop=True)
                        last.then_inc(a_ready, 1)
                    ahead = b_tile(i, n + 1)
                    if ahead:
                        gb, e, t = ahead
                        if t == 0:
                            pe.wait_ge(b_load[e], (i - 1) * 32)
                            pe.wait_ge(aux_load[e], (i - 1) * 16)
                        if not (static(i) and gb == 0):
                            pe.wait_ge(e_ready, gb)
                        for c in range(2):
                            last = nc.tensor.matmul(T.pW[:, c * 512:(c + 1) * 512], T.KB[0:WROWS, e, t * P:(t + 1) * P],
                                                    T.QB[0:WROWS, e, c * 512:(c + 1) * 512], start=True, stop=True)
                        last.then_inc(w_ready, 1)
                    bt = b_tile(i, n)
                    if bt:
                        gb, e, t = bt
                        first = static(i) and gb == 0
                        if b_alone(i) and i == PAIRS and n == 1:
                            pe.wait_ge(a_copied, PAIRS * SLOTS)
                        turns = int(b_alone(i) and not (i == PAIRS and n == 0))
                        if not first:
                            pe.wait_ge(p_ready, gb - turns)
                        for c in range(2):
                            last = nc.tensor.matmul(u_bank(i, n)[:, c * 512:(c + 1) * 512], T.KB[0:UROWS, e, t * P:(t + 1) * P],
                                                    T.QB[0:UROWS, e, c * 512:(c + 1) * 512], start=True, stop=True)
                        last.then_inc(u_ready, 1)
                        if n % 2 == 0 and not first:
                            products(i, n)
                        if t == 1 and not (static(i) and gb < QT):
                            if searches(i):
                                pe.wait_ge(*((ss_copied, 2 * i) if n < QT else (selT_copied, i)))
                            elif n < QT:
                                pe.wait_ge(rows_copied, PAIRS)
                            gather_o(head_before(i, n))
                    if n == 0 and searches(i - 1):
                        transpose_rows(i - 1)
                    if searches(i):
                        search(i, n)
            iterations(pe, body)
            products(last_i, LAG)
            gather_o(HEADS - 1)


def feed_forward(nc, T, out):
    sem = T.sem
    at_ready, att_ready, att_copied = sem("ff_attn"), sem("ff_attnT_ready"), sem("ff_attnT")
    pr_ready, x1_ready, var_ready, std_ready = sem("ff_proj"), sem("ff_x1"), sem("ff_var"), sem("ff_std")
    xhat_ready, xt_ready, ht_ready = sem("ff_xhat"), sem("ff_xt"), sem("ff_ht")
    lg_ready, oh_ready, ohT_ready, ohT_done = sem("ff_logits"), sem("ff_onehot"), sem("ff_ohT"), sem("ff_ohT_done")
    ohb_ready, mask_done, xe_ready, xe_used = sem("ff_ohb_ready"), sem("ff_mask_done"), sem("ff_xe"), sem("ff_xe_used")
    silu_done, h_ready, hm_ready = sem("ff_silu"), sem("ff_h"), sem("ff_hm")
    sh_ready, sh_silu, sh_h = sem("ff_shared"), sem("ff_shared_silu"), sem("ff_shared_h")
    y_ready, ys_ready, yt_ready, y_done = sem("ff_y"), sem("ff_y_scaled"), sem("ff_y_tokens"), sem("ff_y_done")
    out_done, chain, primed = sem("ff_out"), sem("ff_chain"), sem("ff_primed")
    NCH = B * S // CHUNK
    ATT, PROJ, NORM, XT, ROUTE, ONEHOT = 1, 2, 3, 5, 6, 7

    with nc.Block() as block:
        @block.sync
        def _(sp):
            for c in range(NCH):
                sp.wait_ge(y_done, c + 1)
                sp.dma_start(out[c * CHUNK:(c + 1) * CHUNK, :].rearrange("(t p) c -> p t c", p=P), T.x2[:, :, :]).then_inc(out_done, 16)
            sp.wait_ge(out_done, NCH * 16)

        @block.gpsimd
        def _(pool):
            for c in range(NCH):
                b, t0 = c * CT // QT, c * CT % QT
                if c:
                    pool.wait_ge(att_ready, c)
                for t in range(CT):
                    last = pool.tensor_copy(T.ast[:, t, :].rearrange("p (h d) -> p h d", d=D),
                                            T.attn[:, b * H:(b + 1) * H, t0 + t, :])
                last.then_inc(at_ready, 1)

        @block.scalar
        def _(act):
            def copy_att(c):
                act.wait_ge(att_ready, c + 1)
                if c:
                    act.wait_ge(pr_ready, c)
                act.activation(T.attT[:, :], T.pO[:, :], ACT.Copy).then_inc(att_copied, 1)

            def std(c):
                act.wait_ge(var_ready, c + 1)
                act.activation(T.std[:, :], T.mv[:, :, 1], ACT.Sqrt, bias=T.epsc[:, 0:1]).then_inc(std_ready, 1)
                if c:
                    act.wait_ge(primed, c)
                act.activation(T.prime[:, 0:1], T.epsc[:, 0:1], ACT.Silu).then_inc(primed, 1)

            def copy_onehot(c):
                act.wait_ge(ohT_ready, c + 1)
                if c:
                    act.wait_ge(ohb_ready, c * E)
                act.activation(T.ohT[:, :], T.pM[0:E, :], ACT.Copy).then_inc(ohT_done, 1)

            def mask(c, e):
                act.wait_ge(ohb_ready, c * E + e + 1)
                act.activation(T.mask[:, c % 2, e, :], T.pW[:, (e % 2) * 512:(e % 2 + 1) * 512], ACT.Copy).then_inc(mask_done, 1)

            copy_att(0)
            std(0)
            copy_onehot(0)
            mask(0, 0)
            mask(0, 1)
            for c in range(NCH):
                for s in range(E):
                    if s + 2 < E:
                        mask(c, s + 2)
                    if c + 1 < NCH:
                        if s == ATT:
                            copy_att(c + 1)
                        if s == NORM:
                            std(c + 1)
                        if s == ONEHOT:
                            copy_onehot(c + 1)
                act.wait_ge(xe_used, (c + 1) * E)
                act.activation(T.sg2[:, 0, :], T.pA[:, :], ACT.Silu).then_inc(silu_done, 1)
                for f in range(FB):
                    act.wait_ge(sh_ready, FB * c + f + 1)
                    if c:
                        act.wait_ge(sh_h, FB * (c - 1) + f + 1)
                    act.activation(T.sg2[:, 1, f * 512:(f + 1) * 512], (T.pA if f else T.pW)[:, 0:512], ACT.Silu).then_inc(sh_silu, 1)
                if c + 1 < NCH:
                    mask(c + 1, 0)
                    mask(c + 1, 1)

        @block.vector
        def _(dve):
            n = [0]

            def done(ins, s, value):
                ins.then_inc(s, 1)
                dve.wait_ge(s, value)

            def link(ins):
                n[0] += 1
                done(ins, chain, n[0])

            def residual(c):
                b, x1 = c * CT // QT, T.x1[:, c % 2, :, :]
                dve.wait_ge(pr_ready, c + 1)
                pr = T.pM[:, :].rearrange("p (t c) -> p t c", c=C)
                link(dve.tensor_tensor(x1, pr, T.gates[:, b * C:(b + 1) * C].unsqueeze(1).broadcast_to([P, CT, C]), ALU.mult))
                done(dve.tensor_tensor(x1, x1, T.x[:, c * CT:(c + 1) * CT, :], ALU.add), x1_ready, c + 1)
                for t in range(CT):
                    last = dve.bn_stats(T.bn[:, t, :], T.x1[:, c % 2, t, :])
                link(last)
                for t in range(CT):
                    last = dve.bn_aggr(T.mv[:, t, :], T.bn[:, t, :])
                link(last)
                dve.tensor_scalar(T.veps[:, :], T.mv[:, :, 1], EPS, None, ALU.add).then_inc(var_ready, 1)

            def norm(c):
                dve.wait_ge(std_ready, c + 1)
                link(dve.reciprocal(T.rs[:, :], T.std[:, :]))
                link(dve.tensor_tensor(T.rs[:, :], T.rs[:, :], T.veps[:, :], ALU.mult))
                link(dve.tensor_tensor(T.rs[:, :], T.rs[:, :], T.std[:, :], ALU.add))
                link(dve.tensor_scalar(T.rs[:, :], T.rs[:, :], 0.5, None, ALU.mult))
                link(dve.reciprocal(T.rs[:, :], T.rs[:, :]))
                for t in range(CT):
                    last = dve.tensor_scalar(T.xhat[:, t, :], T.x1[:, c % 2, t, :], T.mv[:, t, 0:1], T.rs[:, t:t + 1],
                                             ALU.subtract, ALU.mult)
                last.then_inc(xhat_ready, 1)

            def modulate(c):
                b = c * CT // QT
                dve.wait_ge(xt_ready, c + 1)
                dve.tensor_scalar(T.hT2[:, c % 2, :], T.pO[:, :], T.mod[:, 4 * B + b:4 * B + b + 1],
                                  T.mod[:, 3 * B + b:3 * B + b + 1], ALU.mult, ALU.add).then_inc(ht_ready, 1)

            def route(c):
                dve.wait_ge(lg_ready, c + 1)
                link(dve.tensor_copy(T.lg[:, :, :], T.pM[:, 0:CT * E].rearrange("p (t e) -> p t e", e=E)))
                link(dve.tensor_reduce(T.mx[:, :], T.lg[:, :, :], AX.X, ALU.max))
                link(dve.tensor_tensor(T.lg[:, :, :], T.lg[:, :, :], T.mx[:, :].unsqueeze(2).broadcast_to([P, CT, E]), ALU.is_ge))
                link(dve.tensor_tensor(T.lg[:, :, :], T.lg[:, :, :], T.down_count[:, :].unsqueeze(1).broadcast_to([P, CT, E]), ALU.mult))
                link(dve.tensor_reduce(T.mx[:, :], T.lg[:, :, :], AX.X, ALU.max))
                dve.tensor_tensor(T.oh[:, :, :], T.lg[:, :, :], T.mx[:, :].unsqueeze(2).broadcast_to([P, CT, E]), ALU.is_equal).then_inc(oh_ready, 1)

            def expert_tokens(c, e):
                dve.wait_ge(mask_done, c * E + e + 1)
                if c or e >= 2:
                    dve.wait_ge(xe_used, c * E + e - 1)
                dve.tensor_tensor(T.xe[:, e % 2, :], T.hT2[:, c % 2, :], T.mask[:, c % 2, e, :], ALU.mult).then_inc(xe_ready, 1)

            def shared_hidden(c, f):
                dve.wait_ge(sh_silu, FB * c + f + 1)
                up = T.pU[:, 0:512] if f else T.pW[:, 512:1024]
                dve.tensor_tensor(T.h[:, 1, f * 512:(f + 1) * 512], T.sg2[:, 1, f * 512:(f + 1) * 512], up, ALU.mult).then_inc(sh_h, 1)

            def finish(c):
                dve.wait_ge(yt_ready, c + 1)
                if c:
                    dve.wait_ge(out_done, 16 * c)
                dve.tensor_tensor(T.x2[:, :, :], T.pM[:, :].rearrange("p (t c) -> p t c", c=C), T.x1[:, c % 2, :, :],
                                  ALU.add).then_inc(y_done, 1)

            residual(0)
            norm(0)
            modulate(0)
            route(0)
            expert_tokens(0, 0)
            expert_tokens(0, 1)
            for c in range(NCH):
                b = c * CT // QT
                for s in range(E):
                    if s + 2 < E:
                        expert_tokens(c, s + 2)
                    if s == 0 and c:
                        finish(c - 1)
                    if c + 1 < NCH:
                        if s == PROJ:
                            residual(c + 1)
                        if s == NORM:
                            norm(c + 1)
                        if s == XT:
                            modulate(c + 1)
                        if s == ROUTE:
                            route(c + 1)
                dve.wait_ge(silu_done, c + 1)
                if c:
                    dve.wait_ge(y_ready, c)
                done(dve.tensor_tensor(T.h[:, 0, :], T.sg2[:, 0, :], T.pU[:, :], ALU.mult), h_ready, c + 1)
                for e in range(E):
                    dve.tensor_tensor(T.hm[:, e, :, :], T.h[:, 0, :].rearrange("p (f n) -> p f n", f=FB),
                                      T.mask[:, c % 2, e, :].unsqueeze(1).broadcast_to([P, FB, CHUNK]), ALU.mult).then_inc(hm_ready, 1)
                    if e in (1, 3):
                        shared_hidden(c, e // 2)
                if c + 1 < NCH:
                    expert_tokens(c + 1, 0)
                    expert_tokens(c + 1, 1)
                dve.wait_ge(y_ready, c + 1)
                dve.tensor_scalar(T.yT[:, :], T.pO[:, :], T.mod[:, 5 * B + b:5 * B + b + 1], None, ALU.mult).then_inc(ys_ready, 1)
            finish(NCH - 1)

        @block.tensor
        def _(pe):
            wT = T.wT[:, 4 * C:].rearrange("p (k e f n) -> p k e f n", k=3, e=E + 1, f=FB)
            woT = T.wT[:, 3 * C:4 * C]

            def transpose_att(c):
                pe.wait_ge(at_ready, c + 1)
                if c > 1:
                    pe.wait_ge(ys_ready, c - 1)
                for t in range(CT):
                    last = nc.tensor.transpose(T.pO[:, t * P:(t + 1) * P], T.ast[:, t, :], T.ident[:, :])
                last.then_inc(att_ready, 1)

            def project(c):
                pe.wait_ge(att_copied, c + 1)
                if c > 1:
                    pe.wait_ge(y_done, c - 1)
                for t in range(CT):
                    nc.tensor.matmul(T.pM[:, t * C:(t + 1) * C], T.attT[:, t * P:(t + 1) * P], woT, start=True, stop=False)
                    last = nc.tensor.matmul(T.pM[:, t * C:(t + 1) * C], T.ones_f[0:1, :], T.borow[0:1, :], start=False, stop=True)
                last.then_inc(pr_ready, 1)

            def transpose_xhat(c):
                pe.wait_ge(xhat_ready, c + 1)
                for t in range(CT):
                    last = nc.tensor.transpose(T.pO[:, t * P:(t + 1) * P], T.xhat[:, t, :], T.ident[:, :])
                last.then_inc(xt_ready, 1)

            def logits(c):
                pe.wait_ge(ht_ready, c + 1)
                for t in range(CT):
                    last = nc.tensor.matmul(T.pM[:, t * E:(t + 1) * E], T.hT2[:, c % 2, t * P:(t + 1) * P], T.rT[:, :],
                                            start=True, stop=True)
                last.then_inc(lg_ready, 1)

            def transpose_onehot(c):
                pe.wait_ge(oh_ready, c + 1)
                for t in range(CT):
                    last = nc.tensor.transpose(T.pM[0:E, t * P:(t + 1) * P], T.oh[:, t, :], T.ident[:, :])
                last.then_inc(ohT_ready, 1)

            def spread(c, e):
                if e < 2:
                    pe.wait_ge(ohT_done, c + 1)
                    if c:
                        pe.wait_ge(sh_h, FB * (c - 1) + 1)
                else:
                    pe.wait_ge(mask_done, c * E + e - 1)
                nc.tensor.matmul(T.pW[:, (e % 2) * 512:(e % 2 + 1) * 512], T.ident_b[0:E, e:e + 1].broadcast_to([E, P]), T.ohT[:, :],
                                 start=True, stop=True).then_inc(ohb_ready, 1)

            def transpose_y(c):
                pe.wait_ge(ys_ready, c + 1)
                if c + 1 < NCH:
                    pe.wait_ge(ohT_done, c + 2)
                for t in range(CT):
                    last = nc.tensor.transpose(T.pM[:, t * P:(t + 1) * P], T.yT[:, t * P:(t + 1) * P], T.ident[:, :])
                last.then_inc(yt_ready, 1)

            transpose_att(0)
            project(0)
            transpose_xhat(0)
            logits(0)
            transpose_onehot(0)
            spread(0, 0)
            spread(0, 1)
            for c in range(NCH):
                for e in range(E):
                    if e + 2 < E:
                        spread(c, e + 2)
                    pe.wait_ge(xe_ready, c * E + e + 1)
                    if c and e == 0:
                        pe.wait_ge(sh_h, FB * c)
                    for k, ps in ((0, T.pA), (1, T.pU)):
                        for f in range(FB):
                            last = nc.tensor.matmul(ps[:, f * 512:(f + 1) * 512], wT[:, k, e, f, :], T.xe[:, e % 2, :],
                                                    start=(e == 0), stop=(e == E - 1))
                    last.then_inc(xe_used, 1)
                    if e == 0 and c:
                        transpose_y(c - 1)
                    if c + 1 < NCH:
                        if e == ATT:
                            transpose_att(c + 1)
                        if e == PROJ:
                            project(c + 1)
                        if e == XT:
                            transpose_xhat(c + 1)
                        if e == ROUTE:
                            logits(c + 1)
                        if e == ONEHOT:
                            transpose_onehot(c + 1)
                for f in range(FB):
                    if f:
                        pe.wait_ge(h_ready, c + 1)
                    else:
                        pe.wait_ge(mask_done, (c + 1) * E)
                    for k in range(2):
                        ps = (T.pU if k else T.pA)[:, 0:512] if f else T.pW[:, k * 512:(k + 1) * 512]
                        last = nc.tensor.matmul(ps, wT[:, k, E, f, :], T.hT2[:, c % 2, :], start=True, stop=True)
                    last.then_inc(sh_ready, 1)
                for e in range(E + 1):
                    if e < E:
                        pe.wait_ge(hm_ready, c * E + e + 1)
                    else:
                        pe.wait_ge(sh_h, FB * (c + 1))
                    if e == 0 and c + 1 < NCH:
                        pe.wait_ge(ht_ready, c + 2)
                    elif e == 0:
                        pe.wait_ge(ys_ready, c)
                    for f in range(FB):
                        rhs = T.hm[:, e, f, :] if e < E else T.h[:, 1, f * 512:(f + 1) * 512]
                        last = nc.tensor.matmul(T.pO[:, :], wT[:, 2, e, f, :], rhs, start=(e == 0 and f == 0),
                                                stop=(e == E and f == FB - 1))
                    if e == 3 and c + 1 < NCH:
                        spread(c + 1, 0)
                        spread(c + 1, 1)
                last.then_inc(y_ready, 1)
            transpose_y(NCH - 1)


class Places:

    def __init__(self, nc, ctx):
        def sb(name, shape, dt):
            return ctx.enter_context(nc.sbuf_tensor(name, shape, dt))

        self.ident = sb("ident", [P, P], F32)
        self.ident_b = sb("ident_b", [P, P], BF16)
        self.tri = sb("tri", [P, P], BF16)
        self.ones_b = sb("ones_b", [P, P], BF16)
        self.zeros_b = sb("zeros_b", [P, P], BF16)
        self.ones_f = sb("ones_f", [P, P], F32)
        self.iota_i = sb("iota_i", [P, P], I32)
        self.iota = sb("iota", [P, P], F32)
        self.down_count = sb("down_count", [P, E], F32)
        self.epsc = sb("epsc", [P, 1], F32)
        self.half = sb("half", [P, 2], F32)
        self.osel = sb("osel", [P, 2, D + 1], F32)
        self.thr0 = sb("thr0", [P, 1], F32)
        self.thrc = sb("thrc", [P, 1], F32)
        self.negthr = sb("negthr", [P, 1], F32)
        self.mod = sb("mod", [P, 6 * B], F32)
        self.gates = sb("gates", [P, B * C], F32)
        self.wT = sb("wT", [P, NWT * C], F32)
        self.rT = sb("rT", [P, E], F32)
        self.x = sb("x", [P, B * QT, C], F32)
        self.V = sb("V", [P, HEADS, QT, D], F32)
        self.Qtok = sb("Qtok", [P, HEADS, QT, PARTS, D], BF16)
        self.attn = sb("attn", [P, HEADS, QT, D], F32)
        self.QB = sb("QB", [P, 2, S], BF16)
        self.KB = sb("KB", [P, 2, S], BF16)
        self.V32 = sb("V32", [P, 2, QT, VW], F32)
        self.tpm = sb("tpm", [P, 2, PARTS], BF16)
        self.bn = sb("bn", [P, CT, 6], F32)
        self.mv = sb("mv", [P, CT, 2], F32)
        self.veps = sb("veps", [P, CT], F32)
        self.std = sb("std", [P, CT], F32)
        self.rs = sb("rs", [P, CT], F32)
        self.xhat = sb("xhat", [P, CT, C], F32)
        self.hT = sb("hT", [P, CHUNK], F32)
        self.borow = sb("borow", [1, C], F32)
        ps = ctx.enter_context(nc.psum_tensor("ps", [P, 4096], F32))
        self.pA, self.pU, self.pW = ps[:, 0:1024], ps[:, 1024:2048], ps[:, 2048:3072]
        self.pO, self.pM = ps[:, 3072:3584], ps[:, 3584:4096]
        self.pUW_b, self.pM_b = ps[:, 1024:3072].bitcast(BF16), ps[:, 3584:4096].bitcast(BF16)
        self.sem = lambda name: ctx.enter_context(nc.semaphore(name))


def place_prepare(T, nc, ctx):
    def sb(name, shape, dt):
        return ctx.enter_context(nc.sbuf_tensor(name, shape, dt))

    T.nat = sb("nat", [P, NWT, C], F32)
    T.cT = sb("cT", [P, B], F32)
    T.sc = sb("sc", [P, B], F32)
    T.wmod = sb("wmod", [P, 6 * C], F32)
    T.gabs = sb("gabs", [P, B + B * C], F32)
    T.qkp = sb("qkp", [P, 2, CT, PARTS, 2 * C], BF16)
    T.bnx = sb("bnx", [P, B * QT, 6], F32)
    T.mvx = sb("mvx", [P, B * QT, 2], F32)
    T.vepsx = sb("vepsx", [P, B * QT], F32)
    T.stdx = sb("stdx", [P, B * QT], F32)
    T.rsx = sb("rsx", [P, B * QT], F32)
    T.xhatx = sb("xhatx", [P, B * QT, C], F32)
    T.rem = sb("rem", [P, 2 * C], F32)
    T.qkT = sb("qkT", [P, 2 * PARTS, CHUNK], BF16)
    T.rt_nat = sb("rt_nat", [E, C], F32)


def place_attention(T, nc, ctx):
    def sb(name, shape, dt):
        return ctx.enter_context(nc.sbuf_tensor(name, shape, dt))

    T.QA = sb("QA", [P, 2, S], BF16)
    T.KA = sb("KA", [P, 2, S], BF16)
    T.QS = sb("QS", [P, 2, S], BF16)
    T.KS = sb("KS", [P, 2, S], BF16)
    T.E = sb("E", [P, 4, S], F32)
    T.Sc = sb("Sc", [P, 4, S], F32)
    T.Ss = sb("Ss", [P, S], F32)
    T.Wm = sb("Wm", [P, S], F32)
    T.junk_a = sb("junk_a", [P, 4, S], BF16)
    T.junk_a2 = sb("junk_a2", [P, S], BF16)
    T.M = sb("M", [P, SLOTS], F32)
    T.Mp = sb("Mp", [P, SLOTS], F32)
    T.cnt = sb("cnt", [P, SLOTS], F32)
    T.Fb = sb("Fb", [P, SLOTS], BF16)
    T.st = sb("st", [P, SLOTS, 3], BF16)
    T.posF = sb("posF", [P, SLOTS], F32)
    T.Sel = sb("Sel", [P, QT, 2, CAP], BF16)
    T.SelT = sb("SelT", [P, S], BF16)
    T.QG = sb("QG", [P, 2, QT, KROWS], BF16)
    T.gs = sb("gs", [P, 3], F32)
    T.sl = sb("sl", [P, 1], F32)
    T.dt = sb("dt", [P, 1], F32)
    T.nd = sb("nd", [P, 1], F32)
    T.ns = sb("ns", [P, 1], F32)
    T.Mq = sb("Mq", [P, SLOTS], F32)
    T.tc = sb("tc", [P, len(DAMP) + 1], F32)
    T.sg = sb("sg", [P, len(DAMP)], F32)
    T.c1 = sb("c1", [P, 1], F32)
    T.W8 = sb("W8", [P, 8], F32)
    T.h8 = sb("h8", [P, 8], F32)
    T.ix = sb("ix", [P, 1], F32)
    T.kth = sb("kth", [P, 1], F32)
    T.t3 = sb("t3", [P, PARTS], BF16)
    T.bad = sb("bad", [P, 3], F32)
    T.badb = sb("badb", [P, 1], BF16)
    T.flag = sb("flag", [P, 1], I32)
    T.Tt = sb("Tt", [P, SLOTS], F32)
    T.X = sb("X", [P, 2, SLOTS], F32)
    T.RP = sb("RP", [P, 2 * 2 * PARTS * QT], BF16)
    T.Osb = sb("Osb", [P, CHUNK], F32)
    T.rl = sb("rl", [P, QT], F32)
    T.mp0 = sb("mp0", [P, 1], F32)
    T.sk = sb("sk", [P, 1], F32)
    T.z8 = sb("z8", [P, 8], F32)
    T.cf = sb("cf", [P, 1], F32)
    T.junk_d = sb("junk_d", [P, S], BF16)
    T.lo = sb("lo", [P, 1], F32)
    T.mid = sb("mid", [P, 1], F32)
    T.stp = sb("stp", [P, 1], F32)
    T.Qc = sb("Qc", [KROWS, P], BF16)
    T.rowsT = sb("rowsT", [2 * 2 * PARTS * QT, P], BF16)


def place_feed_forward(T, nc, ctx):
    def sb(name, shape, dt):
        return ctx.enter_context(nc.sbuf_tensor(name, shape, dt))

    T.ast = sb("ast", [P, CT, C], F32)
    T.attT = sb("attT", [P, CHUNK], F32)
    T.x1 = sb("x1", [P, 2, CT, C], F32)
    T.hT2 = sb("hT2", [P, 2, CHUNK], F32)
    T.yT = sb("yT", [P, CHUNK], F32)
    T.prime = sb("prime", [P, 1], F32)
    T.x2 = sb("x2", [P, CT, C], F32)
    T.lg = sb("lg", [P, CT, E], F32)
    T.mx = sb("mx", [P, CT], F32)
    T.oh = sb("oh", [P, CT, E], F32)
    T.mask = sb("mask", [P, 2, E, CHUNK], BF16)
    T.xe = sb("xe", [P, 2, CHUNK], F32)
    T.sg2 = sb("sg2", [P, 2, FB * CHUNK], F32)
    T.h = sb("h", [P, 2, FB * CHUNK], F32)
    T.hm = sb("hm", [P, E, FB, CHUNK], F32)
    T.ohT = sb("ohT", [E, CHUNK], BF16)


def build(nc, x, wq, wk, wv, wo, bo, thr, up, gate, down, router, up_s, gate_s, down_s, c_in, wmod, out, qk_aug):
    with ExitStack() as kept:
        T = Places(nc, kept)
        with ExitStack() as ctx:
            place_prepare(T, nc, ctx)
            prepare(nc, T, x.rearrange("b s c -> (b s) c"), wq, wk, wv, wo, bo, thr, up, gate, down, router,
                    up_s, gate_s, down_s, c_in, wmod, qk_aug)
        with ExitStack() as ctx:
            place_attention(T, nc, ctx)
            attention(nc, T, qk_aug)
        with ExitStack() as ctx:
            place_feed_forward(T, nc, ctx)
            feed_forward(nc, T, out.rearrange("b s c -> (b s) c"))


def kernel(**inputs):
    import numpy as np
    import concourse.bacc as bacc
    from concourse.bass_utils import run_bass_kernel_spmd

    nc = bacc.Bacc("TRN2", target_bir_lowering=False, num_devices=1)
    names = ["attn_x", "attn_Wq", "attn_Wk", "attn_Wv", "attn_Wo", "attn_bo", "attn_adaptive_threshold", "ffn_up", "ffn_gate",
             "ffn_down", "ffn_router", "ffn_w_up_s", "ffn_w_gate_s", "ffn_w_down_s", "c", "wmod"]
    arrays, args = {}, []
    for name in names:
        a = np.ascontiguousarray(inputs["L0_" + name])
        arrays["in_" + name] = a
        args.append(nc.dram_tensor("in_" + name, a.shape, mybir.dt.from_np(a.dtype), kind="ExternalInput").ap())
    out = nc.dram_tensor("out_0", (B, S, C), F32, kind="ExternalOutput").ap()
    qk_aug = nc.dram_tensor("qk_aug", (2, REP, HEADS * D, S), BF16).ap()
    build(nc, *args, out, qk_aug)
    return run_bass_kernel_spmd(nc, [arrays], core_ids=[0]).results[0]["out_0"]
```
